# Optimizing a Trainium2 kernel written in Bass

```python
import numpy as np
import jax
import jax.numpy as jnp

def _softmax(x, axis=-1):
    return jax.nn.softmax(x, axis=axis)

def _gelu(x):
    return jax.nn.gelu(x, approximate=True)

def _silu(x):
    return jax.nn.silu(x)

def _sigmoid(x):
    return jax.nn.sigmoid(x)

def _layernorm(x, axis=-1, eps=1e-05):
    m = jnp.mean(x, axis=axis, keepdims=True)
    v = jnp.var(x, axis=axis, keepdims=True)
    return (x - m) / jnp.sqrt(v + eps)

def _scatter_add(tgt, idx, src, axis=0):
    return tgt.at[idx].add(src)

def _segment_sum(src, seg, n):
    return jax.ops.segment_sum(src, seg, n)
kernel_name = 'mk_adaln_d2_jaxref_r4_f5a8ec'

def setup_inputs(seed: int=0):
    np.random.seed(seed)
    _w = jnp.asarray

    def _L0_attn_setup():
        import jax, jax.numpy as jnp
        import numpy as np
        EMBED_DIM = 512
        NUM_HEADS = 16
        HEAD_DIM = EMBED_DIM // NUM_HEADS
        NUM_KV_GROUPS = 2
        WINDOW = 64
        KV_DIM = NUM_KV_GROUPS * HEAD_DIM
        key = jax.random.key(seed)
        ks = jax.random.split(key, 9)
        B, L, C = (2, 1024, EMBED_DIM)
        s = 1.0 / np.sqrt(C)
        return {'x': jax.random.normal(ks[0], (B, L, C), dtype=jnp.float32), 'Wq': jax.random.normal(ks[1], (C, C), dtype=jnp.float32) * s, 'bq': jnp.zeros((C,), dtype=jnp.float32), 'Wk': jax.random.normal(ks[2], (C, KV_DIM), dtype=jnp.float32) * s, 'bk': jnp.zeros((KV_DIM,), dtype=jnp.float32), 'Wv': jax.random.normal(ks[3], (C, KV_DIM), dtype=jnp.float32) * s, 'bv': jnp.zeros((KV_DIM,), dtype=jnp.float32), 'Wo': jax.random.normal(ks[4], (C, C), dtype=jnp.float32) * s, 'bo': jnp.zeros((C,), dtype=jnp.float32)}
    _L0_attn_in = _L0_attn_setup()

    def _L0_ffn_setup():
        import jax, jax.numpy as jnp
        import numpy as np
        from jax import lax
        E = 64
        TOP_K = 8
        SEL_K = 4
        THRESH = 0.5
        H = 512
        F_INT = 192
        B, S = (1, 512)
        key = jax.random.key(seed)
        k0, k1, k2, k3, k4 = jax.random.split(key, 5)
        return {'hidden_states': jax.random.normal(k0, (B, S, H), jnp.float32), 'gate_weight': jax.random.normal(k1, (E, H), jnp.float32) * 0.02, 'gate_up_proj': jax.random.normal(k2, (E, 2 * F_INT, H), jnp.float32) * 0.02, 'down_proj': jax.random.normal(k3, (E, H, F_INT), jnp.float32) * 0.02, 'similarity': jax.random.uniform(k4, (E, E), jnp.float32)}
    _L0_ffn_in = _L0_ffn_setup()
    _L0_c = _w((lambda *s: np.random.randn(*s).astype(np.float32) * 0.05)(1, 512))
    _L0_wmod = _w((lambda *s: np.random.randn(*s).astype(np.float32) * 0.05)(512, 6 * 512) * 512 ** (-0.5))

    def _L1_attn_setup():
        import jax, jax.numpy as jnp
        import numpy as np
        N_HEADS = 16
        N_KV_HEADS = 4
        WINDOW = 128
        N_META = 16
        ROPE_BASE = 10000.0

        def rotate_half(x):
            x1 = x[..., 0::2]
            x2 = x[..., 1::2]
            return jnp.stack((-x2, x1), axis=-1).reshape(x.shape)

        def apply_rope(x, positions):
            d = x.shape[-1]
            inv_freq = 1.0 / ROPE_BASE ** (jnp.arange(0, d, 2, dtype=jnp.float32) / d)
            angles = positions.astype(jnp.float32)[:, None] * inv_freq
            cos = jnp.repeat(jnp.cos(angles), 2, axis=-1)[None, None]
            sin = jnp.repeat(jnp.sin(angles), 2, axis=-1)[None, None]
            return x * cos + rotate_half(x) * sin
        key = jax.random.key(seed)
        ks = jax.random.split(key, 4)
        B, S, E = (2, 1024, 512)
        hd = E // N_HEADS
        kv_out = 2 * N_KV_HEADS * hd
        sc = 1.0 / np.sqrt(E).astype(np.float32)
        return {'x': jax.random.normal(ks[0], (B, S, E), jnp.float32), 'Wq': jax.random.normal(ks[1], (E, E), jnp.float32) * sc, 'bq': jnp.zeros((E,), jnp.float32), 'Wkv': jax.random.normal(ks[2], (E, kv_out), jnp.float32) * sc, 'bkv': jnp.zeros((kv_out,), jnp.float32), 'Wo': jax.random.normal(ks[3], (E, E), jnp.float32) * sc, 'bo': jnp.zeros((E,), jnp.float32)}
    _L1_attn_in = _L1_attn_setup()

    def _L1_ffn_setup():
        import jax, jax.numpy as jnp
        import numpy as np
        HIDDEN = 512
        INTER = 2048
        SCALE = 64.0

        def fwht(x):
            orig_shape = x.shape
            n = orig_shape[-1]
            x = x.reshape(-1, n)
            h = 1
            while h < n:
                x = x.reshape(-1, n // (2 * h), 2, h)
                a, b = (x[:, :, 0, :], x[:, :, 1, :])
                x = jnp.stack([a + b, a - b], axis=2).reshape(-1, n)
                h *= 2
            return (x / jnp.sqrt(jnp.asarray(n, x.dtype))).reshape(orig_shape)
        key = jax.random.key(seed)
        ks = jax.random.split(key, 8)
        inp = jax.random.normal(ks[0], (4, 512, HIDDEN), dtype=jnp.float32)
        SU_ug = jnp.where(jax.random.bernoulli(ks[1], 0.5, (HIDDEN,)), 1.0, -1.0).astype(jnp.float32)
        SU_dp = jnp.where(jax.random.bernoulli(ks[2], 0.5, (INTER,)), 1.0, -1.0).astype(jnp.float32)
        Wscale_ug = jax.random.uniform(ks[3], (2 * INTER,), jnp.float32, 0.5, 1.5)
        Wscale_dp = jax.random.uniform(ks[4], (HIDDEN,), jnp.float32, 0.5, 1.5)
        W_up = jax.random.normal(ks[5], (INTER, HIDDEN), dtype=jnp.float32) * 0.02
        W_gate = jax.random.normal(ks[6], (INTER, HIDDEN), dtype=jnp.float32) * 0.02
        W_down = jax.random.normal(ks[7], (HIDDEN, INTER), dtype=jnp.float32) * 0.02
        return {'input': inp, 'SU_ug': SU_ug, 'SU_dp': SU_dp, 'Wscale_ug': Wscale_ug, 'Wscale_dp': Wscale_dp, 'W_up': W_up, 'W_gate': W_gate, 'W_down': W_down}
    _L1_ffn_in = _L1_ffn_setup()
    _L1_c = _w((lambda *s: np.random.randn(*s).astype(np.float32) * 0.05)(1, 512))
    _L1_wmod = _w((lambda *s: np.random.randn(*s).astype(np.float32) * 0.05)(512, 6 * 512) * 512 ** (-0.5))
    _d = {'L0_attn_x': _L0_attn_in['x'], 'L0_attn_Wq': _L0_attn_in['Wq'], 'L0_attn_bq': _L0_attn_in['bq'], 'L0_attn_Wk': _L0_attn_in['Wk'], 'L0_attn_bk': _L0_attn_in['bk'], 'L0_attn_Wv': _L0_attn_in['Wv'], 'L0_attn_bv': _L0_attn_in['bv'], 'L0_attn_Wo': _L0_attn_in['Wo'], 'L0_attn_bo': _L0_attn_in['bo'], 'L0_ffn_gate_weight': _L0_ffn_in['gate_weight'], 'L0_ffn_gate_up_proj': _L0_ffn_in['gate_up_proj'], 'L0_ffn_down_proj': _L0_ffn_in['down_proj'], 'L0_ffn_similarity': _L0_ffn_in['similarity'], 'L0_c': _L0_c, 'L0_wmod': _L0_wmod, 'L1_attn_Wq': _L1_attn_in['Wq'], 'L1_attn_bq': _L1_attn_in['bq'], 'L1_attn_Wkv': _L1_attn_in['Wkv'], 'L1_attn_bkv': _L1_attn_in['bkv'], 'L1_attn_Wo': _L1_attn_in['Wo'], 'L1_attn_bo': _L1_attn_in['bo'], 'L1_ffn_SU_ug': _L1_ffn_in['SU_ug'], 'L1_ffn_SU_dp': _L1_ffn_in['SU_dp'], 'L1_ffn_Wscale_ug': _L1_ffn_in['Wscale_ug'], 'L1_ffn_Wscale_dp': _L1_ffn_in['Wscale_dp'], 'L1_ffn_W_up': _L1_ffn_in['W_up'], 'L1_ffn_W_gate': _L1_ffn_in['W_gate'], 'L1_ffn_W_down': _L1_ffn_in['W_down'], 'L1_c': _L1_c, 'L1_wmod': _L1_wmod}
    _x0 = _d['L0_attn_x']
    _d['L0_attn_x'] = jax.random.normal(jax.random.fold_in(jax.random.key(seed), 1), (1, 2048, 512), dtype=_x0.dtype)
    del _x0
    return _d

def reference(L0_attn_x, L0_attn_Wq, L0_attn_bq, L0_attn_Wk, L0_attn_bk, L0_attn_Wv, L0_attn_bv, L0_attn_Wo, L0_attn_bo, L0_ffn_gate_weight, L0_ffn_gate_up_proj, L0_ffn_down_proj, L0_ffn_similarity, L0_c, L0_wmod, L1_attn_Wq, L1_attn_bq, L1_attn_Wkv, L1_attn_bkv, L1_attn_Wo, L1_attn_bo, L1_ffn_SU_ug, L1_ffn_SU_dp, L1_ffn_Wscale_ug, L1_ffn_Wscale_dp, L1_ffn_W_up, L1_ffn_W_gate, L1_ffn_W_down, L1_c, L1_wmod):

    def _L0_attn_ref(x, Wq, bq, Wk, bk, Wv, bv, Wo, bo):
        import jax, jax.numpy as jnp
        import numpy as np
        EMBED_DIM = 512
        NUM_HEADS = 16
        HEAD_DIM = EMBED_DIM // NUM_HEADS
        NUM_KV_GROUPS = 2
        WINDOW = 64
        KV_DIM = NUM_KV_GROUPS * HEAD_DIM
        B, L, C = x.shape
        W = WINDOW
        H, G, D = (NUM_HEADS, NUM_KV_GROUPS, HEAD_DIM)
        R = H // G
        pad_l = (W - L % W) % W
        xp = jnp.pad(x, ((0, 0), (0, pad_l), (0, 0)))
        Lp = xp.shape[1]
        q = (xp @ Wq + bq).reshape(B, Lp, H, D).transpose(0, 2, 1, 3)
        k = (xp @ Wk + bk).reshape(B, Lp, G, D).transpose(0, 2, 1, 3)
        v = (xp @ Wv + bv).reshape(B, Lp, G, D).transpose(0, 2, 1, 3)
        num_windows = (Lp - W) // (W // 2) + 1
        starts = jnp.arange(num_windows) * (W // 2)
        idx = starts[:, None] + jnp.arange(W)
        qw = q[:, :, idx, :]
        kw = k[:, :, idx, :]
        vw = v[:, :, idx, :]
        qg = qw.reshape(B, R, G, num_windows, W, D)
        scale = 1.0 / np.sqrt(D)
        scores = jnp.einsum('brgnqd,bgnkd->brgnqk', qg, kw) * scale
        attn = jax.nn.softmax(scores, axis=-1)
        og = jnp.einsum('brgnqk,bgnkd->brgnqd', attn, vw)
        o = og.reshape(B, H, num_windows, W, D)
        o = o.transpose(0, 2, 3, 1, 4).reshape(B, num_windows * W, H * D)
        o = o[:, :L, :]
        return o @ Wo + bo

    def _L0_ffn_ref(hidden_states, gate_weight, gate_up_proj, down_proj, similarity):
        import jax, jax.numpy as jnp
        import numpy as np
        from jax import lax
        E = 64
        TOP_K = 8
        SEL_K = 4
        THRESH = 0.5
        H = 512
        F_INT = 192
        B, S = (1, 512)
        b, s, h = hidden_states.shape
        x = hidden_states.reshape(-1, h)
        logits = x @ gate_weight.T
        probs = jax.nn.softmax(logits.astype(jnp.float32), axis=-1).astype(logits.dtype)
        top_val, top_idx = lax.top_k(probs, TOP_K)
        top_val = top_val / jnp.clip(top_val.sum(-1, keepdims=True), 1e-12)
        sim = similarity.astype(jnp.float32)
        diag = jnp.arange(E)
        sim = sim.at[diag, diag].set(1.0)
        primary_mask = jnp.zeros((E,), bool).at[top_idx[:, :SEL_K].reshape(-1)].set(True)
        secondary_mask = jnp.zeros((E,), bool).at[top_idx[:, SEL_K:].reshape(-1)].set(True)
        cand = jnp.where(primary_mask[None, :], sim, -jnp.inf)
        best_primary = jnp.argmax(cand, axis=-1)
        best_sim = jnp.max(cand, axis=-1)
        replace = secondary_mask & ~primary_mask & (best_sim >= THRESH)
        mapping = jnp.where(replace, best_primary, jnp.arange(E))
        rerouted = mapping[top_idx]
        rerouted = rerouted.at[:, :SEL_K].set(top_idx[:, :SEL_K])
        flat_e = rerouted.reshape(-1)
        order = jnp.argsort(flat_e)
        tok = order // TOP_K
        xs = x[tok]
        group_sizes = jnp.zeros((E,), jnp.int32).at[flat_e].add(1)
        gu = lax.ragged_dot(xs, jnp.swapaxes(gate_up_proj, 1, 2), group_sizes)
        gate, up = jnp.split(gu, 2, axis=-1)
        hact = jax.nn.silu(gate) * up
        y = lax.ragged_dot(hact, jnp.swapaxes(down_proj, 1, 2), group_sizes)
        w = top_val.reshape(-1)[order]
        out = jnp.zeros_like(x).at[tok].add(y * w[:, None])
        return out.reshape(b, s, h)

    def _L1_attn_ref(x, Wq, bq, Wkv, bkv, Wo, bo):
        import jax, jax.numpy as jnp
        import numpy as np
        N_HEADS = 16
        N_KV_HEADS = 4
        WINDOW = 128
        N_META = 16
        ROPE_BASE = 10000.0

        def rotate_half(x):
            x1 = x[..., 0::2]
            x2 = x[..., 1::2]
            return jnp.stack((-x2, x1), axis=-1).reshape(x.shape)

        def apply_rope(x, positions):
            d = x.shape[-1]
            inv_freq = 1.0 / ROPE_BASE ** (jnp.arange(0, d, 2, dtype=jnp.float32) / d)
            angles = positions.astype(jnp.float32)[:, None] * inv_freq
            cos = jnp.repeat(jnp.cos(angles), 2, axis=-1)[None, None]
            sin = jnp.repeat(jnp.sin(angles), 2, axis=-1)[None, None]
            return x * cos + rotate_half(x) * sin
        B, S, E = x.shape
        hd = E // N_HEADS
        q = (x @ Wq + bq).reshape(B, S, N_HEADS, hd).transpose(0, 2, 1, 3)
        kv = (x @ Wkv + bkv).reshape(B, S, 2, N_KV_HEADS, hd)
        k = kv[:, :, 0].transpose(0, 2, 1, 3)
        v = kv[:, :, 1].transpose(0, 2, 1, 3)
        pos = jnp.arange(S)
        q = apply_rope(q, pos)
        k = apply_rope(k, pos)
        rep = N_HEADS // N_KV_HEADS
        k = jnp.repeat(k, rep, axis=1)
        v = jnp.repeat(v, rep, axis=1)
        meta_end = min(N_META, S)
        scale = 1.0 / float(np.sqrt(hd))
        chunks = []
        for qs in range(0, S, WINDOW):
            qe = min(qs + WINDOW, S)
            ls = max(meta_end, qs - WINDOW + 1)
            q_c = q[:, :, qs:qe]
            k_c = jnp.concatenate([k[:, :, :meta_end], k[:, :, ls:qe]], axis=2)
            v_c = jnp.concatenate([v[:, :, :meta_end], v[:, :, ls:qe]], axis=2)
            k_pos = jnp.concatenate([jnp.arange(meta_end), jnp.arange(ls, qe)])
            q_pos = jnp.arange(qs, qe)
            causal = k_pos[None, :] <= q_pos[:, None]
            in_window = k_pos[None, :] >= q_pos[:, None] - WINDOW + 1
            meta = k_pos[None, :] < meta_end
            allowed = causal & (in_window | meta)
            scores = jnp.einsum('bhqd,bhkd->bhqk', q_c, k_c) * scale
            scores = jnp.where(allowed[None, None], scores, -jnp.inf)
            attn = jax.nn.softmax(scores, axis=-1)
            chunks.append(jnp.einsum('bhqk,bhkd->bhqd', attn, v_c))
        y = jnp.concatenate(chunks, axis=2)
        y = y.transpose(0, 2, 1, 3).reshape(B, S, E)
        return y @ Wo + bo

    def _L1_ffn_ref(input, SU_ug, SU_dp, Wscale_ug, Wscale_dp, W_up, W_gate, W_down):
        import jax, jax.numpy as jnp
        import numpy as np
        HIDDEN = 512
        INTER = 2048
        SCALE = 64.0

        def fwht(x):
            orig_shape = x.shape
            n = orig_shape[-1]
            x = x.reshape(-1, n)
            h = 1
            while h < n:
                x = x.reshape(-1, n // (2 * h), 2, h)
                a, b = (x[:, :, 0, :], x[:, :, 1, :])
                x = jnp.stack([a + b, a - b], axis=2).reshape(-1, n)
                h *= 2
            return (x / jnp.sqrt(jnp.asarray(n, x.dtype))).reshape(orig_shape)
        n = SU_ug.shape[0]
        x = input.reshape(-1, n)
        x = fwht(x * SU_ug) / SCALE
        x_up = x @ W_up.T * (Wscale_ug[:INTER] * SCALE)
        x_gate = x @ W_gate.T * (Wscale_ug[INTER:] * SCALE)
        x = jax.nn.silu(x_gate) * x_up
        x = fwht(x * SU_dp) / SCALE
        x = x @ W_down.T * (Wscale_dp * SCALE)
        return x.reshape(input.shape)
    x = L0_attn_x
    mod = (_silu(L0_c) @ L0_wmod).reshape(L0_c.shape[0], 6, 1, -1)
    sa, ca, ga, sb, cb, gb = (mod[:, 0], mod[:, 1], mod[:, 2], mod[:, 3], mod[:, 4], mod[:, 5])
    ga = (2 * (ga >= 0) - 1) * jnp.maximum(jnp.abs(ga), 0.25)
    gb = (2 * (gb >= 0) - 1) * jnp.maximum(jnp.abs(gb), 0.25)
    h = _layernorm(x, axis=-1) * (1 + ca) + sa
    x = x + ga * _L0_attn_ref(h, L0_attn_Wq, L0_attn_bq, L0_attn_Wk, L0_attn_bk, L0_attn_Wv, L0_attn_bv, L0_attn_Wo, L0_attn_bo)
    h = _layernorm(x, axis=-1) * (1 + cb) + sb
    x = x + gb * _L0_ffn_ref(h, L0_ffn_gate_weight, L0_ffn_gate_up_proj, L0_ffn_down_proj, L0_ffn_similarity)
    mod = (_silu(L1_c) @ L1_wmod).reshape(L1_c.shape[0], 6, 1, -1)
    sa, ca, ga, sb, cb, gb = (mod[:, 0], mod[:, 1], mod[:, 2], mod[:, 3], mod[:, 4], mod[:, 5])
    ga = (2 * (ga >= 0) - 1) * jnp.maximum(jnp.abs(ga), 0.25)
    gb = (2 * (gb >= 0) - 1) * jnp.maximum(jnp.abs(gb), 0.25)
    h = _layernorm(x, axis=-1) * (1 + ca) + sa
    x = x + ga * _L1_attn_ref(h, L1_attn_Wq, L1_attn_bq, L1_attn_Wkv, L1_attn_bkv, L1_attn_Wo, L1_attn_bo)
    h = _layernorm(x, axis=-1) * (1 + cb) + sb
    x = x + gb * _L1_ffn_ref(h, L1_ffn_SU_ug, L1_ffn_SU_dp, L1_ffn_Wscale_ug, L1_ffn_Wscale_dp, L1_ffn_W_up, L1_ffn_W_gate, L1_ffn_W_down)
    return x

_drawn_inputs = setup_inputs


def setup_inputs(seed=0):
    import zlib

    import numpy as np

    out = dict(_drawn_inputs(seed))
    spreads = {'L0_attn_bq': (0.0, 0.8),
     'L0_attn_bk': (0.0, 2.0),
     'L0_attn_bv': (0.0, 0.315),
     'L0_attn_bo': (0.0, 0.318),
     'L1_attn_bq': (0.0, 2.0),
     'L1_attn_bkv': (0.0, 0.322),
     'L1_attn_bo': (0.0, 0.337)}
    factors = {'L0_ffn_gate_weight': 8.0,
     'L0_ffn_gate_up_proj': 8.0,
     'L0_ffn_down_proj': 8.0,
     'L1_ffn_Wscale_ug': 5.08,
     'L1_ffn_Wscale_dp': 7.477,
     'L1_attn_Wq': 3.595,
     'L1_attn_Wkv': 2.68}
    for name, (base, spread) in spreads.items():
        noise = np.random.default_rng([zlib.crc32(name.encode()), seed]).standard_normal(out[name].shape)
        drawn = base * np.exp(spread * noise) if base else spread * noise
        out[name] = jnp.asarray(drawn.astype(out[name].dtype))
    for name, factor in factors.items():
        out[name] = (out[name] * factor).astype(out[name].dtype)
    return out
```

```python
from contextlib import ExitStack

import concourse.bass as bass
from concourse import mybir

ALU = mybir.AluOpType
ACT = mybir.ActivationFunctionType
AX = mybir.AxisListType
F32 = mybir.dt.float32
BF16 = mybir.dt.bfloat16
I32 = mybir.dt.int32
U32 = mybir.dt.uint32

P = 128
S, C = 2048, 512
NT = S // P
KC = C // P
HD = 32
HP = P // HD
EPS = 1e-5
NEG = -1e30

W0 = 64
HOP = W0 // 2
KEYS0 = W0 + HOP
G0 = 2
SCALE0 = float(HD) ** -0.5

E = 64
TOPK, SELK = 8, 4
THRESH = 0.5
FI = 192
FH = FI // 2
PAIRS = S * TOPK
SLOTS = PAIRS // P + E
RING = 4

NKV1 = 4
META = 16
KEYS1 = META + 2 * P
SCALE1 = float(HD) ** -0.5
INTER = 2048
FT = INTER // P
GT = 4
GN = GT * P

DVE_A, POOL_A = 30, 4
POOL_M = 6
DVE_B, POOL_B = 14, 38
DVE_F = 21


class Steps:

    def __init__(self, eng, sem):
        self.eng, self.sem, self.base, self.k = eng, sem, 0, 0

    def did(self, ins):
        self.k += 1
        ins.then_inc(self.sem, 1)

    def settle(self):
        self.eng.wait_ge(self.sem, self.base + self.k)

    def loop(self, i, per):
        self.first, self.per = self.k, per
        self.base, self.k = i * per + self.first, 0

    def end(self, turns):
        assert self.k == self.per, ("steps a turn", self.k)
        self.base, self.k = 0, self.first + turns * self.per


def wait_tile(eng, sem, per, tile, k=None):
    if isinstance(tile, int) and tile < 0:
        return
    eng.wait_ge(sem, tile * per + (per if k is None else k))


def shift(tile, by):
    return tile + by


def tile_of(x, t):
    if isinstance(t, int):
        return x[:, t]
    d = x[:, bass.ds(t, 1)]
    names = "abcdef"[:len(d.shape) - 2]
    return d.rearrange(f"p o {' '.join(names)} -> p (o {names[0]}) {' '.join(names[1:])}")


def windows(q):
    step = q.ap[0]
    return bass.AP(tensor=q.tensor, offset=q.offset, ap=[list(step), [HOP, 2], [1, W0]])


def adaln_two_layers(nc, a, out):
    ctx = ExitStack()
    with ctx:
        def sb(name, shape, dt=F32):
            return ctx.enter_context(nc.sbuf_tensor(name, shape, dt))

        def sem(name):
            return ctx.enter_context(nc.semaphore(name))

        def dram(name, shape, dt=F32):
            return nc.dram_tensor(name, shape, dt).ap()

        def phase_semaphores(ph):
            mine = []
            ph.callback(nc.all_engine_barrier)
            ph.callback(nc.clear_and_free_semaphores, mine)

            def psem(name):
                mine.append(nc.alloc_semaphore(name=name))
                return mine[-1]
            return psem

        h_moe = dram("h_moe", [S, C])
        y_moe = dram("y_moe", [SLOTS * P, C])
        slot_token = dram("slot_token", [SLOTS * P, 1])

        x_res = sb("x_res", [P, NT, C])
        mod = sb("mod", [P, 2, 6, C])
        ident = sb("ident", [P, P])
        ident_b = sb("ident_b", [P, P], BF16)
        ones_b = sb("ones_b", [P, P], BF16)
        upper_b = sb("upper_b", [P, P], BF16)
        mask0 = sb("mask0", [P, KEYS0], BF16)
        mask1 = sb("mask1", [P, 4, KEYS1], BF16)
        neg_half = sb("neg_half", [P, 1])
        route_hot = sb("route_hot", [P, NT, TOPK, E], BF16)
        route_w = sb("route_w", [P, NT, TOPK])
        had = sb("had", [P, P])
        iota_row = sb("iota_row", [P, E])
        iota_col = sb("iota_col", [P, 1])
        down_scale = sb("down_scale", [P, C])
        pos_u = sb("pos_u", [P, NT, TOPK], I32)
        slot_rows = sb("slot_rows", [P, SLOTS + 2], I32)
        tile_expert = sb("tile_expert", [1, SLOTS + 2], I32)
        expert_end = sb("expert_end", [1, E], I32)
        arena = sb("arena", [P, 32200])
        psum = [ctx.enter_context(nc.psum_tensor(f"bank{i}", [P, 512], F32)) for i in range(8)]

        class Carver:
            def __init__(self, at):
                self.at = at

            def __call__(self, *shape):
                n = 1
                for d in shape:
                    n *= d
                v = arena[:, self.at:self.at + n]
                self.at += n
                assert self.at <= 32200, self.at
                names = "abcd"[:len(shape)]
                if len(shape) > 1:
                    v = v.rearrange(f"p ({' '.join(names)}) -> p {' '.join(names)}", **dict(zip(names, shape)))
                return v

        wd = Carver(0)(FT, C)

        with ExitStack() as ph, nc.Block() as block:
            psem = phase_semaphores(ph)
            cv = Carver(0)
            cols = cv(2, KC)
            act_c = cv(2, KC)
            act_b = cv(2, KC, P)
            wm = cv(6, KC, C)
            const_f = cv(3, P)
            masks_f = cv(KEYS0 + 4 * KEYS1)
            su_row = cv(C)
            down_row = cv(C)
            gate_tmp = cv(2, C)
            zero_i = cv(SLOTS)
            iota_i = cv(E + 1).bitcast(I32)
            c_in, consts_in, zeros_out, c_done, c_wide, mod_mm, mod_out, dve_steps, pool_steps = (
                psem(n) for n in
                ("c_in", "consts_in", "zeros_out", "c_done", "c_wide", "mod_mm", "mod_out", "setup_dve_steps", "setup_pool_steps"))
            wm_in = [psem(f"wm_in{j}") for j in range(6)]

            @block.sync
            def _(sp):
                sp.dma_start(cols[:], a["c_cols"]).then_inc(c_in, 16)
                for l in range(2):
                    w = a[f"L{l}_wmod"].rearrange("(k p) (j n) -> j p k n", p=P, j=6)
                    for j in range(6):
                        if l:
                            sp.wait_ge(mod_mm, j + 1)
                        sp.dma_start(wm[:, j], w[j]).then_inc(wm_in[j], 16)
                sp.wait_ge(wm_in[5], 32)

            @block.scalar
            def _(act):
                act.dma_start(const_f[:], a["squares"].rearrange("k p n -> p k n")).then_inc(consts_in, 16)
                act.dma_start(masks_f[:, 0:KEYS0], a["mask0"]).then_inc(consts_in, 16)
                act.dma_start(masks_f[:, KEYS0:], a["mask1"].rearrange("k p n -> p k n")).then_inc(consts_in, 16)
                act.dma_start(su_row, a["L1_ffn_SU_ug"].partition_broadcast(P)).then_inc(consts_in, 16)
                act.dma_start(down_row, a["L1_ffn_Wscale_dp"].partition_broadcast(P)).then_inc(consts_in, 16)
                act.dma_start(x_res[:], a["L0_attn_x"][0].rearrange("(t p) c -> p t c", p=P)).then_inc(consts_in, 16)
                act.wait_ge(c_in, 16)
                nc.scalar.activation(act_c[:], cols[:], ACT.Silu).then_inc(c_done, 1)
                act.wait_ge(consts_in, 16 * 6)

            @block.gpsimd
            def _(pool):
                st = Steps(pool, pool_steps)
                st.did(nc.gpsimd.memset(ones_b[:], 1.0))
                st.did(nc.gpsimd.memset(neg_half[:], -0.5))
                st.did(nc.gpsimd.iota(iota_i[:, 0:E], [[1, E]], base=0, channel_multiplier=0))
                st.did(nc.gpsimd.iota(iota_i[:, E:], [[1, 1]], base=0, channel_multiplier=1))
                st.did(nc.gpsimd.memset(zero_i, 0.0))
                st.did(nc.gpsimd.memset(slot_rows[:, SLOTS:], 0))
                st.did(nc.gpsimd.memset(tile_expert[:, SLOTS:], E - 1))
                st.settle()
                st.did(nc.gpsimd.tensor_copy(iota_row[:], iota_i[:, 0:E]))
                st.did(nc.gpsimd.tensor_copy(iota_col[:], iota_i[:, E:]))
                pool.dma_start(slot_token.rearrange("(p n) o -> p (n o)", p=P), zero_i).then_inc(zeros_out, 16)
                pool.wait_ge(zeros_out, 16)

            @block.tensor
            def _(pe):
                pe.wait_ge(c_wide, 1)
                for l in range(2):
                    for j in range(6):
                        pe.wait_ge(wm_in[j], 16 * (l + 1))
                        n = 6 * l + j
                        if n >= 4:
                            pe.wait_ge(mod_out, n - 3)
                        for k in range(KC):
                            mm = nc.tensor.matmul(psum[n % 4][:], act_b[:, l, k, :], wm[:, j, k, :],
                                                  start=(k == 0), stop=(k == KC - 1))
                        mm.then_inc(mod_mm, 1)

            @block.vector
            def _(dve):
                st = Steps(dve, dve_steps)
                dve.wait_ge(c_done, 1)
                nc.vector.tensor_copy(act_b.rearrange("p l k n -> p (l k) n"),
                                      act_c.rearrange("p l k -> p (l k)").unsqueeze(2).to_broadcast([P, 2 * KC, P])).then_inc(c_wide, 1)
                dve.wait_ge(consts_in, 16 * 6)
                st.did(nc.vector.tensor_copy(ident[:], const_f[:, 0]))
                st.did(nc.vector.tensor_copy(ident_b[:], const_f[:, 0]))
                st.did(nc.vector.tensor_copy(had[:], const_f[:, 2]))
                st.did(nc.vector.tensor_copy(upper_b[:], const_f[:, 1]))
                st.did(nc.vector.tensor_copy(mask0[:], masks_f[:, 0:KEYS0]))
                st.did(nc.vector.tensor_copy(mask1[:],
                                             masks_f[:, KEYS0:].rearrange("p (k n) -> p k n", k=4)))
                for l in range(2):
                    for j in range(6):
                        n = 6 * l + j
                        dve.wait_ge(mod_mm, n + 1)
                        src, dst = psum[n % 4][:], mod[:, l, j, :]
                        if j in (1, 4):
                            nc.vector.tensor_scalar(dst, src, 1.0, None, ALU.add).then_inc(mod_out, 1)
                        elif j in (2, 5):
                            t0, t1 = gate_tmp[:, 0, :], gate_tmp[:, 1, :]
                            st.did(nc.vector.tensor_copy(dst, src))
                            st.settle()
                            st.did(nc.vector.tensor_scalar(t0, dst, -1.0, 0.25, ALU.mult, ALU.max))
                            st.did(nc.vector.tensor_scalar(t1, dst, 0.0, 2.0, ALU.is_ge, ALU.mult))
                            st.settle()
                            st.did(nc.vector.tensor_tensor(t0, t0, dst, ALU.max))
                            st.did(nc.vector.tensor_scalar(t1, t1, -1.0, None, ALU.add))
                            st.settle()
                            nc.vector.tensor_tensor(dst, t0, t1, ALU.mult).then_inc(mod_out, 1)
                        else:
                            nc.vector.tensor_copy(dst, src).then_inc(mod_out, 1)
                dve.wait_ge(mod_out, 12)
                for j in (3, 4):
                    st.did(nc.vector.tensor_tensor(mod[:, 1, j, :], mod[:, 1, j, :], su_row, ALU.mult))
                st.did(nc.vector.scalar_tensor_tensor(down_scale[:], down_row, float(INTER) ** -0.5, mod[:, 1, 5, :],
                                                      ALU.mult, ALU.mult))
                st.settle()

        with ExitStack() as ph, nc.Block() as block:
            psem = phase_semaphores(ph)

            cv = Carver(0)
            xa = cv(NT, C)[0:KEYS0]
            wq, wk, wv = cv(KC, C), cv(KC, P), cv(KC, G0 * HD)
            wo, wgate = cv(KC, C), cv(KC, E)
            bq, bk, bv, bo = cv(KC), cv(1), cv(G0 * HD)[0:KEYS0], cv(C)
            h = cv(2, C)[0:KEYS0]
            hT = cv(2, KC, KEYS0)
            qT = cv(2, KC, P)
            kT = cv(2, HP, KEYS0)
            v = cv(2, G0, HD + 1)[0:KEYS0]
            prob = cv(4 * KC, KEYS0)
            probT = cv(4 * KC, P)[0:KEYS0]
            o = cv(2, C)
            oT = cv(KC, P)
            h2 = cv(2, C)
            h2T = cv(KC, P)
            st1, st2 = cv(8), cv(8)
            r1, r2 = cv(2), cv(2)
            mx = cv(4 * KC)
            rsum = cv(4 * KC)
            lg = cv(NT, E)
            l16 = cv(5, NT)
            spare = cv(1)
            top = cv(NT, TOPK)
            idx_u = cv(NT, TOPK).bitcast(U32)
            idx_f = cv(NT, TOPK)

            (xa_in, w_in, ready, stats1, rstd1, xhat1, h_done, hT_mm, hT_out, q_mm, q_out, kv_mm, kv_out,
             s_mm, p_sub, p_exp, pT_mm, pT_act, pT_dve, o_mm, o_out, oT_mm, oT_out, wo_mm, x_pre, x_out,
             rstd2, xhat2, h2_done, h2T_mm, h2T_out, lg_mm, lg_shift, lg_exp, lg_out, store_h, dve_steps, pool_steps) = (
                psem("a_" + n) for n in
                ("xa_in", "w_in", "ready", "stats1", "rstd1", "xhat1", "h_done", "hT_mm", "hT_out", "q_mm", "q_out",
                 "kv_mm", "kv_out", "s_mm", "p_sub", "p_exp", "pT_mm", "pT_act", "pT_dve", "o_mm", "o_out", "oT_mm",
                 "oT_out", "wo_mm", "x_pre", "x_out", "rstd2", "xhat2", "h2_done", "h2T_mm", "h2T_out", "lg_mm",
                 "lg_shift", "lg_exp", "lg_out", "store_h", "dve_steps", "pool_steps"))
            h2_stored = [psem(f"a_h2_stored{b}") for b in range(2)]
            sq, kvb, tp = psum[5], psum[6], psum[7]
            N_DMA = 11

            def schedule(eng, turn, steps=None, per=0):
                def tile(t):
                    return (t, t % 2, t // 2) if 0 <= t < NT else None
                stages = (2, 1, 0, -1, -2)
                for m in range(-2, 4):
                    turn(*[tile(m + n) for n in stages])
                turns = (NT - 6) // 2
                with eng.Fori(0, turns) as i:
                    if steps:
                        steps.loop(i, per)
                    for m in (4, 5):
                        turn(*[(i * 2 + (m + n), (m + n) % 2, i + (m + n) // 2) for n in stages])
                if steps:
                    steps.end(turns)
                for m in range(NT - 2, NT + 2):
                    turn(*[tile(m + n) for n in stages])

            @block.sync
            def _(sp):
                xw = bass.AP(tensor=a["L0_attn_x"].tensor, offset=0, ap=[[C, KEYS0], [W0 * C, NT], [1, C]])
                sp.dma_start(xa[:], xw).then_inc(xa_in, 16)
                sp.dma_start(wq[:], a["L0_attn_Wq"].rearrange("(k p) n -> p k n", p=P)).then_inc(w_in, 16)
                wk_v = a["L0_attn_Wk"].rearrange("(k p) n -> p k n", p=P)
                sp.dma_start(wk[:, :, 0:W0], wk_v).then_inc(w_in, 16)
                sp.dma_start(wk[:, :, W0:P], wk_v).then_inc(w_in, 16)
                sp.dma_start(wv[:], a["L0_attn_Wv"].rearrange("(k p) n -> p k n", p=P)).then_inc(w_in, 16)
                sp.dma_start(wo[:], a["L0_attn_Wo"].rearrange("(k p) n -> p k n", p=P)).then_inc(w_in, 16)
                sp.dma_start(wgate[:], a["gate_T"].rearrange("(k p) n -> p k n", p=P)).then_inc(w_in, 16)
                sp.dma_start(bq, a["bq_cols"]).then_inc(w_in, 16)
                for r in range(2):
                    sp.dma_start(bk[W0 * r:W0 * r + W0], a["L0_attn_bk"].rearrange("(p o) -> p o", o=1)).then_inc(w_in, 16)
                sp.dma_start(bv, a["L0_attn_bv"].partition_broadcast(KEYS0)).then_inc(w_in, 16)
                sp.dma_start(bo, a["L0_attn_bo"].partition_broadcast(P)).then_inc(w_in, 16)

                def turn(g, f, m, w, z):
                    if z is not None:
                        t, b, half = z
                        wait_tile(sp, h2_done, 1, t)
                        rows = h_moe.rearrange("(t p) c -> p t c", p=P)
                        sp.dma_start(rows[:, t] if isinstance(t, int) else rows[:, bass.ds(t, 1)].rearrange("p o c -> p (o c)"),
                                     h2[:, b]).then_inc(h2_stored[b], 16)
                schedule(sp, turn)
                for b in range(2):
                    sp.wait_ge(h2_stored[b], 16 * NT // 2)

            @block.gpsimd
            def _(pool):
                st = Steps(pool, pool_steps)
                st.did(nc.gpsimd.memset(kT[:], 0.0))
                st.did(nc.gpsimd.memset(v[:], 1.0))
                st.settle()
                pool.sem_inc(ready, 1)

                def turn(g, f, m, w, z):
                    if z is not None:
                        t, b, _ = z
                        wait_tile(pool, xhat2, 1, t)
                        st.did(nc.gpsimd.tensor_tensor(h2[:, b], h2[:, b], mod[:, 0, 4], ALU.mult))
                        st.settle()
                        nc.gpsimd.tensor_tensor(h2[:, b], h2[:, b], mod[:, 0, 3], ALU.add).then_inc(h2_done, 1)
                    if w is not None:
                        pool.wait_ge(ready, 2)
                        xt = tile_of(x_res, w[0])
                        nc.gpsimd.tensor_tensor(xt, xt, bo, ALU.add).then_inc(x_pre, 1)
                    if g is not None:
                        t, b, _ = g
                        wait_tile(pool, stats1, 1, t)
                        nc.gpsimd.tensor_tensor(r1[0:KEYS0, 1:2], st1[0:KEYS0, 7:8], neg_half[0:KEYS0], ALU.pow).then_inc(rstd1, 1)
                        wait_tile(pool, xhat1, 1, t)
                        st.did(nc.gpsimd.tensor_tensor(h[:, b], h[:, b], mod[0:KEYS0, 0, 1], ALU.mult))
                        st.settle()
                        nc.gpsimd.tensor_tensor(h[:, b], h[:, b], mod[0:KEYS0, 0, 0], ALU.add).then_inc(h_done, 1)
                    if w is not None:
                        wait_tile(pool, x_out, 1, w[0])
                        nc.gpsimd.tensor_tensor(r2[:, 1:2], st2[:, 7:8], neg_half[:], ALU.pow).then_inc(rstd2, 1)
                schedule(pool, turn, st, POOL_A)

            def copy_probs(copy, t, c):
                return copy(probT[:, HP * c:HP * c + HP], psum[c][0:KEYS0].rearrange("p (h n) -> p h n", h=HP))

            @block.scalar
            def _(act):
                def turn(g, f, m, w, z):
                    if f is not None:
                        t, b, _ = f
                        wait_tile(act, hT_mm, 1, t)
                        wait_tile(act, kv_mm, 1, shift(t, -2))
                        nc.scalar.copy(hT[:, b], psum[4][:, 0:KC * KEYS0].rearrange("p (k n) -> p k n", k=KC)).then_inc(hT_out, 1)
                    if m is not None:
                        for c in range(KC):
                            wait_tile(act, p_sub, KC, m[0], c + 1)
                            some = prob[:, HP * c:HP * c + HP]
                            nc.scalar.activation(some, some, ACT.Exp, scale=SCALE0).then_inc(p_exp, 1)
                    if f is not None:
                        t, b, _ = f
                        wait_tile(act, q_mm, 1, t)
                        wait_tile(act, s_mm, KC, shift(t, -2))
                        for c in range(KC):
                            last = nc.scalar.activation(qT[:, b, c], sq[:, c * P:(c + 1) * P], ACT.Identity,
                                                        bias=bq[:, c:c + 1])
                        last.then_inc(q_out, 1)
                    if z is not None:
                        t, b, _ = z
                        wait_tile(act, h2T_mm, 1, t)
                        wait_tile(act, lg_mm, 1, shift(t, -1))
                        nc.scalar.copy(h2T.rearrange("p k n -> p (k n)"), tp[:]).then_inc(h2T_out, 1)
                    if m is not None:
                        t, b, _ = m
                        wait_tile(act, o_mm, 1, shift(t, -1))
                        for c in range(2):
                            wait_tile(act, pT_mm, KC, t, c + 1)
                            copy_probs(nc.scalar.copy, t, c).then_inc(pT_act, 1)
                    if w is not None:
                        t, b, _ = w
                        wait_tile(act, oT_mm, 1, t)
                        wait_tile(act, wo_mm, 1, shift(t, -1))
                        nc.scalar.copy(oT.rearrange("p k n -> p (k n)"), tp[:]).then_inc(oT_out, 1)
                schedule(act, turn)
                act.wait_ge(lg_shift, 1)
                nc.scalar.activation(lg[:], lg[:], ACT.Exp).then_inc(lg_exp, 1)

            @block.tensor
            def _(pe):
                def turn(g, f, m, w, z):
                    if m is not None:
                        t, b, _ = m
                        wait_tile(pe, q_out, 1, t)
                        wait_tile(pe, kv_out, 1, t)
                        wait_tile(pe, pT_act, 2, shift(t, -1))
                        wait_tile(pe, pT_dve, 2, shift(t, -1))
                        for c in range(KC):
                            bank = psum[c][:, 0:HP * KEYS0]
                            nc.tensor.matmul(bank, ident_b[:], mask0[:].unsqueeze(1).to_broadcast([P, HP, KEYS0]),
                                             start=True, stop=False)
                            nc.tensor.matmul(bank, qT[:, b, c], kT[:, b], start=False, stop=True).then_inc(s_mm, 1)
                    if f is not None:
                        t, b, _ = f
                        wait_tile(pe, h_done, 1, t)
                        wait_tile(pe, o_out, 1, shift(t, -2))
                        for k in range(KC):
                            mm = nc.tensor.transpose(psum[4][:, k * KEYS0:(k + 1) * KEYS0], h[:, b, k * P:(k + 1) * P],
                                                     ident[0:KEYS0, 0:KEYS0])
                        mm.then_inc(hT_mm, 1)
                        wait_tile(pe, hT_out, 1, t)
                        pe.wait_ge(w_in, 16 * N_DMA)
                        for c in range(KC):
                            for k in range(KC):
                                mm = nc.tensor.matmul(sq[:, c * P:(c + 1) * P], wq[:, k, c * P:(c + 1) * P], windows(hT[:, b, k]),
                                                      start=(k == 0), stop=(k == KC - 1))
                        mm.then_inc(q_mm, 1)
                    if z is not None:
                        t, b, _ = z
                        wait_tile(pe, h2_done, 1, t)
                        for k in range(KC):
                            mm = nc.tensor.transpose(tp[:, k * P:(k + 1) * P], h2[:, b, k * P:(k + 1) * P], ident[:])
                        mm.then_inc(h2T_mm, 1)
                    if m is not None:
                        t, b, _ = m
                        for c in range(KC):
                            wait_tile(pe, p_exp, KC, t, c + 1)
                            for j in range(HP):
                                mm = nc.tensor.transpose(psum[c][0:KEYS0, j * P:(j + 1) * P], prob[:, HP * c + j], ident[:])
                            mm.then_inc(pT_mm, 1)
                    if w is not None:
                        t, b, _ = w
                        wait_tile(pe, o_out, 1, t)
                        if z is not None:
                            wait_tile(pe, h2T_out, 1, z[0])
                        for k in range(KC):
                            mm = nc.tensor.transpose(tp[:, k * P:(k + 1) * P], o[:, b, k * P:(k + 1) * P], ident[:])
                        mm.then_inc(oT_mm, 1)
                    if f is not None:
                        wait_tile(pe, kv_out, 1, shift(f[0], -1))
                    if z is not None:
                        t, b, _ = z
                        wait_tile(pe, lg_out, 1, shift(t, -1))
                        wait_tile(pe, h2T_out, 1, t)
                        for k in range(KC):
                            mm = nc.tensor.matmul(kvb[:, 2 * P:2 * P + E], h2T[:, k], wgate[:, k], start=(k == 0), stop=(k == KC - 1))
                        mm.then_inc(lg_mm, 1)
                    if f is not None:
                        t, b, _ = f
                        for k in range(KC):
                            nc.tensor.matmul(kvb[:, 0:KEYS0], wk[:, k], hT[:, b, k], start=(k == 0), stop=(k == KC - 1))
                        for k in range(KC):
                            mm = nc.tensor.matmul(kvb[0:KEYS0, P:P + G0 * HD], hT[:, b, k], wv[:, k],
                                                  start=(k == 0), stop=(k == KC - 1))
                        mm.then_inc(kv_mm, 1)
                    if w is not None:
                        t, b, _ = w
                        wait_tile(pe, oT_out, 1, t)
                        pe.wait_ge(ready, 2)
                        for k in range(KC):
                            mm = nc.tensor.matmul(tp[:], oT[:, k], wo[:, k], start=(k == 0), stop=(k == KC - 1))
                        mm.then_inc(wo_mm, 1)
                    if m is not None:
                        t, b, _ = m
                        if f is not None:
                            wait_tile(pe, q_out, 1, f[0])
                            wait_tile(pe, hT_out, 1, f[0])
                        for n in range(4 * KC):
                            if n % (2 * HP) == 0:
                                wait_tile(pe, pT_act if n == 0 else pT_dve, 2, t)
                            mm = nc.tensor.matmul(o_at(n), probT[:, n], v[:, b, n % G0], start=True, stop=True)
                        mm.then_inc(o_mm, 1)

                def o_at(n):
                    q = HD + 1
                    return psum[4 + n // 8][:, (n % 8) * q:(n % 8 + 1) * q]
                pe.wait_ge(ready, 1)
                schedule(pe, turn)

            @block.vector
            def _(dve):
                st = Steps(dve, dve_steps)

                def absorb():
                    st.settle()
                    st.did(nc.vector.memset(spare[0:1], 0.0))
                dve.wait_ge(w_in, 16 * N_DMA)
                st.did(nc.vector.tensor_tensor(wo[:], wo[:], mod[:, 0, 2].unsqueeze(1).to_broadcast([P, KC, C]), ALU.mult))
                st.did(nc.vector.tensor_tensor(bo, bo, mod[:, 0, 2], ALU.mult))
                dve.wait_ge(ready, 1)
                st.settle()
                dve.sem_inc(ready, 1)
                dve.wait_ge(xa_in, 16)

                def norm_stats(x, st8, rows, done):
                    absorb()
                    st.did(nc.vector.bn_stats(st8[rows, 0:6], x))
                    absorb()
                    st.did(nc.vector.bn_aggr(st8[rows, 6:8], st8[rows, 0:6]))
                    st.settle()
                    nc.vector.tensor_scalar(st8[rows, 7:8], st8[rows, 7:8], EPS, None, ALU.add).then_inc(done, 1)

                def turn(g, f, m, w, z):
                    if w is not None:
                        t, b, _ = w
                        wait_tile(dve, o_mm, 1, t)
                        wait_tile(dve, oT_mm, 1, shift(t, -2))
                        for i in range(2):
                            ob = psum[4 + i][:, 0:8 * (HD + 1)].rearrange("p (h d) -> p h d", h=8)
                            st.did(nc.vector.reciprocal(rsum[:, 8 * i:8 * i + 8].unsqueeze(2), ob[:, :, HD:HD + 1]))
                        st.settle()
                        for i in range(2):
                            ob = psum[4 + i][:, 0:8 * (HD + 1)].rearrange("p (h d) -> p h d", h=8)
                            last = nc.vector.tensor_tensor(o[:, b, 256 * i:256 * i + 256].rearrange("p (h d) -> p h d", h=8), ob[:, :, 0:HD],
                                                           rsum[:, 8 * i:8 * i + 8].unsqueeze(2).to_broadcast([P, 8, HD]), ALU.mult)
                        last.then_inc(o_out, 1)
                    if z is not None:
                        t, b, half = z
                        wait_tile(dve, rstd2, 1, t)
                        wait_tile(dve, x_out, 1, t)
                        wait_tile(dve, h2T_mm, 1, shift(t, -2))
                        wait_tile(dve, h2_stored[b], 16, shift(half, -1))
                        nc.vector.tensor_scalar(h2[:, b], tile_of(x_res, t), st2[:, 6:7], r2[:, 1:2], ALU.subtract, ALU.mult).then_inc(xhat2, 1)
                    if m is not None:
                        t, b, _ = m
                        wait_tile(dve, pT_mm, KC, shift(t, -1))
                        scores = lambda c: psum[c][:, 0:HP * KEYS0].rearrange("p (h n) -> p h n", h=HP)
                        for c in range(KC + 1):
                            if c < KC:
                                wait_tile(dve, s_mm, KC, t, c + 1)
                                st.did(nc.vector.tensor_reduce(mx[:, HP * c:HP * c + HP], scores(c), AX.X, ALU.max))
                            if c:
                                if c == KC:
                                    st.settle()
                                else:
                                    dve.wait_ge(dve_steps, st.base + (st.k - 1))
                                i = slice(HP * c - HP, HP * c)
                                nc.vector.tensor_tensor(prob[:, i], scores(c - 1), mx[:, i].unsqueeze(2).to_broadcast([P, HP, KEYS0]),
                                                        ALU.subtract).then_inc(p_sub, 1)
                    if g is not None:
                        wait_tile(dve, xhat1, 1, shift(g[0], -1))
                        norm_stats(tile_of(xa, g[0]), st1, slice(0, KEYS0), stats1)
                    if m is not None:
                        t, b, _ = m
                        wait_tile(dve, o_mm, 1, shift(t, -1))
                        for c in range(2, KC):
                            wait_tile(dve, pT_mm, KC, t, c + 1)
                            copy_probs(nc.vector.tensor_copy, t, c).then_inc(pT_dve, 1)
                    if g is not None:
                        t, b, _ = g
                        wait_tile(dve, rstd1, 1, t)
                        wait_tile(dve, stats1, 1, t)
                        wait_tile(dve, hT_mm, 1, shift(t, -2))
                        nc.vector.tensor_scalar(h[:, b], tile_of(xa, t), st1[0:KEYS0, 6:7], r1[0:KEYS0, 1:2],
                                                ALU.subtract, ALU.mult).then_inc(xhat1, 1)
                    if z is not None:
                        t, b, _ = z
                        wait_tile(dve, lg_mm, 1, t)
                    if f is not None:
                        t, b, _ = f
                        wait_tile(dve, kv_mm, 1, t)
                        wait_tile(dve, s_mm, KC, shift(t, -2))
                        wait_tile(dve, o_mm, 1, shift(t, -2))
                        for r in range(HP):
                            q = slice(HD * r, HD * r + HD)
                            nc.vector.tensor_scalar(kT[q, b, r], kvb[q, 0:KEYS0], bk[q], None, ALU.add)
                        nc.vector.tensor_tensor(v[:, b, :, 0:HD], kvb[0:KEYS0, P:P + G0 * HD].rearrange("p (g d) -> p g d", g=G0),
                                                bv.rearrange("p (g d) -> p g d", g=G0), ALU.add).then_inc(kv_out, 1)
                    if z is not None:
                        nc.vector.tensor_copy(tile_of(lg, z[0]), kvb[:, 2 * P:2 * P + E]).then_inc(lg_out, 1)
                    if w is not None:
                        t, b, _ = w
                        xt = tile_of(x_res, t)
                        wait_tile(dve, wo_mm, 1, t)
                        wait_tile(dve, x_pre, 1, t)
                        wait_tile(dve, xhat2, 1, shift(t, -1))
                        st.did(nc.vector.tensor_tensor(xt, tp[:], xt, ALU.add))
                        norm_stats(xt, st2, slice(0, P), x_out)
                schedule(dve, turn, st, DVE_A)

                def step(ins):
                    st.did(ins)
                    st.settle()
                over = lambda x, n: x.unsqueeze(2).to_broadcast([P, NT, n])
                dve.wait_ge(lg_out, NT)
                step(nc.vector.tensor_reduce(l16[:, 0], lg[:], AX.X, ALU.max))
                nc.vector.tensor_tensor(lg[:], lg[:], over(l16[:, 0], E), ALU.subtract).then_inc(lg_shift, 1)
                dve.wait_ge(lg_exp, 1)
                step(nc.vector.tensor_reduce(l16[:, 1], lg[:], AX.X, ALU.add))
                step(nc.vector.reciprocal(l16[:, 2], l16[:, 1]))
                st.did(nc.vector.tensor_tensor(lg[:], lg[:], over(l16[:, 2], E), ALU.mult))
                absorb()
                absorb()
                for t in range(NT):
                    st.did(nc.vector.max(top[:, t], lg[:, t]))
                absorb()
                absorb()
                for t in range(NT):
                    st.did(nc.vector.max_index(idx_u[:, t], top[:, t], lg[:, t]))
                step(nc.vector.tensor_reduce(l16[:, 3], top[:], AX.X, ALU.add))
                step(nc.vector.tensor_scalar(l16[:, 3], l16[:, 3], 1e-12, None, ALU.max))
                step(nc.vector.reciprocal(l16[:, 4], l16[:, 3]))
                st.did(nc.vector.tensor_tensor(route_w[:], top[:], over(l16[:, 4], TOPK), ALU.mult))
                step(nc.vector.tensor_copy(idx_f[:], idx_u[:]))
                for t in range(NT):
                    st.did(nc.vector.tensor_tensor(route_hot[:, t], idx_f[:, t].unsqueeze(2).to_broadcast([P, TOPK, E]),
                                                   iota_row[:].unsqueeze(1).to_broadcast([P, TOPK, E]), ALU.is_equal))
                st.settle()

        with ExitStack() as ph, nc.Block() as block:
            psem = phase_semaphores(ph)

            cv = Carver(FT * C)
            SCR = cv.at
            back = cv(FT, C)
            sim = cv(E)[0:E]
            cand = cv(E)[0:E]
            best, best_f = cv(8)[0:E], cv(8)[0:E]
            best_u = cv(8)[0:E].bitcast(U32)
            cnt_j = cv(2 * E)
            dtmp = cv(2, E)[0:E]
            sec = cv(8)[0:E]
            diag = cv(E // 2).bitcast(BF16)[0:E]
            map_row = cv(E)
            chosen = cv(NT * E // 2).bitcast(BF16).rearrange("p (t e) -> p t e", t=NT)
            moved = cv(NT, SELK)
            counts, upto = cv(E, NT), cv(E, NT)
            again = cv(E, NT)
            tiles_f, tile_end = cv(E), cv(E)
            base, ones_row = cv(E), cv(E)
            tiles_i = cv(E).bitcast(I32)
            pos = cv(NT, E)
            gcol = cv(4)
            picked = cv(2, TOPK, E)
            pos_f = cv(NT, TOPK)
            tok_i = cv(NT).bitcast(I32)
            tok_f = cv(NT)
            st_pos = cv(2, TOPK).bitcast(I32)
            st_tok = cv(2, 1)
            su_dp = cv(FT)
            dtmp0 = cv(2 * E)
            spare = cv(1)
            slots_in_row = cv(2 * P)[0:SLOTS // 2]
            (r_in, wd_in, n_mm, d_rows, map_mm, sel_done, rank_mm, eid_done, eid_mm, had_mm, had_out,
             wide, tok_done, staged, slots_in, slot_mm, dve_steps, pool_steps) = (
                psem("r_" + n) for n in
                ("r_in", "wd_in", "n_mm", "d_rows", "map_mm", "sel_done", "rank_mm", "eid_done", "eid_mm", "had_mm",
                 "had_out", "wide", "tok_done", "staged", "slots_in", "slot_mm", "dve_steps", "pool_steps"))
            scattered = [psem(f"r_scattered{b}") for b in range(2)]
            pos_done = psem("r_pos_done")

            @block.sync
            def _(sp):
                sp.dma_start(sim, a["L0_ffn_similarity"]).then_inc(r_in, 16)
                sp.dma_start(su_dp, a["su_dp_cols"]).then_inc(r_in, 16)
                sp.dma_start(wd[:], a["ffn_down"]).then_inc(wd_in, 16)
                for b in range(2):
                    sp.wait_ge(scattered[b], 16 * TOPK * NT // 2)
                sp.dma_start(slots_in_row, slot_token.rearrange("(q n) o -> q (n o)", n=2 * P)).then_inc(slots_in, 16)
                sp.wait_ge(slots_in, 16)

            @block.gpsimd
            def _(pool):
                st = Steps(pool, pool_steps)
                st.did(nc.gpsimd.iota(tok_i[:], [[P, NT]], base=0, channel_multiplier=1))
                st.settle()
                nc.gpsimd.tensor_copy(tok_f, tok_i[:]).then_inc(tok_done, 1)
                pool.wait_ge(tok_done, 1)

                def scatter(t, b, half):
                    if not isinstance(t, int) or t >= 2:
                        wait_tile(pool, scattered[b], 16 * TOPK, shift(half, -1))
                    wait_tile(pool, pos_done, 1, t)
                    st.did(nc.gpsimd.tensor_copy(st_pos[:, b], tile_of(pos_u, t)))
                    st.did(nc.gpsimd.tensor_copy(st_tok[:, b], tok_f[:, t:t + 1] if isinstance(t, int) else tok_f[:, bass.ds(t, 1)]))
                    st.settle()
                    st.did(nc.gpsimd.tensor_tensor(spare, neg_half[:], neg_half[:], ALU.add))
                    for j in range(TOPK):
                        nc.gpsimd.indirect_dma_start(out=slot_token, out_offset=bass.IndirectOffsetOnAxis(ap=st_pos[:, b, j:j + 1], axis=0),
                                                     in_=st_tok[:, b], in_offset=None).then_inc(scattered[b], 16)
                scatter(0, 0, 0)
                scatter(1, 1, 0)
                with pool.Fori(0, NT // 2 - 1) as i:
                    st.loop(i, 6)
                    scatter(i * 2 + 2, 0, i + 1)
                    scatter(i * 2 + 3, 1, i + 1)
                st.end(NT // 2 - 1)

            @block.tensor
            def _(pe):
                hot = route_hot[:].rearrange("p t j e -> p t (j e)")
                for t in range(NT):
                    mm = nc.tensor.matmul(psum[0][:], ones_b[:], hot[:, t], start=(t == 0), stop=(t == NT - 1))
                mm.then_inc(n_mm, 1)
                pe.wait_ge(d_rows, 1)
                nc.tensor.matmul(psum[1][:, 0:E], ones_b[0:E], diag, start=True, stop=True).then_inc(map_mm, 1)
                pe.wait_ge(sel_done, 1)
                ch = chosen.rearrange("p (h t) e -> p h (t e)", h=2)
                for n in range(2):
                    nc.tensor.matmul(psum[2 + n][:], upper_b[:], ch[:, n], start=True, stop=True)
                    mm = nc.tensor.matmul(psum[4 + n][:], ones_b[:], ch[:, n], start=True, stop=True)
                mm.then_inc(rank_mm, 1)
                pe.wait_ge(eid_done, 1)
                for n in range(2):
                    mm = nc.tensor.transpose(psum[6][0:1, n * P:(n + 1) * P], gcol[:, n:n + 1], ident[:])
                mm.then_inc(eid_mm, 1)
                pe.wait_ge(wd_in, 16)
                for f in range(FT):
                    if f >= 2:
                        pe.wait_ge(had_out, f - 1)
                    nc.tensor.matmul(psum[f % 2][:], had[:], wd[:, f], start=True, stop=True).then_inc(had_mm, 1)
                pe.wait_ge(slots_in, 16)
                for n in range(2):
                    mm = nc.tensor.transpose(psum[7][:, n * (SLOTS // 2):(n + 1) * (SLOTS // 2)],
                                             slots_in_row[:, n * P:(n + 1) * P], ident[0:SLOTS // 2, 0:SLOTS // 2])
                mm.then_inc(slot_mm, 1)

            @block.vector
            def _(dve):
                st = Steps(dve, dve_steps)

                def step(ins):
                    st.did(ins)
                    st.settle()

                tt, ts = nc.vector.tensor_tensor, nc.vector.tensor_scalar
                dve.wait_ge(r_in, 32)
                st.did(ts(dtmp[:, 0], ident[0:E, 0:E], -1.0, 1.0, ALU.mult, ALU.add))
                st.did(nc.vector.memset(again[:], 1.0))
                st.did(nc.vector.memset(ones_row, 1.0))
                st.settle()
                st.did(nc.vector.memset(again[:, :, 0:1], 0.0))
                step(tt(dtmp[:, 1], sim, dtmp[:, 0], ALU.mult))
                step(tt(sim, dtmp[:, 1], ident[0:E, 0:E], ALU.add))
                dve.wait_ge(n_mm, 1)
                cj = psum[0][:].rearrange("p (h j e) -> p h e j", h=2, j=SELK)
                step(nc.vector.tensor_reduce(cnt_j.rearrange("p (h e) -> p h e", h=2), cj, AX.X, ALU.add))
                step(ts(cnt_j, cnt_j, 1.0, None, ALU.min))
                prim, secd = cnt_j[0:E, 0:E], cnt_j[0:E, E:2 * E]
                st.did(tt(dtmp[:, 0], sim, prim, ALU.mult))
                st.did(ts(dtmp[:, 1], prim, -1.0, 3e38, ALU.add, ALU.mult))
                st.settle()
                step(tt(cand, dtmp[:, 0], dtmp[:, 1], ALU.add))
                step(nc.vector.max(best, cand))
                step(nc.vector.max_index(best_u, best, cand))
                st.did(nc.vector.tensor_copy(best_f, best_u))
                st.did(tt(dtmp[:, 0], prim, ident[0:E, 0:E], ALU.mult))
                st.did(tt(dtmp[:, 1], secd, ident[0:E, 0:E], ALU.mult))
                st.settle()
                step(nc.vector.tensor_reduce(sec[:, 0:2], dtmp[:], AX.X, ALU.add))
                st.did(ts(sec[:, 2:3], sec[:, 0:1], -1.0, 1.0, ALU.mult, ALU.add))
                st.did(ts(sec[:, 3:4], best[:, 0:1], THRESH, None, ALU.is_ge))
                st.did(tt(sec[:, 5:6], best_f[:, 0:1], iota_col[0:E], ALU.subtract))
                st.settle()
                step(tt(sec[:, 4:5], sec[:, 1:2], sec[:, 2:3], ALU.mult))
                step(tt(sec[:, 4:5], sec[:, 4:5], sec[:, 3:4], ALU.mult))
                step(tt(sec[:, 5:6], sec[:, 5:6], sec[:, 4:5], ALU.mult))
                step(tt(sec[:, 6:7], sec[:, 5:6], iota_col[0:E], ALU.add))
                ts(diag, ident[0:E, 0:E], sec[:, 6:7], None, ALU.mult).then_inc(d_rows, 1)
                dve.wait_ge(map_mm, 1)
                step(nc.vector.tensor_copy(map_row, psum[1][:, 0:E]))
                flat = back[:].rearrange("p f c -> p (f c)")
                prod = flat[:, 0:SELK * NT * E // 2].bitcast(BF16).rearrange("p (t j e) -> p t j e", t=NT, j=SELK)
                for t in range(NT):
                    st.did(tt(prod[:, t], route_hot[:, t, SELK:], map_row.unsqueeze(1).to_broadcast([P, SELK, E]), ALU.mult))
                st.settle()
                step(nc.vector.tensor_reduce(moved[:], prod, AX.X, ALU.add))
                for t in range(NT):
                    st.did(tt(route_hot[:, t, SELK:], moved[:, t].unsqueeze(2).to_broadcast([P, SELK, E]),
                              iota_row[:].unsqueeze(1).to_broadcast([P, SELK, E]), ALU.is_equal))
                st.settle()
                nc.vector.tensor_reduce(chosen, route_hot[:].rearrange("p t j e -> p t e j"), AX.X, ALU.max).then_inc(sel_done, 1)
                dve.wait_ge(rank_mm, 1)
                for n in range(2):
                    half = psum[4 + n][:].rearrange("p (t e) -> p e t", e=E)
                    st.did(nc.vector.tensor_copy(counts[:, :, 8 * n:8 * n + 8], half))
                st.settle()
                fl = "p e t -> p (e t)"
                step(nc.vector.tensor_tensor_scan(upto.rearrange(fl), again.rearrange(fl), counts.rearrange(fl), 0.0, ALU.mult, ALU.add))
                st.did(ts(tiles_f.unsqueeze(2), upto[:, :, NT - 1:NT], float(P - 1), None, ALU.add))
                st.did(tt(counts[:], upto[:], counts[:], ALU.subtract))
                st.settle()
                step(nc.vector.tensor_copy(tiles_i, tiles_f))
                step(ts(tiles_i, tiles_i, 7, None, ALU.logical_shift_right))
                step(nc.vector.tensor_copy(tiles_f, tiles_i))
                step(ts(tiles_f, tiles_f, 1.0, None, ALU.max))
                step(nc.vector.tensor_tensor_scan(tile_end, ones_row, tiles_f, 0.0, ALU.mult, ALU.add))
                step(tt(base, tile_end, tiles_f, ALU.subtract))
                step(ts(base, base, float(P), None, ALU.mult))
                for n in range(2):
                    st.did(tt(pos[:, 8 * n:8 * n + 8], psum[2 + n][:].rearrange("p (t e) -> p t e", e=E),
                              base.unsqueeze(1).to_broadcast([P, 8, E]), ALU.add))
                st.settle()
                step(tt(pos[:], pos[:], counts.rearrange("p e t -> p t e"), ALU.add))
                for t in range(NT):
                    if t >= 2:
                        dve.wait_ge(pos_done, t - 1)
                    step(tt(picked[:, t % 2], route_hot[:, t], pos[:, t].unsqueeze(1).to_broadcast([P, TOPK, E]), ALU.mult))
                    step(nc.vector.tensor_reduce(pos_f[:, t], picked[:, t % 2], AX.X, ALU.add))
                    nc.vector.tensor_copy(pos_u[:, t], pos_f[:, t]).then_inc(pos_done, 1)
                step(ts(gcol[:, 2:3], iota_col[:], float(P), None, ALU.add))
                st.did(nc.vector.tensor_scalar(dtmp0[:, 0:E], tile_end, iota_col[:], None, ALU.is_le, ALU.add, accum_out=gcol[:, 0:1]))
                st.did(nc.vector.tensor_scalar(dtmp0[:, E:], tile_end, gcol[:, 2:3], None, ALU.is_le, ALU.add, accum_out=gcol[:, 1:2]))
                st.settle()
                ts(gcol[:, 0:2], gcol[:, 0:2], float(E - 1), None, ALU.min).then_inc(eid_done, 1)
                dve.wait_ge(eid_mm, 1)
                st.did(nc.vector.tensor_copy(tile_expert[:, 0:SLOTS], psum[6][0:1, 0:SLOTS]))
                st.did(ts(expert_end[:], tile_end[0:1], 1.0, None, ALU.add))
                for f in range(FT):
                    dve.wait_ge(had_mm, f + 1)
                    nc.vector.tensor_copy(wd[:, f], psum[f % 2][:]).then_inc(had_out, 1)
                dve.wait_ge(had_out, FT)
                src, dst = wd, back
                n = 1
                while n < FT:
                    sv = src[:].rearrange("p (a two n) c -> p a two (n c)", two=2, n=n)
                    dv = dst[:].rearrange("p (a two n) c -> p a two (n c)", two=2, n=n)
                    st.settle()
                    st.did(tt(dv[:, :, 0], sv[:, :, 0], sv[:, :, 1], ALU.add))
                    st.did(tt(dv[:, :, 1], sv[:, :, 0], sv[:, :, 1], ALU.subtract))
                    src, dst = dst, src
                    n *= 2
                st.settle()
                for f in range(FT):
                    st.did(nc.vector.scalar_tensor_tensor(wd[:, f], wd[:, f], su_dp[:, f:f + 1], down_scale[:], ALU.mult, ALU.mult))
                dve.wait_ge(slot_mm, 1)
                st.did(nc.vector.tensor_copy(slot_rows[:, 0:SLOTS].rearrange("p (q n) -> p n q", n=2),
                                             psum[7][:, 0:SLOTS].rearrange("p (n q) -> p n q", n=2)))
                st.settle()


        with ExitStack() as ph, nc.Block() as block:
            psem = phase_semaphores(ph)

            cv = Carver(FT * C)
            UPW, DOWNW = KC * 2 * FI, 2 * C
            up_ring = cv(RING * UPW)
            down_ring = cv(RING * DOWNW)[0:FH]
            xg = cv(2, C)
            xgT = cv(2, KC, P)
            gate_act = cv(2, FI)
            hidden = cv(2, FI)
            hiddenT = cv(2, 2, P)[0:FH]
            y = cv(2, C)
            st_tok = cv(2, 1).bitcast(I32)
            spare = cv(1)
            (experts_ready, xT_mm, xT_out, gu_mm, gate_done, hidden_done, hT_mm, hT_out, y_mm, y_out,
             pool_steps) = (psem("m_" + n) for n in
                            ("experts_ready",  "xT_mm", "xT_out", "gu_mm", "gate_done", "hidden_done",
                             "hT_mm", "hT_out", "y_mm", "y_out", "pool_steps"))
            w_in = [psem(f"m_w_in{r}") for r in range(RING)]
            x_in = [psem(f"m_x_in{b}") for b in range(2)]
            y_stored = [psem(f"m_y_stored{b}") for b in range(2)]

            def schedule(eng, turn, steps=None, per=0, unused=None):
                def tile(t):
                    return (t, t % 2, t // 2) if t >= 0 else None
                used = eng.value_load(expert_end[0:1, E - 1:E], min_val=E + 1, max_val=SLOTS + 1) - 1
                for g in range(-1, 3):
                    turn(tile(g - 1) if g > 0 else None, tile(g), tile(g + 1))
                with eng.Fori(0, (SLOTS - 2) // 2) as i:
                    with eng.If(i * 2 + 2 < used):
                        if steps:
                            steps.loop(i, per)
                        turn((i * 2 + 2, 0, i + 1), (i * 2 + 3, 1, i + 1), (i * 2 + 4, 0, i + 2))
                        turn((i * 2 + 3, 1, i + 1), (i * 2 + 4, 0, i + 2), (i * 2 + 5, 1, i + 2))
                    if unused:
                        with eng.Else():
                            unused(i * 2 + 2, 0)
                            unused(i * 2 + 3, 1)

            @block.sync
            def _(sp):
                def load(e, r):
                    up, down = a["moe_up"], a["moe_down"]
                    one = (lambda x: x[e]) if isinstance(e, int) else (lambda x: x[bass.ds(e, 1)].rearrange("o p k n -> (o p) k n"))
                    sp.dma_start(up_ring[:, r * UPW:(r + 1) * UPW], one(up).rearrange("p k n -> p (k n)")).then_inc(w_in[r], 16)
                    sp.dma_start(down_ring[:, r * DOWNW:(r + 1) * DOWNW], one(down).rearrange("p k n -> p (k n)")).then_inc(w_in[r], 16)

                def landed(e, r):
                    sp.wait_ge(w_in[r], e)
                    sp.sem_inc(experts_ready, 1)

                for e in range(RING):
                    load(e, e)
                    if e:
                        landed(32, e - 1)
                with sp.Fori(1, E // RING) as n:
                    for r in range(RING):
                        e = n * RING + r
                        done = sp.value_load(expert_end[0:1, bass.ds(e - RING, 1)], min_val=2, max_val=SLOTS + 1)
                        sp.wait_ge(y_mm, done)
                        load(e, r)
                        landed(n * 32 if r == 0 else n * 32 + 32, (r - 1) % RING)
                landed(32 * E // RING, RING - 1)

            @block.gpsimd
            def _(pool):
                st = Steps(pool, pool_steps)

                def turn(before, g, after):
                    if after is not None:
                        t, b, half = after
                        wait_tile(pool, x_in[b], 16, shift(half, -1))
                        st.did(nc.gpsimd.tensor_copy(st_tok[:, b], slot_rows[:, t:t + 1] if isinstance(t, int) else slot_rows[:, bass.ds(t, 1)]))
                        st.settle()
                        st.did(nc.gpsimd.tensor_tensor(spare, neg_half[:], neg_half[:], ALU.add))
                        wait_tile(pool, xT_mm, 1, shift(t, -2))
                        st.settle()
                        st.did(nc.gpsimd.tensor_tensor(spare, neg_half[:], neg_half[:], ALU.add))
                        nc.gpsimd.indirect_dma_start(out=xg[:, b], out_offset=None, in_=h_moe,
                                                     in_offset=bass.IndirectOffsetOnAxis(ap=st_tok[:, b], axis=0)).then_inc(x_in[b], 16)
                schedule(pool, turn, st, POOL_M)

            @block.tensor
            def _(pe):
                def turn(before, g, after):
                    if before is not None:
                        t, b, _ = before
                        wait_tile(pe, hidden_done, 1, t)
                        wait_tile(pe, hT_out, 1, shift(t, -2))
                        for n in range(2):
                            mm = nc.tensor.transpose(psum[4 + b][0:FH, n * P:(n + 1) * P], hidden[:, b, n * FH:(n + 1) * FH], ident[:])
                        mm.then_inc(hT_mm, 1)
                    if g is not None:
                        t, b, _ = g
                        e = pe.value_load(tile_expert[0:1, bass.ds(t, 1)], min_val=0, max_val=E - 1)
                        wait_tile(pe, xT_out, 1, t)
                        wait_tile(pe, hidden_done, 1, shift(t, -2))
                        pe.wait_ge(experts_ready, e + 1)
                        for k in range(KC):
                            mm = nc.tensor.matmul(psum[2 + b][:, 0:2 * FI], xgT[:, b, k],
                                                  up_ring[:, bass.ds((e % RING) * UPW + k * 2 * FI, 2 * FI)],
                                                  start=(k == 0), stop=(k == KC - 1))
                        mm.then_inc(gu_mm, 1)
                    if after is not None:
                        t, b, half = after
                        wait_tile(pe, x_in[b], 16, half)
                        wait_tile(pe, xT_out, 1, shift(t, -2))
                        for k in range(KC):
                            mm = nc.tensor.transpose(psum[b][:, k * P:(k + 1) * P], xg[:, b, k * P:(k + 1) * P], ident[:])
                        mm.then_inc(xT_mm, 1)
                    if before is not None:
                        t, b, _ = before
                        e = pe.value_load(tile_expert[0:1, bass.ds(t, 1)], min_val=0, max_val=E - 1)
                        wait_tile(pe, hT_out, 1, t)
                        wait_tile(pe, y_out, 1, shift(t, -2))
                        for n in range(2):
                            mm = nc.tensor.matmul(psum[6 + b][:], hiddenT[:, b, n],
                                                  down_ring[:, bass.ds((e % RING) * DOWNW + n * C, C)],
                                                  start=(n == 0), stop=(n == 1))
                        mm.then_inc(y_mm, 1)
                pe.sem_inc(y_mm, 1)
                schedule(pe, turn)

            @block.scalar
            def _(act):
                y_rows = y_moe.rearrange("(g p) c -> g p c", p=P)

                def turn(before, g, after):
                    if before is not None:
                        t, b, _ = before
                        wait_tile(act, hT_mm, 1, t)
                        wait_tile(act, y_mm, 1, shift(t, -2), 2)
                        nc.scalar.copy(hiddenT[:, b], psum[4 + b][0:FH, 0:2 * P].rearrange("p (n q) -> p n q", n=2)).then_inc(hT_out, 1)
                    if g is not None:
                        t, b, _ = g
                        wait_tile(act, gu_mm, 1, t)
                        wait_tile(act, hidden_done, 1, shift(t, -2))
                        nc.scalar.activation(gate_act[:, b], psum[2 + b][:, 0:FI], ACT.Silu).then_inc(gate_done, 1)
                    if after is not None:
                        t, b, _ = after
                        wait_tile(act, xT_mm, 1, t)
                        wait_tile(act, gu_mm, 1, shift(t, -2))
                        nc.scalar.copy(xgT[:, b].rearrange("p k n -> p (k n)"), psum[b][:]).then_inc(xT_out, 1)
                    if before is not None:
                        t, b, _ = before
                        wait_tile(act, y_out, 1, t)
                        dst = y_rows[t] if isinstance(t, int) else y_rows[bass.ds(t, 1)].rearrange("o p c -> (o p) c")
                        act.dma_start(dst, y[:, b]).then_inc(y_stored[b], 16)

                def unused(t, b):
                    act.dma_start(y_rows[bass.ds(t, 1)].rearrange("o p c -> (o p) c"), x_res[:, 0]).then_inc(y_stored[b], 16)
                schedule(act, turn, unused=unused)
                for b in range(2):
                    act.wait_ge(y_stored[b], 16 * SLOTS // 2)

            @block.vector
            def _(dve):
                def turn(before, g, after):
                    if g is not None:
                        t, b, _ = g
                        wait_tile(dve, gate_done, 1, t)
                        wait_tile(dve, hT_mm, 1, shift(t, -2))
                        nc.vector.tensor_tensor(hidden[:, b], gate_act[:, b], psum[2 + b][:, FI:2 * FI], ALU.mult).then_inc(hidden_done, 1)
                    if before is not None:
                        t, b, half = before
                        wait_tile(dve, y_mm, 1, t, 2)
                        wait_tile(dve, y_stored[b], 16, shift(half, -1))
                        nc.vector.tensor_tensor(y[:, b], psum[6 + b][:], mod[:, 0, 5], ALU.mult).then_inc(y_out, 1)
                schedule(dve, turn)


        with ExitStack() as ph, nc.Block() as block:
            psem = phase_semaphores(ph)

            NHEAD = C // HD
            NQK = NHEAD + NKV1
            V1 = HD + 1
            cv = Carver(FT * C)
            wq, wkv, wo = cv(KC, C), cv(KC, 2 * NKV1 * HD), cv(KC, C)
            bqk_row, bv_row, bo = cv(NQK * HD), cv(NKV1 * HD), cv(C)
            rope = cv(2, 4, HD)
            yg = cv(TOPK, C)
            kT = cv(NKV1, HP, KEYS1)
            qT = cv(KC, P)
            qk = cv(2, NQK, HD)
            rot = cv(NQK, HD)
            vrow = cv(2, NKV1, HD)
            v = cv(2, NKV1, V1)
            v_meta = cv(NKV1, V1)
            prob = cv(4, KEYS1)
            probT = cv(4, 3 * P)
            kx = cv(NKV1, HP, HD)
            hT = cv(KC, P)
            h = cv(C)
            o = cv(2, C)
            oT = cv(KC, P)
            st1, r1 = cv(8), cv(2)
            nmx = cv(2, NHEAD)
            rsum = cv(2, NHEAD)
            st_pos = cv(TOPK).bitcast(I32)
            spare = cv(2)
            names = ("w_in", "ready", "y_sum", "stats", "rstd", "xhat", "h_done", "hT_mm", "hT_out", "q_mm", "kv_mm", "q_rows",
                     "kv_rows", "roped", "kx_done", "kT_mm", "qT_mm", "k_act", "k_dve", "q_in", "v_in", "s_mm", "mx_done", "exp_done", "pT_mm",
                     "pT_act", "pT_dve", "o_mm", "o_out", "oT_mm", "oT_out", "wo_mm", "x_pre", "x_out", "dve_steps", "pool_steps")
            (w_in, ready, y_sum, stats, rstd, xhat, h_done, hT_mm, hT_out, q_mm, kv_mm, q_rows,
             kv_rows, roped, kx_done, kT_mm, qT_mm, k_act, k_dve, q_in, v_in, s_mm, mx_done, exp_done, pT_mm,
             pT_act, pT_dve, o_mm, o_out, oT_mm, oT_out, wo_mm, x_pre, x_out, dve_steps, pool_steps) = (psem("b_" + n) for n in names)
            y_in = [psem(f"b_y_in{j}") for j in range(TOPK)]
            rope_in = [psem(f"b_rope_in{b}") for b in range(2)]
            ba, bb = psum[6], psum[7]
            N_DMA = 7

            def schedule(eng, turn, steps=None, per=0):
                def tile(t):
                    return (t, t % 2, t // 2) if 0 <= t < NT else None

                def tiles(t):
                    return [tile(t + n) for n in (3, 2, 1, 0, -1)]
                for t in range(-3, 3):
                    turn(*tiles(t))
                turns = (NT - 6) // 2
                with eng.Fori(0, turns) as i:
                    if steps:
                        steps.loop(i, per)
                    for u in range(2):
                        turn(*[(i * 2 + (3 + u + n), (3 + u + n) % 2, i + (3 + u + n) // 2) for n in (3, 2, 1, 0, -1)])
                if steps:
                    steps.end(turns)
                for t in range(NT - 3, NT + 1):
                    turn(*tiles(t))

            def by_dve(n):
                return n % 2 == 0

            def turned(eng, t, n):
                wait_tile(eng, pT_dve if by_dve(n) else pT_act, NHEAD // 2, t, n // 2 + 1)

            def copy_keys(copy, t, b, quadrants, done):
                src = ba[:].rearrange("p (c n) -> p c n", c=NKV1)
                at = META + P * b
                for r in quadrants:
                    q = slice(HD * r, HD * r + HD)
                    if isinstance(t, int) and t == 0:
                        copy(kT[q, :, r, 0:META], src[q, :, 0:META])
                    last = copy(kT[q, :, r, at:at + P], src[q])
                last.then_inc(done, 1)

            @block.sync
            def _(sp):
                sp.dma_start(wq[:], a["L1_attn_Wq"].rearrange("(k p) n -> p k n", p=P)).then_inc(w_in, 16)
                sp.dma_start(wkv[:], a["L1_attn_Wkv"].rearrange("(k p) n -> p k n", p=P)).then_inc(w_in, 16)
                sp.dma_start(wo[:], a["L1_attn_Wo"].rearrange("(k p) n -> p k n", p=P)).then_inc(w_in, 16)
                sp.dma_start(bqk_row[:, 0:C], a["L1_attn_bq"].partition_broadcast(P)).then_inc(w_in, 16)
                sp.dma_start(bqk_row[:, C:], a["L1_attn_bkv"][0:NKV1 * HD].partition_broadcast(P)).then_inc(w_in, 16)
                sp.dma_start(bv_row, a["L1_attn_bkv"][NKV1 * HD:].partition_broadcast(P)).then_inc(w_in, 16)
                sp.dma_start(bo, a["L1_attn_bo"].partition_broadcast(P)).then_inc(w_in, 16)
                tables = a["rope"].rearrange("(t p) k d -> t p k d", p=P)

                def turn(g, s, f, m, w):
                    if s is not None:
                        t, b, half = s
                        wait_tile(sp, roped, 1, shift(t, -2))
                        one = tables[t] if isinstance(t, int) else tables[bass.ds(t, 1)].rearrange("o p k d -> (o p) k d")
                        sp.dma_start(rope[:, b], one).then_inc(rope_in[b], 16)
                schedule(sp, turn)
                for b in range(2):
                    sp.wait_ge(rope_in[b], 16 * NT // 2)

            @block.gpsimd
            def _(pool):
                st = Steps(pool, pool_steps)
                st.did(nc.gpsimd.memset(kT[:], 0.0))
                st.did(nc.gpsimd.memset(v_meta[:], 0.0))
                st.did(nc.gpsimd.memset(v[:], 0.0))
                st.settle()
                st.did(nc.gpsimd.memset(v[:, :, :, HD:V1], 1.0))
                st.settle()
                pool.sem_inc(ready, 1)
                mul = lambda out, x, y: nc.gpsimd.tensor_tensor(out, x, y, ALU.mult)

                def absorb():
                    st.settle()
                    st.did(nc.gpsimd.tensor_tensor(spare[:, 0:1], neg_half[:], neg_half[:], ALU.add))

                def turn(g, s, f, m, w):
                    if f is not None:
                        t, b, half = f
                        wait_tile(pool, stats, 1, t)
                        nc.gpsimd.tensor_tensor(r1[:, 1:2], st1[:, 7:8], neg_half[:], ALU.pow).then_inc(rstd, 1)
                        wait_tile(pool, xhat, 1, t)
                        st.did(mul(h, h, mod[:, 1, 1]))
                        st.settle()
                        nc.gpsimd.tensor_tensor(h, h, mod[:, 1, 0], ALU.add).then_inc(h_done, 1)
                    if w is not None:
                        t, b, half = w
                        pool.wait_ge(ready, 2)
                        nc.gpsimd.tensor_tensor(tile_of(x_res, t), tile_of(x_res, t), bo, ALU.add).then_inc(x_pre, 1)
                    if f is not None:
                        t, b, half = f
                        wait_tile(pool, rope_in[b], 16, half)
                        for rows, at, n, sem in ((slice(0, NHEAD), 0, NHEAD, q_rows), (slice(NHEAD, NQK), 2, NKV1, kv_rows)):
                            wait_tile(pool, sem, 1, t)
                            x = qk[:, b, rows]
                            pairs = x.rearrange("p h (i two) -> p h i two", two=2)
                            out = rot[:, rows].rearrange("p h (i two) -> p h i two", two=2)
                            tab = rope[:, b, at + 1].rearrange("p (i two) -> p i two", two=2)
                            st.settle()
                            for one in range(2):
                                st.did(mul(out[:, :, :, one], pairs[:, :, :, 1 - one],
                                           tab[:, :, one].unsqueeze(1).to_broadcast([P, n, HD // 2])))
                            st.settle()
                            st.did(mul(x, x, rope[:, b, at].unsqueeze(1).to_broadcast([P, n, HD])))
                            st.settle()
                            last = nc.gpsimd.tensor_tensor(x, x, rot[:, rows], ALU.add)
                            if at == 0:
                                st.did(last)
                        last.then_inc(roped, 1)
                        st.settle()
                    if g is not None:
                        t, b, half = g
                        wait_tile(pool, y_in[TOPK - 1], 16, shift(t, -1))
                        absorb()
                        st.did(nc.gpsimd.tensor_copy(st_pos, tile_of(pos_u, t)))
                        for j in range(TOPK):
                            wait_tile(pool, y_sum, TOPK, shift(t, -1), j + 1)
                            absorb()
                            nc.gpsimd.indirect_dma_start(out=yg[:, j], out_offset=None, in_=y_moe,
                                                         in_offset=bass.IndirectOffsetOnAxis(ap=st_pos[:, j:j + 1], axis=0)).then_inc(y_in[j], 16)
                    if f is not None:
                        t, b, half = f
                        wait_tile(pool, kv_rows, 1, t)
                        wait_tile(pool, o_mm, NHEAD, shift(t, -1))
                        if isinstance(t, int) and t == 0:
                            st.did(nc.gpsimd.tensor_copy(v_meta[0:META, :, 0:HD], vrow[0:META, b]))
                            st.did(nc.gpsimd.memset(v_meta[0:META, :, HD:V1], 1.0))
                            st.settle()
                        absorb()
                        nc.gpsimd.tensor_copy(v[:, b, :, 0:HD], vrow[:, b]).then_inc(v_in, 1)
                schedule(pool, turn, st, POOL_B)

            @block.scalar
            def _(act):
                def turn(g, s, f, m, w):
                    def copy_pT(t, n):
                        wait_tile(act, pT_mm, NHEAD, t, n + 1)
                        if n >= 4:
                            wait_tile(act, o_mm, NHEAD, t, n - 3)
                        else:
                            wait_tile(act, o_mm, NHEAD, shift(t, -1), NHEAD + n - 3)
                        nc.scalar.copy(probT[:, n % 4], psum[n % 4][:, 0:3 * P]).then_inc(pT_act, 1)

                    for n in range(NHEAD + 2):
                        if m is not None:
                            t, b, _ = m
                            if n >= 2 and not by_dve(n - 2):
                                copy_pT(t, n - 2)
                            if n < NHEAD:
                                wait_tile(act, mx_done, NHEAD, t, n + 1)
                                if n >= 4:
                                    wait_tile(act, pT_mm, NHEAD, t, n - 3)
                                else:
                                    wait_tile(act, pT_mm, NHEAD, shift(t, -1), NHEAD + n - 3)
                                nc.scalar.activation(prob[:, n % 4], psum[n % 4][:, 0:KEYS1], ACT.Exp,
                                                     bias=nmx[:, b, n:n + 1]).then_inc(exp_done, 1)
                        if f is not None:
                            t, b, _ = f
                            if n == 4:
                                wait_tile(act, hT_mm, 1, t)
                                wait_tile(act, kv_mm, 1, shift(t, -1))
                                nc.scalar.copy(hT.rearrange("p k n -> p (k n)"), bb[:]).then_inc(hT_out, 1)
                            if n == NHEAD + 1:
                                wait_tile(act, kT_mm, 1, t)
                                wait_tile(act, s_mm, NHEAD, shift(t, -1))
                                copy_keys(nc.scalar.copy, t, b, (2, 3), k_act)
                schedule(act, turn)

            @block.tensor
            def _(pe):
                def turn(g, s, f, m, w):
                    def pT(t, n):
                        wait_tile(pe, exp_done, NHEAD, t, n + 1)
                        for k in range(3):
                            at = (META, META + P, 0)[k]
                            mm = nc.tensor.transpose(psum[n % 4][:, k * P:(k + 1) * P], prob[:, n % 4, at:at + P], ident[:])
                        mm.then_inc(pT_mm, 1)

                    def pv(t, b, n):
                        turned(pe, t, n)
                        if n == 0:
                            wait_tile(pe, v_in, 1, t)
                        if n % 8 == 0:
                            wait_tile(pe, o_out, 2, shift(t, -1), n // 8 + 1)
                        out = psum[4 + n // 8][:, (n % 8) * V1:(n % 8 + 1) * V1]
                        c = n // HP
                        nc.tensor.matmul(out, probT[:, n % 4, 0:P], v[:, 0, c], start=True, stop=False)
                        nc.tensor.matmul(out, probT[:, n % 4, P:2 * P], v[:, 1, c], start=False, stop=False)
                        nc.tensor.matmul(out, probT[:, n % 4, 2 * P:], v_meta[:, c], start=False, stop=True).then_inc(o_mm, 1)

                    for n in range(NHEAD + 3):
                        if m is not None:
                            t, b, _ = m
                            if n < NHEAD:
                                if n == 0:
                                    for ks in (k_act, k_dve, q_in):
                                        wait_tile(pe, ks, 1, t)
                                if n >= 4:
                                    turned(pe, t, n - 4)
                                elif not (isinstance(t, int) and t == 0):
                                    turned(pe, shift(t, -1), NHEAD + n - 4)
                                kind = t if isinstance(t, int) and t < 2 else 2 + b
                                c, r = n // HP, n % HP
                                bank = psum[n % 4][:, 0:KEYS1]
                                nc.tensor.matmul(bank, ident_b[:], mask1[:, kind], start=True, stop=False)
                                nc.tensor.matmul(bank, qT[:, c], kT[:, c, r], start=False, stop=True).then_inc(s_mm, 1)
                            if 2 <= n < NHEAD + 2:
                                pT(t, n - 2)
                            if n >= 3:
                                pv(t, b, n - 3)
                        if w is not None:
                            t, b, _ = w
                            if n == 0:
                                wait_tile(pe, o_out, 2, t)
                                wait_tile(pe, k_act, 1, shift(t, 1) if m is not None else t)
                                wait_tile(pe, k_dve, 1, shift(t, 1) if m is not None else t)
                                for k in range(KC):
                                    mm = nc.tensor.transpose(ba[:, k * P:(k + 1) * P], o[:, b, k * P:(k + 1) * P], ident[:])
                                mm.then_inc(oT_mm, 1)
                            if n == 5:
                                wait_tile(pe, oT_out, 1, t)
                                pe.wait_ge(ready, 2)
                                for k in range(KC):
                                    mm = nc.tensor.matmul(ba[:], oT[:, k], wo[:, k], start=(k == 0), stop=(k == KC - 1))
                                mm.then_inc(wo_mm, 1)
                        if f is not None:
                            t, b, _ = f
                            if n == 3:
                                wait_tile(pe, h_done, 1, t)
                                wait_tile(pe, q_in, 1, shift(t, -1))
                                for k in range(KC):
                                    mm = nc.tensor.transpose(bb[:, k * P:(k + 1) * P], h[:, k * P:(k + 1) * P], ident[:])
                                mm.then_inc(hT_mm, 1)
                            if n == 7:
                                pe.wait_ge(w_in, 16 * N_DMA)
                                wait_tile(pe, hT_out, 1, t)
                                for k in range(KC):
                                    mm = nc.tensor.matmul(bb[:], hT[:, k], wq[:, k], start=(k == 0), stop=(k == KC - 1))
                                mm.then_inc(q_mm, 1)
                            if n == 9:
                                if w is not None:
                                    wait_tile(pe, x_out, 1, w[0])
                                elif m is not None:
                                    for ks in (k_act, k_dve):
                                        wait_tile(pe, ks, 1, m[0])
                                for k in range(KC):
                                    mm = nc.tensor.matmul(ba[:, 0:2 * NKV1 * HD], hT[:, k], wkv[:, k], start=(k == 0), stop=(k == KC - 1))
                                mm.then_inc(kv_mm, 1)
                            if n == NHEAD:
                                wait_tile(pe, roped, 1, t)
                                for k in range(KC):
                                    mm = nc.tensor.transpose(bb[:, k * P:(k + 1) * P], qk[:, b, HP * k:HP * k + HP].rearrange("p h d -> p (h d)"), ident[:])
                                mm.then_inc(qT_mm, 1)
                                wait_tile(pe, kx_done, 1, t)
                                for c in range(NKV1):
                                    mm = nc.tensor.transpose(ba[:, c * P:(c + 1) * P], kx[:, c].rearrange("p r d -> p (r d)"), ident[:])
                                mm.then_inc(kT_mm, 1)
                schedule(pe, turn)

            @block.vector
            def _(dve):
                st = Steps(dve, dve_steps)
                dve.wait_ge(w_in, 16 * N_DMA)
                st.did(nc.vector.tensor_tensor(wo[:], wo[:], mod[:, 1, 2].unsqueeze(1).to_broadcast([P, KC, C]), ALU.mult))
                st.did(nc.vector.tensor_tensor(bo, bo, mod[:, 1, 2], ALU.mult))
                st.settle()
                dve.wait_ge(ready, 1)
                dve.sem_inc(ready, 1)

                def absorb():
                    st.settle()
                    st.did(nc.vector.memset(spare[:, 1:2], 0.0))

                def turn(g, s, f, m, w):
                    def copy_pT(t, n):
                        wait_tile(dve, pT_mm, NHEAD, t, n + 1)
                        if n >= 4:
                            wait_tile(dve, o_mm, NHEAD, t, n - 3)
                        else:
                            wait_tile(dve, o_mm, NHEAD, shift(t, -1), NHEAD + n - 3)
                        nc.vector.tensor_copy(probT[:, n % 4], psum[n % 4][:, 0:3 * P]).then_inc(pT_dve, 1)

                    def o_norm(t, b, i):
                        wait_tile(dve, o_mm, NHEAD, t, 8 * i + 8)
                        if i == 0:
                            wait_tile(dve, oT_mm, 1, shift(t, -2))
                        ob = psum[4 + i][:, 0:8 * V1].rearrange("p (h d) -> p h d", h=8)
                        rs = rsum[:, b, 8 * i:8 * i + 8]
                        st.did(nc.vector.reciprocal(rs.unsqueeze(2), ob[:, :, HD:V1]))
                        st.settle()
                        nc.vector.tensor_tensor(o[:, b, 256 * i:256 * i + 256].rearrange("p (h d) -> p h d", h=8), ob[:, :, 0:HD],
                                                rs.unsqueeze(2).to_broadcast([P, 8, HD]), ALU.mult).then_inc(o_out, 1)

                    for n in range(NHEAD + 3):
                        if m is not None:
                            t, b, _ = m
                            if n < NHEAD:
                                wait_tile(dve, s_mm, NHEAD, t, n + 1)
                                if n == 0:
                                    wait_tile(dve, exp_done, NHEAD, shift(t, -2))
                                nc.vector.tensor_reduce(nmx[:, b, n:n + 1], psum[n % 4][:, 0:KEYS1], AX.X, ALU.max,
                                                        negate=True).then_inc(mx_done, 1)
                            if 2 <= n < NHEAD + 2 and by_dve(n - 2):
                                copy_pT(t, n - 2)
                            if n == 12:
                                o_norm(t, b, 0)
                        if f is not None and n == 0:
                            t, b, _ = f
                            xt = tile_of(x_res, t)
                            wait_tile(dve, y_sum, TOPK, t)
                            wait_tile(dve, xhat, 1, shift(t, -1))
                            absorb()
                            st.did(nc.vector.bn_stats(st1[:, 0:6], xt))
                            absorb()
                            st.did(nc.vector.bn_aggr(st1[:, 6:8], st1[:, 0:6]))
                            st.settle()
                            nc.vector.tensor_scalar(st1[:, 7:8], st1[:, 7:8], EPS, None, ALU.add).then_inc(stats, 1)
                        if f is not None and n == 1:
                            t, b, _ = f
                            wait_tile(dve, rstd, 1, t)
                            wait_tile(dve, stats, 1, t)
                            wait_tile(dve, hT_mm, 1, shift(t, -1))
                            nc.vector.tensor_scalar(h, tile_of(x_res, t), st1[:, 6:7], r1[:, 1:2],
                                                    ALU.subtract, ALU.mult).then_inc(xhat, 1)
                        if w is not None and n == 2:
                            t, b, _ = w
                            wait_tile(dve, oT_mm, 1, t)
                            wait_tile(dve, wo_mm, 1, shift(t, -1))
                            nc.vector.tensor_copy(oT.rearrange("p k n -> p (k n)"), ba[:]).then_inc(oT_out, 1)
                        if w is not None and n == 7:
                            t, b, _ = w
                            wait_tile(dve, wo_mm, 1, t)
                            wait_tile(dve, x_pre, 1, t)
                            nc.vector.tensor_tensor(tile_of(x_res, t), ba[:], tile_of(x_res, t), ALU.add).then_inc(x_out, 1)
                        if f is not None and n == 9:
                            t, b, _ = f
                            wait_tile(dve, q_mm, 1, t)
                            wait_tile(dve, kT_mm, 1, shift(t, -2))
                            nc.vector.tensor_tensor(qk[:, b, 0:NHEAD].rearrange("p h d -> p (h d)"), bb[:], bqk_row[:, 0:C], ALU.add).then_inc(q_rows, 1)
                        if f is not None and n == 11:
                            t, b, _ = f
                            wait_tile(dve, kv_mm, 1, t)
                            st.did(nc.vector.tensor_tensor(qk[:, b, NHEAD:].rearrange("p h d -> p (h d)"), ba[:, 0:NKV1 * HD], bqk_row[:, C:], ALU.add))
                            st.settle()
                            wait_tile(dve, v_in, 1, shift(t, -2))
                            nc.vector.tensor_tensor(vrow[:, b].rearrange("p h d -> p (h d)"), ba[:, NKV1 * HD:2 * NKV1 * HD], bv_row, ALU.add).then_inc(kv_rows, 1)
                        if s is not None and n >= 3 and n < 3 + TOPK:
                            t, b, _ = s
                            j = n - 3
                            xt = tile_of(x_res, t)
                            wait_tile(dve, y_in[j], 16, t)
                            if j:
                                wait_tile(dve, y_sum, TOPK, t, j)
                            wt = route_w[:, t, j:j + 1] if isinstance(t, int) else tile_of(route_w, t)[:, j:j + 1]
                            nc.vector.scalar_tensor_tensor(xt, yg[:, j], wt, xt, ALU.mult, ALU.add).then_inc(y_sum, 1)
                        if f is not None and n == 14:
                            t, b, _ = f
                            wait_tile(dve, roped, 1, t)
                            wait_tile(dve, kT_mm, 1, shift(t, -1))
                            nc.vector.tensor_copy(kx[:], qk[:, b, NHEAD:].unsqueeze(2).to_broadcast([P, NKV1, HP, HD])).then_inc(kx_done, 1)
                    if f is not None:
                        t, b, _ = f
                        wait_tile(dve, qT_mm, 1, t)
                        wait_tile(dve, s_mm, NHEAD, shift(t, -1))
                        nc.vector.tensor_copy(qT.rearrange("p k n -> p (k n)"), bb[:]).then_inc(q_in, 1)
                        wait_tile(dve, kT_mm, 1, t)
                        wait_tile(dve, k_act, 1, t)
                        copy_keys(nc.vector.tensor_copy, t, b, (0, 1), k_dve)
                    if m is not None:
                        o_norm(m[0], m[1], 1)
                schedule(dve, turn, st, DVE_B)
                wait_tile(dve, x_out, 1, NT - 1)

        with ExitStack() as ph, nc.Block() as block:
            psem = phase_semaphores(ph)

            NG = NT // GT
            cv = Carver(FT * C)
            up_ring = cv(RING, KC, 2, P)
            inner = cv(FT, GN)
            hT = cv(KC, GN)
            mixT = cv(KC, GN)
            xT = cv(KC, GN)
            h = cv(2, C)
            y = cv(2, C)
            gate_act = cv(2, GN)
            scales = cv(2, FT)
            st1, r1 = cv(8), cv(2)
            spare = cv(1)
            (scale_in, stats, rstd, xhat, h_done, hT_mm, hT_out, mixed, xT_mm, xT_out, up_mm, gate_done, inner_done,
             down_mm, y_out, scaled, dve_steps, pool_steps) = (psem("f_" + n) for n in
                ("scale_in", "stats", "rstd", "xhat", "h_done", "hT_mm", "hT_out", "mixed", "xT_mm", "xT_out", "up_mm", "gate_done",
                 "inner_done", "down_mm", "y_out", "scaled", "dve_steps", "pool_steps"))
            w_in = [psem(f"f_w_in{r}") for r in range(RING)]
            y_stored = [psem(f"f_y_stored{b}") for b in range(2)]

            def schedule(eng, prepare, group, steps=None, per=0):
                prepare(0)
                group(0, False)
                with eng.Fori(1, NG - 1) as g:
                    if steps:
                        steps.loop(g - 1, per)
                    group(g, False)
                if steps:
                    steps.end(NG - 2)
                group(NG - 1, True)

            def tile_at(f):
                return (f - 1) // 3 if f % 3 == 1 and 0 < f < 3 * GT else None

            @block.sync
            def _(sp):
                sp.dma_start(scales[:], a["ug_cols"]).then_inc(scale_in, 16)
                for r in range(RING):
                    sp.dma_start(up_ring[:, r], a["ffn_up"][r]).then_inc(w_in[r], 16)

                def prepare(g):
                    pass

                def group(g, last):
                    for f in range(FT):
                        if last and f >= FT - RING:
                            break
                        nxt = (f + RING) % FT
                        sp.wait_ge(up_mm, g * FT + f + 1)
                        sp.dma_start(up_ring[:, nxt % RING], a["ffn_up"][nxt]).then_inc(w_in[nxt % RING], 16)
                schedule(sp, prepare, group)
                for r in range(RING):
                    sp.wait_ge(w_in[r], 16 * NG * FT // RING)

            @block.gpsimd
            def _(pool):
                st = Steps(pool, pool_steps)

                def norm(t, b):
                    wait_tile(pool, stats, 1, t)
                    nc.gpsimd.tensor_tensor(r1[:, b:b + 1], st1[:, 7:8], neg_half[:], ALU.pow).then_inc(rstd, 1)
                    wait_tile(pool, xhat, 1, t)
                    st.did(nc.gpsimd.tensor_tensor(h[:, b], h[:, b], mod[:, 1, 4], ALU.mult))
                    st.settle()
                    nc.gpsimd.tensor_tensor(h[:, b], h[:, b], mod[:, 1, 3], ALU.add).then_inc(h_done, 1)
                norm(0, 0)
                norm(1, 1)
                with pool.Fori(0, NT // 2 - 1) as i:
                    st.loop(i, 2)
                    norm(i * 2 + 2, 0)
                    norm(i * 2 + 3, 1)
                st.end(NT // 2 - 1)

            @block.tensor
            def _(pe):
                def transposes(t, i):
                    b = i % 2
                    wait_tile(pe, h_done, 1, t)
                    wait_tile(pe, hT_out, 1, shift(t, -2))
                    for k in range(KC):
                        mm = nc.tensor.transpose(psum[6 + b][:, k * P:(k + 1) * P], h[:, b, k * P:(k + 1) * P], ident[:])
                    mm.then_inc(hT_mm, 1)

                def transform(g, k):
                    wait_tile(pe, mixed, 1, g)
                    if k >= 2:
                        wait_tile(pe, xT_out, KC, g, k - 1)
                    nc.tensor.matmul(psum[6 + k % 2][:], had[:], hT[:, k], start=True, stop=True).then_inc(xT_mm, 1)

                def prepare(g):
                    for i in range(GT):
                        transposes(i, i)
                    for k in range(KC):
                        transform(g, k)

                def group(g, last):
                    wait_tile(pe, xT_out, KC, g)
                    for f in range(FT):
                        n, b = g * FT + f, f % 2
                        pe.wait_ge(w_in[f % RING], g * (16 * FT // RING) + 16 * (f // RING + 1))
                        wait_tile(pe, inner_done, 1, shift(n, -2))
                        for half in range(2):
                            for k in range(KC):
                                mm = nc.tensor.matmul(psum[2 * half + b][:], up_ring[:, f % RING, k, half], xT[:, k],
                                                      start=(k == 0), stop=(k == KC - 1))
                        mm.then_inc(up_mm, 1)
                        if not last and tile_at(f - 2) is not None:
                            i = tile_at(f - 2)
                            transposes((g + 1) * GT + i, i)
                    for i in range(GT):
                        t = g * GT + i
                        wait_tile(pe, y_out, 1, shift(t, -2))
                        for f in range(FT):
                            if i == 0:
                                wait_tile(pe, inner_done, FT, g, f + 1)
                            mm = nc.tensor.matmul(psum[4 + i % 2][:], inner[:, f, i * P:(i + 1) * P], wd[:, f],
                                                  start=(f == 0), stop=(f == FT - 1))
                        mm.then_inc(down_mm, 1)
                        if not last and i < 2:
                            for k in (2 * i, 2 * i + 1):
                                transform(g + 1, k)
                schedule(pe, prepare, group)

            @block.scalar
            def _(act):
                out_rows = out[0].rearrange("(t p) c -> t p c", p=P)

                def copy_hT(t, i):
                    wait_tile(act, hT_mm, 1, t)
                    if i == 0:
                        wait_tile(act, xT_mm, 1, shift(t, -1))
                    nc.scalar.copy(hT[:, :, i * P:(i + 1) * P], psum[6 + i % 2][:].rearrange("p (k n) -> p k n", k=KC)).then_inc(hT_out, 1)

                def copy_xT(g, k):
                    wait_tile(act, xT_mm, KC, g, k + 1)
                    nc.scalar.copy(xT[:, k], psum[6 + k % 2][:]).then_inc(xT_out, 1)

                def prepare(g):
                    for i in range(GT):
                        copy_hT(i, i)
                    for k in range(KC):
                        copy_xT(g, k)

                def group(g, last):
                    for f in range(FT):
                        n, b = g * FT + f, f % 2
                        if isinstance(g, int) and g == 0 and f == 0:
                            act.wait_ge(scaled, 1)
                        wait_tile(act, up_mm, 1, n)
                        wait_tile(act, inner_done, 1, shift(n, -2))
                        nc.scalar.activation(gate_act[:, b], psum[b][:], ACT.Silu, scale=scales[:, 0, f:f + 1]).then_inc(gate_done, 1)
                        if not last and tile_at(f - 2) is not None:
                            i = tile_at(f - 2)
                            copy_hT((g + 1) * GT + i, i)
                    for i in range(GT):
                        if not last and 0 < i < 3:
                            for k in (2 * i - 2, 2 * i - 1):
                                copy_xT(g + 1, k)
                        t = g * GT + i
                        wait_tile(act, y_out, 1, t)
                        dst = out_rows[t] if isinstance(t, int) else out_rows[bass.ds(t, 1)].rearrange("o p c -> (o p) c")
                        act.dma_start(dst, y[:, i % 2]).then_inc(y_stored[i % 2], 16)
                schedule(act, prepare, group)
                for b in range(2):
                    act.wait_ge(y_stored[b], 16 * NT // 2)

            @block.vector
            def _(dve):
                st = Steps(dve, dve_steps)

                def absorb():
                    st.settle()
                    st.did(nc.vector.memset(spare[:], 0.0))

                def stats_of(t):
                    wait_tile(dve, xhat, 1, shift(t, -1))
                    absorb()
                    st.did(nc.vector.bn_stats(st1[:, 0:6], tile_of(x_res, t)))
                    absorb()
                    st.did(nc.vector.bn_aggr(st1[:, 6:8], st1[:, 0:6]))
                    st.settle()
                    nc.vector.tensor_scalar(st1[:, 7:8], st1[:, 7:8], EPS, None, ALU.add).then_inc(stats, 1)

                def xhat_of(t, b):
                    wait_tile(dve, rstd, 1, t)
                    wait_tile(dve, stats, 1, t)
                    wait_tile(dve, hT_mm, 1, shift(t, -2))
                    nc.vector.tensor_scalar(h[:, b], tile_of(x_res, t), st1[:, 6:7], r1[:, b:b + 1],
                                            ALU.subtract, ALU.mult).then_inc(xhat, 1)

                def mix(g):
                    wait_tile(dve, hT_out, GT, g)
                    pairs = lambda x, n: x.rearrange("p (x two n) c -> p x two n c", two=2, n=n)
                    sv, dv = pairs(hT, 1), pairs(mixT, 1)
                    for x in range(KC // 2):
                        st.did(nc.vector.tensor_tensor(dv[:, x, 0], sv[:, x, 0], sv[:, x, 1], ALU.add))
                        st.did(nc.vector.tensor_tensor(dv[:, x, 1], sv[:, x, 0], sv[:, x, 1], ALU.subtract))
                    st.settle()
                    sv, dv = pairs(mixT, 2), pairs(hT, 2)
                    st.did(nc.vector.tensor_tensor(dv[:, 0, 0], sv[:, 0, 0], sv[:, 0, 1], ALU.add))
                    st.settle()
                    nc.vector.tensor_tensor(dv[:, 0, 1], sv[:, 0, 0], sv[:, 0, 1], ALU.subtract).then_inc(mixed, 1)

                def prepare(g):
                    dve.wait_ge(scale_in, 16)
                    nc.vector.tensor_scalar(scales[:], scales[:], float(C) ** -0.5, None, ALU.mult).then_inc(scaled, 1)
                    dve.wait_ge(scaled, 1)
                    for t in range(GT):
                        stats_of(t)
                        xhat_of(t, t % 2)
                    mix(g)

                def group(g, last):
                    for f in range(FT):
                        n, b = g * FT + f, f % 2
                        i = tile_at(f)
                        if not last and i is not None:
                            stats_of((g + 1) * GT + i)
                        wait_tile(dve, gate_done, 1, n)
                        if f == 0:
                            wait_tile(dve, down_mm, GT, shift(g, -1))
                        nc.vector.scalar_tensor_tensor(inner[:, f], psum[2 + b][:], scales[:, 1, f:f + 1], gate_act[:, b],
                                                       ALU.mult, ALU.mult).then_inc(inner_done, 1)
                        if not last and i is not None:
                            xhat_of((g + 1) * GT + i, i % 2)
                    if not last:
                        mix(g + 1)
                    for i in range(GT):
                        t = g * GT + i
                        wait_tile(dve, down_mm, 1, t)
                        wait_tile(dve, y_stored[i % 2], 16, shift(g * (GT // 2) + i // 2, -1))
                        nc.vector.tensor_tensor(y[:, i % 2], psum[4 + i % 2][:], tile_of(x_res, t), ALU.add).then_inc(y_out, 1)
                schedule(dve, prepare, group, st, DVE_F)
                wait_tile(dve, y_out, 1, NT - 1)



_IN = ["L0_attn_x", "L0_attn_Wq", "L0_attn_Wk", "L0_attn_bk", "L0_attn_Wv", "L0_attn_bv", "L0_attn_Wo",
       "L0_attn_bo", "L0_ffn_similarity", "L0_wmod", "L1_attn_Wq", "L1_attn_bq", "L1_attn_Wkv", "L1_attn_bkv",
       "L1_attn_Wo", "L1_attn_bo", "L1_ffn_SU_ug", "L1_ffn_Wscale_dp",
       "L1_wmod"]


def constants():
    import numpy as np

    r = np.arange(P)
    had = np.ones((1, 1), np.float32)
    while had.shape[0] < P:
        had = np.block([[had, had], [had, -had]]).astype(np.float32)
    squares = np.stack([np.eye(P), (r[:, None] < r[None, :]), had]).astype(np.float32)
    at = HOP * (r[:, None] // W0)
    k0 = np.arange(KEYS0)[None]
    mask0 = np.where((k0 >= at) & (k0 < at + W0), 0.0, NEG).astype(np.float32)
    mask1 = np.full((4, P, KEYS1), NEG, np.float32)
    for n in range(4):
        q = n * P + r[:, None]
        even = n - n % 2
        odd = n if n % 2 else n - 1
        key = np.concatenate([np.arange(META), even * P + r, odd * P + r])[None]
        local = np.arange(KEYS1)[None] >= META
        ok = (key <= q) & np.where(local, (key >= META) & (key > q - P), True)
        mask1[n][ok] = 0.0
    freq = (1.0 / np.float32(10000.0) ** (np.arange(0, HD, 2, dtype=np.float32) / np.float32(HD))).astype(np.float32)
    ang = np.arange(S, dtype=np.float32)[:, None] * freq
    cos, sin = np.repeat(np.cos(ang), 2, -1), np.repeat(np.sin(ang), 2, -1)
    sin[:, 0::2] *= -1
    rope = np.stack([cos * SCALE1, sin * SCALE1, cos, sin], 1).astype(np.float32)
    return {"squares": squares, "mask0": mask0, "mask1": mask1, "rope": rope}


def kernel(**inputs):
    import numpy as np
    import concourse.bacc as bacc
    from concourse.bass_utils import run_bass_kernel_spmd

    arrays = {n: np.ascontiguousarray(inputs[n]) for n in _IN}
    arrays["gate_T"] = np.ascontiguousarray(np.asarray(inputs["L0_ffn_gate_weight"]).T)
    cs = np.stack([np.asarray(inputs["L0_c"])[0], np.asarray(inputs["L1_c"])[0]])
    arrays["c_cols"] = np.ascontiguousarray(cs.reshape(2, KC, P).transpose(2, 0, 1))
    arrays["bq_cols"] = np.ascontiguousarray(np.asarray(inputs["L0_attn_bq"]).reshape(KC, P).T)
    arrays["su_dp_cols"] = np.ascontiguousarray(np.asarray(inputs["L1_ffn_SU_dp"]).reshape(FT, P).T)
    ug_scale = np.asarray(inputs["L1_ffn_Wscale_ug"]).reshape(2, FT, P)
    arrays["ug_cols"] = np.ascontiguousarray(ug_scale[::-1].transpose(2, 0, 1))
    up = np.asarray(inputs["L0_ffn_gate_up_proj"]).reshape(E, 2 * FI, KC, P)
    arrays["moe_up"] = np.ascontiguousarray(up.transpose(0, 3, 2, 1))
    down = np.asarray(inputs["L0_ffn_down_proj"]).reshape(E, C, 2, FH)
    arrays["moe_down"] = np.ascontiguousarray(down.transpose(0, 3, 2, 1))
    ug = np.stack([np.asarray(inputs["L1_ffn_W_gate"]), np.asarray(inputs["L1_ffn_W_up"])]).reshape(2, FT, P, KC, P)
    arrays["ffn_up"] = np.ascontiguousarray(ug.transpose(1, 4, 3, 0, 2))
    arrays["ffn_down"] = np.ascontiguousarray(np.asarray(inputs["L1_ffn_W_down"]).reshape(C, FT, P).transpose(2, 1, 0))
    arrays.update(constants())

    nc = bacc.Bacc("TRN2", target_bir_lowering=False, num_devices=1)
    aps = {n: nc.dram_tensor("in_" + n, a.shape, mybir.dt.from_np(a.dtype), kind="ExternalInput").ap()
           for n, a in arrays.items()}
    out = nc.dram_tensor("out_0", (1, S, C), F32, kind="ExternalOutput").ap()
    adaln_two_layers(nc, aps, out)
    r = run_bass_kernel_spmd(nc, [{"in_" + n: a for n, a in arrays.items()}], core_ids=[0])
    return r.results[0]["out_0"]
```

```python
from contextlib import ExitStack

import concourse.bass as bass
from concourse import mybir

ALU = mybir.AluOpType
ACT = mybir.ActivationFunctionType
AX = mybir.AxisListType
F32 = mybir.dt.float32
BF16 = mybir.dt.bfloat16
I32 = mybir.dt.int32
U32 = mybir.dt.uint32

P = 128
S, C = 2048, 512
NT = S // P
KC = C // P
HD = 32
HP = P // HD
EPS = 1e-5
NEG = -1e30

W0 = 64
HOP = W0 // 2
KEYS0 = W0 + HOP
G0 = 2
SCALE0 = float(HD) ** -0.5

E = 64
TOPK, SELK = 8, 4
THRESH = 0.5
FI = 192
FH = FI // 2
PAIRS = S * TOPK
SLOTS = PAIRS // P + E
RING = 4

NKV1 = 4
META = 16
KEYS1 = META + 2 * P
SCALE1 = float(HD) ** -0.5
INTER = 2048
FT = INTER // P
GT = 4
GN = GT * P

DVE_A, POOL_A = 30, 4
POOL_M = 6
DVE_B, POOL_B = 14, 40
DVE_F = 21

ARENA = 24208


class Steps:

    def __init__(self, eng, sem):
        self.eng, self.sem, self.base, self.k = eng, sem, 0, 0

    def did(self, ins):
        self.k += 1
        ins.then_inc(self.sem, 1)

    def settle(self):
        self.eng.wait_ge(self.sem, self.base + self.k)

    def loop(self, i, per):
        self.first, self.per = self.k, per
        self.base, self.k = i * per + self.first, 0

    def end(self, turns):
        assert self.k == self.per, ("steps a turn", self.k)
        self.base, self.k = 0, self.first + turns * self.per


def wait_tile(eng, sem, per, tile, k=None):
    if isinstance(tile, int) and tile < 0:
        return
    eng.wait_ge(sem, tile * per + (per if k is None else k))


def shift(tile, by):
    return tile + by


def tile_of(x, t):
    if isinstance(t, int):
        return x[:, t]
    d = x[:, bass.ds(t, 1)]
    names = "abcdef"[:len(d.shape) - 2]
    return d.rearrange(f"p o {' '.join(names)} -> p (o {names[0]}) {' '.join(names[1:])}")


def windows(q):
    step = q.ap[0]
    return bass.AP(tensor=q.tensor, offset=q.offset, ap=[list(step), [HOP, 2], [1, W0]])


def adaln_two_layers(nc, a, out):
    ctx = ExitStack()
    with ctx:
        def sb(name, shape, dt=F32):
            return ctx.enter_context(nc.sbuf_tensor(name, shape, dt))

        def sem(name):
            return ctx.enter_context(nc.semaphore(name))

        def dram(name, shape, dt=F32):
            return nc.dram_tensor(name, shape, dt).ap()

        def phase_semaphores(ph):
            mine = []
            ph.callback(nc.all_engine_barrier)
            ph.callback(nc.clear_and_free_semaphores, mine)

            def psem(name):
                mine.append(nc.alloc_semaphore(name=name))
                return mine[-1]
            return psem

        h_moe = dram("h_moe", [S, C])
        y_moe = dram("y_moe", [SLOTS * P, C])
        slot_token = dram("slot_token", [SLOTS * P, 1])

        x_res = sb("x_res", [P, NT, C])
        mod = sb("mod", [P, 2, 6, C])
        ident = sb("ident", [P, P])
        ident_b = sb("ident_b", [P, P], BF16)
        ones_b = sb("ones_b", [P, P], BF16)
        upper_b = sb("upper_b", [P, P], BF16)
        mask0 = sb("mask0", [P, KEYS0], BF16)
        mask1 = sb("mask1", [P, 4, KEYS1], BF16)
        neg_half = sb("neg_half", [P, 1])
        route_hot = sb("route_hot", [P, NT, TOPK, E], BF16)
        route_w = sb("route_w", [P, NT, TOPK])
        had = sb("had", [P, P])
        iota_row = sb("iota_row", [P, E])
        iota_col = sb("iota_col", [P, 1])
        down_scale = sb("down_scale", [P, C])
        pos_u = sb("pos_u", [P, NT, TOPK], I32)
        slot_rows = sb("slot_rows", [P, SLOTS + 2], I32)
        tile_expert = sb("tile_expert", [1, SLOTS + 2], I32)
        expert_end = sb("expert_end", [1, E], I32)
        scoped = ctx.enter_context(ExitStack())
        wd = scoped.enter_context(nc.sbuf_tensor("wd", [P, FT, C], F32))
        arena = scoped.enter_context(nc.sbuf_tensor("arena", [P, ARENA], F32))
        psum = [ctx.enter_context(nc.psum_tensor(f"bank{i}", [P, 512], F32)) for i in range(8)]

        class Carver:
            def __init__(self):
                self.at = 0

            def __call__(self, *shape):
                n = 1
                for d in shape:
                    n *= d
                v = arena[:, self.at:self.at + n]
                self.at += n
                assert self.at <= ARENA, self.at
                names = "abcd"[:len(shape)]
                if len(shape) > 1:
                    v = v.rearrange(f"p ({' '.join(names)}) -> p {' '.join(names)}", **dict(zip(names, shape)))
                return v

        def mod_product(bank, act_b, w):
            for k in range(KC):
                mm = nc.tensor.matmul(bank[:], act_b[:, k], w[:, k], start=(k == 0), stop=(k == KC - 1))
            return mm

        def mod_vector(st, l, j, src, tmp, done):
            dst = mod[:, l, j, :]
            if j in (1, 4):
                nc.vector.tensor_scalar(dst, src, 1.0, None, ALU.add).then_inc(done, 1)
            elif j in (2, 5):
                t0, t1 = tmp[:, 0, :], tmp[:, 1, :]
                st.did(nc.vector.tensor_copy(dst, src))
                st.settle()
                st.did(nc.vector.tensor_scalar(t0, dst, -1.0, 0.25, ALU.mult, ALU.max))
                st.did(nc.vector.tensor_scalar(t1, dst, 0.0, 2.0, ALU.is_ge, ALU.mult))
                st.settle()
                st.did(nc.vector.tensor_tensor(t0, t0, dst, ALU.max))
                st.did(nc.vector.tensor_scalar(t1, t1, -1.0, None, ALU.add))
                st.settle()
                nc.vector.tensor_tensor(dst, t0, t1, ALU.mult).then_inc(done, 1)
            else:
                nc.vector.tensor_copy(dst, src).then_inc(done, 1)

        with ExitStack() as ph, nc.Block() as block:
            psem = phase_semaphores(ph)
            cv = Carver()
            cols = cv(KC)
            act_c = cv(KC)
            act_b = cv(KC, P)
            wm = cv(6, KC, C)
            const_f = cv(3, P)
            masks_f = cv(KEYS0 + 4 * KEYS1)
            gate_tmp = cv(2, C)
            zero_i = cv(SLOTS)
            iota_i = cv(E + 1).bitcast(I32)
            c_in, consts_in, zeros_out, c_done, c_wide, mod_mm, mod_out, dve_steps, pool_steps = (
                psem(n) for n in
                ("c_in", "consts_in", "zeros_out", "c_done", "c_wide", "mod_mm", "mod_out", "setup_dve_steps", "setup_pool_steps"))
            wm_in = [psem(f"wm_in{j}") for j in range(6)]

            @block.sync
            def _(sp):
                sp.dma_start(cols, a["c_cols"][:, 0]).then_inc(c_in, 16)
                w = a["L0_wmod"].rearrange("(k p) (j n) -> j p k n", p=P, j=6)
                for j in range(6):
                    sp.dma_start(wm[:, j], w[j]).then_inc(wm_in[j], 16)

            @block.scalar
            def _(act):
                act.dma_start(const_f[:], a["squares"].rearrange("k p n -> p k n")).then_inc(consts_in, 16)
                act.dma_start(masks_f[:, 0:KEYS0], a["mask0"]).then_inc(consts_in, 16)
                act.dma_start(masks_f[:, KEYS0:], a["mask1"].rearrange("k p n -> p k n")).then_inc(consts_in, 16)
                act.wait_ge(c_in, 16)
                nc.scalar.activation(act_c, cols, ACT.Silu).then_inc(c_done, 1)

            @block.gpsimd
            def _(pool):
                st = Steps(pool, pool_steps)
                st.did(nc.gpsimd.memset(ones_b[:], 1.0))
                st.did(nc.gpsimd.memset(neg_half[:], -0.5))
                st.did(nc.gpsimd.iota(iota_i[:, 0:E], [[1, E]], base=0, channel_multiplier=0))
                st.did(nc.gpsimd.iota(iota_i[:, E:], [[1, 1]], base=0, channel_multiplier=1))
                st.did(nc.gpsimd.memset(zero_i, 0.0))
                st.did(nc.gpsimd.memset(slot_rows[:, SLOTS:], 0))
                st.did(nc.gpsimd.memset(tile_expert[:, SLOTS:], E - 1))
                st.settle()
                st.did(nc.gpsimd.tensor_copy(iota_row[:], iota_i[:, 0:E]))
                st.did(nc.gpsimd.tensor_copy(iota_col[:], iota_i[:, E:]))
                pool.dma_start(slot_token.rearrange("(p n) o -> p (n o)", p=P), zero_i).then_inc(zeros_out, 16)
                pool.wait_ge(zeros_out, 16)

            @block.tensor
            def _(pe):
                pe.wait_ge(c_wide, 1)
                for j in range(6):
                    pe.wait_ge(wm_in[j], 16)
                    if j >= 4:
                        pe.wait_ge(mod_out, j - 3)
                    mod_product(psum[j % 4], act_b, wm[:, j]).then_inc(mod_mm, 1)

            @block.vector
            def _(dve):
                st = Steps(dve, dve_steps)
                dve.wait_ge(c_done, 1)
                nc.vector.tensor_copy(act_b[:], act_c.unsqueeze(2).to_broadcast([P, KC, P])).then_inc(c_wide, 1)
                dve.wait_ge(consts_in, 16 * 3)
                st.did(nc.vector.tensor_copy(ident[:], const_f[:, 0]))
                st.did(nc.vector.tensor_copy(ident_b[:], const_f[:, 0]))
                st.did(nc.vector.tensor_copy(had[:], const_f[:, 2]))
                st.did(nc.vector.tensor_copy(upper_b[:], const_f[:, 1]))
                st.did(nc.vector.tensor_copy(mask0[:], masks_f[:, 0:KEYS0]))
                st.did(nc.vector.tensor_copy(mask1[:],
                                             masks_f[:, KEYS0:].rearrange("p (k n) -> p k n", k=4)))
                for j in range(6):
                    dve.wait_ge(mod_mm, j + 1)
                    mod_vector(st, 0, j, psum[j % 4][:], gate_tmp, mod_out)

        with ExitStack() as ph, nc.Block() as block:
            psem = phase_semaphores(ph)

            cv = Carver()
            xa = wd[0:KEYS0]
            assert NT == FT
            wq, wk, wv = cv(KC, C), cv(KC, P), cv(KC, G0 * HD)
            wo, wgate = cv(KC, C), cv(KC, E)
            bq, bk, bv, bo = cv(KC), cv(1), cv(G0 * HD)[0:KEYS0], cv(C)
            h = cv(2, C)[0:KEYS0]
            hT = cv(2, KC, KEYS0)
            qT = cv(2, KC, P)
            kT = cv(2, HP, KEYS0)
            v = cv(2, G0, HD + 1)[0:KEYS0]
            prob = cv(4 * KC, KEYS0)
            probT = cv(4 * KC, P)[0:KEYS0]
            o = cv(2, C)
            oT = cv(KC, P)
            h2 = cv(2, C)
            h2T = cv(KC, P)
            st1, st2 = cv(8), cv(8)
            r1, r2 = cv(2), cv(2)
            mx = cv(4 * KC)
            rsum = cv(4 * KC)
            lg = cv(NT, E)
            l16 = cv(5, NT)
            spare = cv(1)
            top = cv(NT, TOPK)
            idx_u = cv(NT, TOPK).bitcast(U32)
            idx_f = cv(NT, TOPK)

            (xa_in, w_in, ready, stats1, rstd1, xhat1, h_done, hT_mm, hT_out, q_mm, q_out, kv_mm, kv_out,
             s_mm, p_sub, p_exp, pT_mm, pT_act, pT_dve, o_mm, o_out, oT_mm, oT_out, wo_mm, x_pre, x_out,
             rstd2, xhat2, h2_done, h2T_mm, h2T_out, lg_mm, lg_shift, lg_exp, lg_out, dve_steps, pool_steps) = (
                psem("a_" + n) for n in
                ("xa_in", "w_in", "ready", "stats1", "rstd1", "xhat1", "h_done", "hT_mm", "hT_out", "q_mm", "q_out",
                 "kv_mm", "kv_out", "s_mm", "p_sub", "p_exp", "pT_mm", "pT_act", "pT_dve", "o_mm", "o_out", "oT_mm",
                 "oT_out", "wo_mm", "x_pre", "x_out", "rstd2", "xhat2", "h2_done", "h2T_mm", "h2T_out", "lg_mm",
                 "lg_shift", "lg_exp", "lg_out", "dve_steps", "pool_steps"))
            h2_stored = [psem(f"a_h2_stored{b}") for b in range(2)]
            filled = psem("a_filled")
            x_in = psem("a_x_in")
            FILL = 4
            sq, kvb, tp = psum[5], psum[6], psum[7]
            N_DMA = 11

            def schedule(eng, turn, steps=None, per=0):
                def tile(t):
                    return (t, t % 2, t // 2) if 0 <= t < NT else None
                stages = (2, 1, 0, -1, -2)
                for m in range(-2, 4):
                    turn(*[tile(m + n) for n in stages])
                turns = (NT - 6) // 2
                with eng.Fori(0, turns) as i:
                    if steps:
                        steps.loop(i, per)
                    for m in (4, 5):
                        turn(*[(i * 2 + (m + n), (m + n) % 2, i + (m + n) // 2) for n in stages])
                if steps:
                    steps.end(turns)
                for m in range(NT - 2, NT + 2):
                    turn(*[tile(m + n) for n in stages])

            @block.sync
            def _(sp):
                xw = bass.AP(tensor=a["L0_attn_x"].tensor, offset=0, ap=[[C, KEYS0], [W0 * C, NT], [1, C]])
                sp.dma_start(xa[:], xw).then_inc(xa_in, 16)
                sp.dma_start(wq[:], a["L0_attn_Wq"].rearrange("(k p) n -> p k n", p=P)).then_inc(w_in, 16)
                wk_v = a["L0_attn_Wk"].rearrange("(k p) n -> p k n", p=P)
                sp.dma_start(wk[:, :, 0:W0], wk_v).then_inc(w_in, 16)
                sp.dma_start(wk[:, :, W0:P], wk_v).then_inc(w_in, 16)
                sp.dma_start(wv[:], a["L0_attn_Wv"].rearrange("(k p) n -> p k n", p=P)).then_inc(w_in, 16)
                sp.dma_start(wo[:], a["L0_attn_Wo"].rearrange("(k p) n -> p k n", p=P)).then_inc(w_in, 16)
                sp.dma_start(wgate[:], a["gate_T"].rearrange("(k p) n -> p k n", p=P)).then_inc(w_in, 16)
                sp.dma_start(bq, a["bq_cols"]).then_inc(w_in, 16)
                for r in range(2):
                    sp.dma_start(bk[W0 * r:W0 * r + W0], a["L0_attn_bk"].rearrange("(p o) -> p o", o=1)).then_inc(w_in, 16)
                sp.dma_start(bv, a["L0_attn_bv"].partition_broadcast(KEYS0)).then_inc(w_in, 16)
                sp.dma_start(bo, a["L0_attn_bo"].partition_broadcast(P)).then_inc(w_in, 16)

                sp.dma_start(x_res[:], a["L0_attn_x"][0].rearrange("(t p) c -> p t c", p=P)).then_inc(x_in, 16)
                some = mod[:, 0, 0:FILL]
                for g in range(E, SLOTS, FILL):
                    sp.dma_start(y_moe[g * P:(g + FILL) * P].rearrange("(g p) c -> p g c", p=P), some).then_inc(filled, 16)

                def turn(g, f, m, w, z):
                    if z is not None:
                        t, b, half = z
                        wait_tile(sp, h2_done, 1, t)
                        rows = h_moe.rearrange("(t p) c -> p t c", p=P)
                        sp.dma_start(rows[:, t] if isinstance(t, int) else rows[:, bass.ds(t, 1)].rearrange("p o c -> p (o c)"),
                                     h2[:, b]).then_inc(h2_stored[b], 16)
                schedule(sp, turn)
                for b in range(2):
                    sp.wait_ge(h2_stored[b], 16 * NT // 2)
                sp.wait_ge(filled, 16 * (SLOTS - E) // FILL)

            @block.gpsimd
            def _(pool):
                st = Steps(pool, pool_steps)
                st.did(nc.gpsimd.memset(kT[:], 0.0))
                st.did(nc.gpsimd.memset(v[:], 1.0))
                st.settle()
                pool.sem_inc(ready, 1)

                def turn(g, f, m, w, z):
                    if z is not None:
                        t, b, _ = z
                        wait_tile(pool, xhat2, 1, t)
                        st.did(nc.gpsimd.tensor_tensor(h2[:, b], h2[:, b], mod[:, 0, 4], ALU.mult))
                        st.settle()
                        nc.gpsimd.tensor_tensor(h2[:, b], h2[:, b], mod[:, 0, 3], ALU.add).then_inc(h2_done, 1)
                    if w is not None:
                        pool.wait_ge(ready, 2)
                        pool.wait_ge(x_in, 16)
                        xt = tile_of(x_res, w[0])
                        nc.gpsimd.tensor_tensor(xt, xt, bo, ALU.add).then_inc(x_pre, 1)
                    if g is not None:
                        t, b, _ = g
                        wait_tile(pool, stats1, 1, t)
                        nc.gpsimd.tensor_tensor(r1[0:KEYS0, 1:2], st1[0:KEYS0, 7:8], neg_half[0:KEYS0], ALU.pow).then_inc(rstd1, 1)
                        wait_tile(pool, xhat1, 1, t)
                        st.did(nc.gpsimd.tensor_tensor(h[:, b], h[:, b], mod[0:KEYS0, 0, 1], ALU.mult))
                        st.settle()
                        nc.gpsimd.tensor_tensor(h[:, b], h[:, b], mod[0:KEYS0, 0, 0], ALU.add).then_inc(h_done, 1)
                    if w is not None:
                        wait_tile(pool, x_out, 1, w[0])
                        nc.gpsimd.tensor_tensor(r2[:, 1:2], st2[:, 7:8], neg_half[:], ALU.pow).then_inc(rstd2, 1)
                schedule(pool, turn, st, POOL_A)

            def copy_probs(copy, t, c):
                return copy(probT[:, HP * c:HP * c + HP], psum[c][0:KEYS0].rearrange("p (h n) -> p h n", h=HP))

            @block.scalar
            def _(act):
                def turn(g, f, m, w, z):
                    if f is not None:
                        t, b, _ = f
                        wait_tile(act, hT_mm, 1, t)
                        wait_tile(act, kv_mm, 1, shift(t, -2))
                        nc.scalar.copy(hT[:, b], psum[4][:, 0:KC * KEYS0].rearrange("p (k n) -> p k n", k=KC)).then_inc(hT_out, 1)
                    if m is not None:
                        for c in range(KC):
                            wait_tile(act, p_sub, KC, m[0], c + 1)
                            some = prob[:, HP * c:HP * c + HP]
                            nc.scalar.activation(some, some, ACT.Exp, scale=SCALE0).then_inc(p_exp, 1)
                    if f is not None:
                        t, b, _ = f
                        wait_tile(act, q_mm, 1, t)
                        wait_tile(act, s_mm, KC, shift(t, -2))
                        for c in range(KC):
                            last = nc.scalar.activation(qT[:, b, c], sq[:, c * P:(c + 1) * P], ACT.Identity,
                                                        bias=bq[:, c:c + 1])
                        last.then_inc(q_out, 1)
                    if z is not None:
                        t, b, _ = z
                        wait_tile(act, h2T_mm, 1, t)
                        wait_tile(act, lg_mm, 1, shift(t, -1))
                        nc.scalar.copy(h2T.rearrange("p k n -> p (k n)"), tp[:]).then_inc(h2T_out, 1)
                    if m is not None:
                        t, b, _ = m
                        wait_tile(act, o_mm, 1, shift(t, -1))
                        for c in range(2):
                            wait_tile(act, pT_mm, KC, t, c + 1)
                            copy_probs(nc.scalar.copy, t, c).then_inc(pT_act, 1)
                    if w is not None:
                        t, b, _ = w
                        wait_tile(act, oT_mm, 1, t)
                        wait_tile(act, wo_mm, 1, shift(t, -1))
                        nc.scalar.copy(oT.rearrange("p k n -> p (k n)"), tp[:]).then_inc(oT_out, 1)
                schedule(act, turn)
                act.wait_ge(lg_shift, 1)
                nc.scalar.activation(lg[:], lg[:], ACT.Exp).then_inc(lg_exp, 1)

            @block.tensor
            def _(pe):
                def turn(g, f, m, w, z):
                    if m is not None:
                        t, b, _ = m
                        wait_tile(pe, q_out, 1, t)
                        wait_tile(pe, kv_out, 1, t)
                        wait_tile(pe, pT_act, 2, shift(t, -1))
                        wait_tile(pe, pT_dve, 2, shift(t, -1))
                        for c in range(KC):
                            bank = psum[c][:, 0:HP * KEYS0]
                            nc.tensor.matmul(bank, ident_b[:], mask0[:].unsqueeze(1).to_broadcast([P, HP, KEYS0]),
                                             start=True, stop=False)
                            nc.tensor.matmul(bank, qT[:, b, c], kT[:, b], start=False, stop=True).then_inc(s_mm, 1)
                    if f is not None:
                        t, b, _ = f
                        wait_tile(pe, h_done, 1, t)
                        wait_tile(pe, o_out, 1, shift(t, -2))
                        for k in range(KC):
                            mm = nc.tensor.transpose(psum[4][:, k * KEYS0:(k + 1) * KEYS0], h[:, b, k * P:(k + 1) * P],
                                                     ident[0:KEYS0, 0:KEYS0])
                        mm.then_inc(hT_mm, 1)
                        wait_tile(pe, hT_out, 1, t)
                        pe.wait_ge(w_in, 16 * N_DMA)
                        for c in range(KC):
                            for k in range(KC):
                                mm = nc.tensor.matmul(sq[:, c * P:(c + 1) * P], wq[:, k, c * P:(c + 1) * P], windows(hT[:, b, k]),
                                                      start=(k == 0), stop=(k == KC - 1))
                        mm.then_inc(q_mm, 1)
                    if z is not None:
                        t, b, _ = z
                        wait_tile(pe, h2_done, 1, t)
                        for k in range(KC):
                            mm = nc.tensor.transpose(tp[:, k * P:(k + 1) * P], h2[:, b, k * P:(k + 1) * P], ident[:])
                        mm.then_inc(h2T_mm, 1)
                    if m is not None:
                        t, b, _ = m
                        for c in range(KC):
                            wait_tile(pe, p_exp, KC, t, c + 1)
                            for j in range(HP):
                                mm = nc.tensor.transpose(psum[c][0:KEYS0, j * P:(j + 1) * P], prob[:, HP * c + j], ident[:])
                            mm.then_inc(pT_mm, 1)
                    if w is not None:
                        t, b, _ = w
                        wait_tile(pe, o_out, 1, t)
                        if z is not None:
                            wait_tile(pe, h2T_out, 1, z[0])
                        for k in range(KC):
                            mm = nc.tensor.transpose(tp[:, k * P:(k + 1) * P], o[:, b, k * P:(k + 1) * P], ident[:])
                        mm.then_inc(oT_mm, 1)
                    if f is not None:
                        wait_tile(pe, kv_out, 1, shift(f[0], -1))
                    if z is not None:
                        t, b, _ = z
                        wait_tile(pe, lg_out, 1, shift(t, -1))
                        wait_tile(pe, h2T_out, 1, t)
                        for k in range(KC):
                            mm = nc.tensor.matmul(kvb[:, 2 * P:2 * P + E], h2T[:, k], wgate[:, k], start=(k == 0), stop=(k == KC - 1))
                        mm.then_inc(lg_mm, 1)
                    if f is not None:
                        t, b, _ = f
                        for k in range(KC):
                            nc.tensor.matmul(kvb[:, 0:KEYS0], wk[:, k], hT[:, b, k], start=(k == 0), stop=(k == KC - 1))
                        for k in range(KC):
                            mm = nc.tensor.matmul(kvb[0:KEYS0, P:P + G0 * HD], hT[:, b, k], wv[:, k],
                                                  start=(k == 0), stop=(k == KC - 1))
                        mm.then_inc(kv_mm, 1)
                    if w is not None:
                        t, b, _ = w
                        wait_tile(pe, oT_out, 1, t)
                        pe.wait_ge(ready, 2)
                        for k in range(KC):
                            mm = nc.tensor.matmul(tp[:], oT[:, k], wo[:, k], start=(k == 0), stop=(k == KC - 1))
                        mm.then_inc(wo_mm, 1)
                    if m is not None:
                        t, b, _ = m
                        if f is not None:
                            wait_tile(pe, q_out, 1, f[0])
                            wait_tile(pe, hT_out, 1, f[0])
                        for n in range(4 * KC):
                            if n % (2 * HP) == 0:
                                wait_tile(pe, pT_act if n == 0 else pT_dve, 2, t)
                            mm = nc.tensor.matmul(o_at(n), probT[:, n], v[:, b, n % G0], start=True, stop=True)
                        mm.then_inc(o_mm, 1)

                def o_at(n):
                    q = HD + 1
                    return psum[4 + n // 8][:, (n % 8) * q:(n % 8 + 1) * q]
                pe.wait_ge(ready, 1)
                schedule(pe, turn)

            @block.vector
            def _(dve):
                st = Steps(dve, dve_steps)

                def absorb():
                    st.settle()
                    st.did(nc.vector.memset(spare[0:1], 0.0))
                dve.wait_ge(w_in, 16 * N_DMA)
                st.did(nc.vector.tensor_tensor(wo[:], wo[:], mod[:, 0, 2].unsqueeze(1).to_broadcast([P, KC, C]), ALU.mult))
                st.did(nc.vector.tensor_tensor(bo, bo, mod[:, 0, 2], ALU.mult))
                dve.wait_ge(ready, 1)
                st.settle()
                dve.sem_inc(ready, 1)
                dve.wait_ge(xa_in, 16)

                def norm_stats(x, st8, rows, done):
                    absorb()
                    st.did(nc.vector.bn_stats(st8[rows, 0:6], x))
                    absorb()
                    st.did(nc.vector.bn_aggr(st8[rows, 6:8], st8[rows, 0:6]))
                    st.settle()
                    nc.vector.tensor_scalar(st8[rows, 7:8], st8[rows, 7:8], EPS, None, ALU.add).then_inc(done, 1)

                def turn(g, f, m, w, z):
                    if w is not None:
                        t, b, _ = w
                        wait_tile(dve, o_mm, 1, t)
                        wait_tile(dve, oT_mm, 1, shift(t, -2))
                        for i in range(2):
                            ob = psum[4 + i][:, 0:8 * (HD + 1)].rearrange("p (h d) -> p h d", h=8)
                            st.did(nc.vector.reciprocal(rsum[:, 8 * i:8 * i + 8].unsqueeze(2), ob[:, :, HD:HD + 1]))
                        st.settle()
                        for i in range(2):
                            ob = psum[4 + i][:, 0:8 * (HD + 1)].rearrange("p (h d) -> p h d", h=8)
                            last = nc.vector.tensor_tensor(o[:, b, 256 * i:256 * i + 256].rearrange("p (h d) -> p h d", h=8), ob[:, :, 0:HD],
                                                           rsum[:, 8 * i:8 * i + 8].unsqueeze(2).to_broadcast([P, 8, HD]), ALU.mult)
                        last.then_inc(o_out, 1)
                    if z is not None:
                        t, b, half = z
                        wait_tile(dve, rstd2, 1, t)
                        wait_tile(dve, x_out, 1, t)
                        wait_tile(dve, h2T_mm, 1, shift(t, -2))
                        wait_tile(dve, h2_stored[b], 16, shift(half, -1))
                        nc.vector.tensor_scalar(h2[:, b], tile_of(x_res, t), st2[:, 6:7], r2[:, 1:2], ALU.subtract, ALU.mult).then_inc(xhat2, 1)
                    if m is not None:
                        t, b, _ = m
                        wait_tile(dve, pT_mm, KC, shift(t, -1))
                        scores = lambda c: psum[c][:, 0:HP * KEYS0].rearrange("p (h n) -> p h n", h=HP)
                        for c in range(KC + 1):
                            if c < KC:
                                wait_tile(dve, s_mm, KC, t, c + 1)
                                st.did(nc.vector.tensor_reduce(mx[:, HP * c:HP * c + HP], scores(c), AX.X, ALU.max))
                            if c:
                                if c == KC:
                                    st.settle()
                                else:
                                    dve.wait_ge(dve_steps, st.base + (st.k - 1))
                                i = slice(HP * c - HP, HP * c)
                                nc.vector.tensor_tensor(prob[:, i], scores(c - 1), mx[:, i].unsqueeze(2).to_broadcast([P, HP, KEYS0]),
                                                        ALU.subtract).then_inc(p_sub, 1)
                    if g is not None:
                        wait_tile(dve, xhat1, 1, shift(g[0], -1))
                        norm_stats(tile_of(xa, g[0]), st1, slice(0, KEYS0), stats1)
                    if m is not None:
                        t, b, _ = m
                        wait_tile(dve, o_mm, 1, shift(t, -1))
                        for c in range(2, KC):
                            wait_tile(dve, pT_mm, KC, t, c + 1)
                            copy_probs(nc.vector.tensor_copy, t, c).then_inc(pT_dve, 1)
                    if g is not None:
                        t, b, _ = g
                        wait_tile(dve, rstd1, 1, t)
                        wait_tile(dve, stats1, 1, t)
                        wait_tile(dve, hT_mm, 1, shift(t, -2))
                        nc.vector.tensor_scalar(h[:, b], tile_of(xa, t), st1[0:KEYS0, 6:7], r1[0:KEYS0, 1:2],
                                                ALU.subtract, ALU.mult).then_inc(xhat1, 1)
                    if z is not None:
                        t, b, _ = z
                        wait_tile(dve, lg_mm, 1, t)
                    if f is not None:
                        t, b, _ = f
                        wait_tile(dve, kv_mm, 1, t)
                        wait_tile(dve, s_mm, KC, shift(t, -2))
                        wait_tile(dve, o_mm, 1, shift(t, -2))
                        for r in range(HP):
                            q = slice(HD * r, HD * r + HD)
                            nc.vector.tensor_scalar(kT[q, b, r], kvb[q, 0:KEYS0], bk[q], None, ALU.add)
                        nc.vector.tensor_tensor(v[:, b, :, 0:HD], kvb[0:KEYS0, P:P + G0 * HD].rearrange("p (g d) -> p g d", g=G0),
                                                bv.rearrange("p (g d) -> p g d", g=G0), ALU.add).then_inc(kv_out, 1)
                    if z is not None:
                        nc.vector.tensor_copy(tile_of(lg, z[0]), kvb[:, 2 * P:2 * P + E]).then_inc(lg_out, 1)
                    if w is not None:
                        t, b, _ = w
                        xt = tile_of(x_res, t)
                        wait_tile(dve, wo_mm, 1, t)
                        wait_tile(dve, x_pre, 1, t)
                        wait_tile(dve, xhat2, 1, shift(t, -1))
                        st.did(nc.vector.tensor_tensor(xt, tp[:], xt, ALU.add))
                        norm_stats(xt, st2, slice(0, P), x_out)
                schedule(dve, turn, st, DVE_A)

                def step(ins):
                    st.did(ins)
                    st.settle()
                over = lambda x, n: x.unsqueeze(2).to_broadcast([P, NT, n])
                dve.wait_ge(lg_out, NT)
                step(nc.vector.tensor_reduce(l16[:, 0], lg[:], AX.X, ALU.max))
                nc.vector.tensor_tensor(lg[:], lg[:], over(l16[:, 0], E), ALU.subtract).then_inc(lg_shift, 1)
                dve.wait_ge(lg_exp, 1)
                step(nc.vector.tensor_reduce(l16[:, 1], lg[:], AX.X, ALU.add))
                step(nc.vector.reciprocal(l16[:, 2], l16[:, 1]))
                st.did(nc.vector.tensor_tensor(lg[:], lg[:], over(l16[:, 2], E), ALU.mult))
                absorb()
                absorb()
                for t in range(NT):
                    st.did(nc.vector.max(top[:, t], lg[:, t]))
                absorb()
                absorb()
                for t in range(NT):
                    st.did(nc.vector.max_index(idx_u[:, t], top[:, t], lg[:, t]))
                step(nc.vector.tensor_reduce(l16[:, 3], top[:], AX.X, ALU.add))
                step(nc.vector.tensor_scalar(l16[:, 3], l16[:, 3], 1e-12, None, ALU.max))
                step(nc.vector.reciprocal(l16[:, 4], l16[:, 3]))
                st.did(nc.vector.tensor_tensor(route_w[:], top[:], over(l16[:, 4], TOPK), ALU.mult))
                step(nc.vector.tensor_copy(idx_f[:], idx_u[:]))
                for t in range(NT):
                    st.did(nc.vector.tensor_tensor(route_hot[:, t], idx_f[:, t].unsqueeze(2).to_broadcast([P, TOPK, E]),
                                                   iota_row[:].unsqueeze(1).to_broadcast([P, TOPK, E]), ALU.is_equal))
                st.settle()

        with ExitStack() as ph, nc.Block() as block:
            psem = phase_semaphores(ph)

            cv = Carver()
            back = cv(FT, C)
            sim = cv(E)[0:E]
            cand = cv(E)[0:E]
            best, best_f = cv(8)[0:E], cv(8)[0:E]
            best_u = cv(8)[0:E].bitcast(U32)
            cnt_j = cv(2 * E)
            dtmp = cv(2, E)[0:E]
            sec = cv(8)[0:E]
            diag = cv(E // 2).bitcast(BF16)[0:E]
            map_row = cv(E)
            chosen = cv(NT * E // 2).bitcast(BF16).rearrange("p (t e) -> p t e", t=NT)
            moved = cv(NT, SELK)
            counts, upto = cv(E, NT), cv(E, NT)
            again = cv(E, NT)
            tiles_f, tile_end = cv(E), cv(E)
            base, ones_row = cv(E), cv(E)
            tiles_i = cv(E).bitcast(I32)
            pos = cv(NT, E)
            gcol = cv(4)
            picked = cv(2, TOPK, E)
            pos_f = cv(NT, TOPK)
            tok_i = cv(NT).bitcast(I32)
            tok_f = cv(NT)
            st_pos = cv(2, TOPK).bitcast(I32)
            st_tok = cv(2, 1)
            su_dp = cv(FT)
            dtmp0 = cv(2 * E)
            spare = cv(1)
            slots_in_row = cv(2 * P)[0:SLOTS // 2]
            WMB = 3
            cols, act_c = cv(KC), cv(KC)
            act_b = cv(KC, P)
            wm = cv(WMB, KC, C)
            gate_tmp = cv(2, C)
            su_row, down_row = cv(C), cv(C)
            c_in, c_done, c_wide, mod_mm, mod_out, rows_in = (
                psem("r_" + n) for n in ("c_in", "c_done", "c_wide", "mod_mm", "mod_out", "rows_in"))
            wm_in = [psem(f"r_wm_in{j}") for j in range(WMB)]
            (r_in, wd_in, n_mm, d_rows, map_mm, sel_done, rank_mm, eid_done, eid_mm, had_mm, had_out,
             tok_done, slots_in, slot_mm, dve_steps, pool_steps) = (
                psem("r_" + n) for n in
                ("r_in", "wd_in", "n_mm", "d_rows", "map_mm", "sel_done", "rank_mm", "eid_done", "eid_mm", "had_mm",
                 "had_out", "tok_done", "slots_in", "slot_mm", "dve_steps", "pool_steps"))
            scattered = [psem(f"r_scattered{b}") for b in range(2)]
            pos_done = psem("r_pos_done")

            @block.sync
            def _(sp):
                sp.dma_start(sim, a["L0_ffn_similarity"]).then_inc(r_in, 16)
                sp.dma_start(su_dp, a["su_dp_cols"]).then_inc(r_in, 16)
                sp.dma_start(cols, a["c_cols"][:, 1]).then_inc(c_in, 16)
                sp.dma_start(wd[:], a["ffn_down"]).then_inc(wd_in, 16)
                sp.dma_start(su_row, a["L1_ffn_SU_ug"].partition_broadcast(P)).then_inc(rows_in, 16)
                sp.dma_start(down_row, a["L1_ffn_Wscale_dp"].partition_broadcast(P)).then_inc(rows_in, 16)
                w = a["L1_wmod"].rearrange("(k p) (j n) -> j p k n", p=P, j=6)
                for j in range(6):
                    if j >= WMB:
                        sp.wait_ge(mod_mm, j - WMB + 1)
                    sp.dma_start(wm[:, j % WMB], w[j]).then_inc(wm_in[j % WMB], 16)
                for b in range(2):
                    sp.wait_ge(scattered[b], 16 * TOPK * NT // 2)
                sp.dma_start(slots_in_row, slot_token.rearrange("(q n) o -> q (n o)", n=2 * P)).then_inc(slots_in, 16)
                sp.wait_ge(slots_in, 16)

            @block.gpsimd
            def _(pool):
                st = Steps(pool, pool_steps)
                st.did(nc.gpsimd.iota(tok_i[:], [[P, NT]], base=0, channel_multiplier=1))
                st.settle()
                nc.gpsimd.tensor_copy(tok_f, tok_i[:]).then_inc(tok_done, 1)
                pool.wait_ge(tok_done, 1)

                def scatter(t, b, half):
                    if not isinstance(t, int) or t >= 2:
                        wait_tile(pool, scattered[b], 16 * TOPK, shift(half, -1))
                    wait_tile(pool, pos_done, 1, t)
                    st.did(nc.gpsimd.tensor_copy(st_pos[:, b], tile_of(pos_u, t)))
                    st.did(nc.gpsimd.tensor_copy(st_tok[:, b], tok_f[:, t:t + 1] if isinstance(t, int) else tok_f[:, bass.ds(t, 1)]))
                    st.settle()
                    st.did(nc.gpsimd.tensor_tensor(spare, neg_half[:], neg_half[:], ALU.add))
                    for j in range(TOPK):
                        nc.gpsimd.indirect_dma_start(out=slot_token, out_offset=bass.IndirectOffsetOnAxis(ap=st_pos[:, b, j:j + 1], axis=0),
                                                     in_=st_tok[:, b], in_offset=None).then_inc(scattered[b], 16)
                scatter(0, 0, 0)
                scatter(1, 1, 0)
                with pool.Fori(0, NT // 2 - 1) as i:
                    st.loop(i, 6)
                    scatter(i * 2 + 2, 0, i + 1)
                    scatter(i * 2 + 3, 1, i + 1)
                st.end(NT // 2 - 1)

            @block.scalar
            def _(act):
                act.wait_ge(c_in, 16)
                nc.scalar.activation(act_c, cols, ACT.Silu).then_inc(c_done, 1)

            @block.tensor
            def _(pe):
                hot = route_hot[:].rearrange("p t j e -> p t (j e)")
                for t in range(NT):
                    mm = nc.tensor.matmul(psum[0][:], ones_b[:], hot[:, t], start=(t == 0), stop=(t == NT - 1))
                mm.then_inc(n_mm, 1)
                pe.wait_ge(d_rows, 1)
                nc.tensor.matmul(psum[1][:, 0:E], ones_b[0:E], diag, start=True, stop=True).then_inc(map_mm, 1)
                pe.wait_ge(sel_done, 1)
                ch = chosen.rearrange("p (h t) e -> p h (t e)", h=2)
                for n in range(2):
                    nc.tensor.matmul(psum[2 + n][:], upper_b[:], ch[:, n], start=True, stop=True)
                    mm = nc.tensor.matmul(psum[4 + n][:], ones_b[:], ch[:, n], start=True, stop=True)
                mm.then_inc(rank_mm, 1)
                pe.wait_ge(eid_done, 1)
                for n in range(2):
                    mm = nc.tensor.transpose(psum[6][0:1, n * P:(n + 1) * P], gcol[:, n:n + 1], ident[:])
                mm.then_inc(eid_mm, 1)
                pe.wait_ge(wd_in, 16)
                for f in range(FT):
                    if f >= 2:
                        pe.wait_ge(had_out, f - 1)
                    nc.tensor.matmul(psum[f % 2][:], had[:], wd[:, f], start=True, stop=True).then_inc(had_mm, 1)
                pe.wait_ge(c_wide, 1)
                pe.wait_ge(pos_done, NT)
                for j in range(6):
                    pe.wait_ge(wm_in[j % WMB], 16 * (j // WMB + 1))
                    if j >= 4:
                        pe.wait_ge(mod_out, j - 3)
                    mod_product(psum[2 + j % 4], act_b, wm[:, j % WMB]).then_inc(mod_mm, 1)
                pe.wait_ge(slots_in, 16)
                for n in range(2):
                    mm = nc.tensor.transpose(psum[7][:, n * (SLOTS // 2):(n + 1) * (SLOTS // 2)],
                                             slots_in_row[:, n * P:(n + 1) * P], ident[0:SLOTS // 2, 0:SLOTS // 2])
                mm.then_inc(slot_mm, 1)

            @block.vector
            def _(dve):
                st = Steps(dve, dve_steps)

                def step(ins):
                    st.did(ins)
                    st.settle()

                tt, ts = nc.vector.tensor_tensor, nc.vector.tensor_scalar
                dve.wait_ge(r_in, 32)
                st.did(ts(dtmp[:, 0], ident[0:E, 0:E], -1.0, 1.0, ALU.mult, ALU.add))
                st.did(nc.vector.memset(again[:], 1.0))
                st.did(nc.vector.memset(ones_row, 1.0))
                st.settle()
                st.did(nc.vector.memset(again[:, :, 0:1], 0.0))
                step(tt(dtmp[:, 1], sim, dtmp[:, 0], ALU.mult))
                step(tt(sim, dtmp[:, 1], ident[0:E, 0:E], ALU.add))
                dve.wait_ge(n_mm, 1)
                cj = psum[0][:].rearrange("p (h j e) -> p h e j", h=2, j=SELK)
                step(nc.vector.tensor_reduce(cnt_j.rearrange("p (h e) -> p h e", h=2), cj, AX.X, ALU.add))
                step(ts(cnt_j, cnt_j, 1.0, None, ALU.min))
                prim, secd = cnt_j[0:E, 0:E], cnt_j[0:E, E:2 * E]
                st.did(tt(dtmp[:, 0], sim, prim, ALU.mult))
                st.did(ts(dtmp[:, 1], prim, -1.0, 3e38, ALU.add, ALU.mult))
                st.settle()
                step(tt(cand, dtmp[:, 0], dtmp[:, 1], ALU.add))
                step(nc.vector.max(best, cand))
                step(nc.vector.max_index(best_u, best, cand))
                st.did(nc.vector.tensor_copy(best_f, best_u))
                st.did(tt(dtmp[:, 0], prim, ident[0:E, 0:E], ALU.mult))
                st.did(tt(dtmp[:, 1], secd, ident[0:E, 0:E], ALU.mult))
                st.settle()
                step(nc.vector.tensor_reduce(sec[:, 0:2], dtmp[:], AX.X, ALU.add))
                st.did(ts(sec[:, 2:3], sec[:, 0:1], -1.0, 1.0, ALU.mult, ALU.add))
                st.did(ts(sec[:, 3:4], best[:, 0:1], THRESH, None, ALU.is_ge))
                st.did(tt(sec[:, 5:6], best_f[:, 0:1], iota_col[0:E], ALU.subtract))
                st.settle()
                step(tt(sec[:, 4:5], sec[:, 1:2], sec[:, 2:3], ALU.mult))
                step(tt(sec[:, 4:5], sec[:, 4:5], sec[:, 3:4], ALU.mult))
                step(tt(sec[:, 5:6], sec[:, 5:6], sec[:, 4:5], ALU.mult))
                step(tt(sec[:, 6:7], sec[:, 5:6], iota_col[0:E], ALU.add))
                ts(diag, ident[0:E, 0:E], sec[:, 6:7], None, ALU.mult).then_inc(d_rows, 1)
                dve.wait_ge(map_mm, 1)
                step(nc.vector.tensor_copy(map_row, psum[1][:, 0:E]))
                flat = back[:].rearrange("p f c -> p (f c)")
                prod = flat[:, 0:SELK * NT * E // 2].bitcast(BF16).rearrange("p (t j e) -> p t j e", t=NT, j=SELK)
                for t in range(NT):
                    st.did(tt(prod[:, t], route_hot[:, t, SELK:], map_row.unsqueeze(1).to_broadcast([P, SELK, E]), ALU.mult))
                st.settle()
                step(nc.vector.tensor_reduce(moved[:], prod, AX.X, ALU.add))
                for t in range(NT):
                    st.did(tt(route_hot[:, t, SELK:], moved[:, t].unsqueeze(2).to_broadcast([P, SELK, E]),
                              iota_row[:].unsqueeze(1).to_broadcast([P, SELK, E]), ALU.is_equal))
                st.settle()
                nc.vector.tensor_reduce(chosen, route_hot[:].rearrange("p t j e -> p t e j"), AX.X, ALU.max).then_inc(sel_done, 1)
                dve.wait_ge(rank_mm, 1)
                for n in range(2):
                    half = psum[4 + n][:].rearrange("p (t e) -> p e t", e=E)
                    st.did(nc.vector.tensor_copy(counts[:, :, 8 * n:8 * n + 8], half))
                st.settle()
                fl = "p e t -> p (e t)"
                step(nc.vector.tensor_tensor_scan(upto.rearrange(fl), again.rearrange(fl), counts.rearrange(fl), 0.0, ALU.mult, ALU.add))
                st.did(ts(tiles_f.unsqueeze(2), upto[:, :, NT - 1:NT], float(P - 1), None, ALU.add))
                st.did(tt(counts[:], upto[:], counts[:], ALU.subtract))
                st.settle()
                step(nc.vector.tensor_copy(tiles_i, tiles_f))
                step(ts(tiles_i, tiles_i, 7, None, ALU.logical_shift_right))
                step(nc.vector.tensor_copy(tiles_f, tiles_i))
                step(ts(tiles_f, tiles_f, 1.0, None, ALU.max))
                step(nc.vector.tensor_tensor_scan(tile_end, ones_row, tiles_f, 0.0, ALU.mult, ALU.add))
                step(tt(base, tile_end, tiles_f, ALU.subtract))
                step(ts(base, base, float(P), None, ALU.mult))
                for n in range(2):
                    st.did(tt(pos[:, 8 * n:8 * n + 8], psum[2 + n][:].rearrange("p (t e) -> p t e", e=E),
                              base.unsqueeze(1).to_broadcast([P, 8, E]), ALU.add))
                st.settle()
                step(tt(pos[:], pos[:], counts.rearrange("p e t -> p t e"), ALU.add))
                for t in range(NT):
                    if t >= 2:
                        dve.wait_ge(pos_done, t - 1)
                    step(tt(picked[:, t % 2], route_hot[:, t], pos[:, t].unsqueeze(1).to_broadcast([P, TOPK, E]), ALU.mult))
                    step(nc.vector.tensor_reduce(pos_f[:, t], picked[:, t % 2], AX.X, ALU.add))
                    nc.vector.tensor_copy(pos_u[:, t], pos_f[:, t]).then_inc(pos_done, 1)
                step(ts(gcol[:, 2:3], iota_col[:], float(P), None, ALU.add))
                st.did(nc.vector.tensor_scalar(dtmp0[:, 0:E], tile_end, iota_col[:], None, ALU.is_le, ALU.add, accum_out=gcol[:, 0:1]))
                st.did(nc.vector.tensor_scalar(dtmp0[:, E:], tile_end, gcol[:, 2:3], None, ALU.is_le, ALU.add, accum_out=gcol[:, 1:2]))
                st.settle()
                ts(gcol[:, 0:2], gcol[:, 0:2], float(E - 1), None, ALU.min).then_inc(eid_done, 1)
                dve.wait_ge(eid_mm, 1)
                st.did(nc.vector.tensor_copy(tile_expert[:, 0:SLOTS], psum[6][0:1, 0:SLOTS]))
                st.did(ts(expert_end[:], tile_end[0:1], 1.0, None, ALU.add))
                for f in range(FT):
                    dve.wait_ge(had_mm, f + 1)
                    nc.vector.tensor_copy(wd[:, f], psum[f % 2][:]).then_inc(had_out, 1)
                dve.wait_ge(had_out, FT)
                src, dst = wd, back
                n = 1
                while n < FT:
                    sv = src[:].rearrange("p (a two n) c -> p a two (n c)", two=2, n=n)
                    dv = dst[:].rearrange("p (a two n) c -> p a two (n c)", two=2, n=n)
                    st.settle()
                    st.did(tt(dv[:, :, 0], sv[:, :, 0], sv[:, :, 1], ALU.add))
                    st.did(tt(dv[:, :, 1], sv[:, :, 0], sv[:, :, 1], ALU.subtract))
                    src, dst = dst, src
                    n *= 2
                dve.wait_ge(c_done, 1)
                nc.vector.tensor_copy(act_b[:], act_c.unsqueeze(2).to_broadcast([P, KC, P])).then_inc(c_wide, 1)
                for j in range(6):
                    dve.wait_ge(mod_mm, j + 1)
                    mod_vector(st, 1, j, psum[2 + j % 4][:], gate_tmp, mod_out)
                dve.wait_ge(mod_out, 6)
                dve.wait_ge(rows_in, 32)
                for j in (3, 4):
                    st.did(nc.vector.tensor_tensor(mod[:, 1, j, :], mod[:, 1, j, :], su_row, ALU.mult))
                st.did(nc.vector.scalar_tensor_tensor(down_scale[:], down_row, float(INTER) ** -0.5, mod[:, 1, 5, :],
                                                      ALU.mult, ALU.mult))
                st.settle()
                for f in range(FT):
                    st.did(nc.vector.scalar_tensor_tensor(wd[:, f], wd[:, f], su_dp[:, f:f + 1], down_scale[:], ALU.mult, ALU.mult))
                dve.wait_ge(slot_mm, 1)
                st.did(nc.vector.tensor_copy(slot_rows[:, 0:SLOTS].rearrange("p (q n) -> p n q", n=2),
                                             psum[7][:, 0:SLOTS].rearrange("p (n q) -> p n q", n=2)))
                st.settle()


        with ExitStack() as ph, nc.Block() as block:
            psem = phase_semaphores(ph)

            cv = Carver()
            UPW, DOWNW = KC * 2 * FI, 2 * C
            up_ring = cv(RING * UPW)
            down_ring = cv(RING * DOWNW)[0:FH]
            xg = cv(2, C)
            xgT = cv(2, KC, P)
            gate_act = cv(2, FI)
            hidden = cv(2, FI)
            hiddenT = cv(2, 2, P)[0:FH]
            y = cv(2, C)
            st_tok = cv(2, 1).bitcast(I32)
            spare, dve_spare = cv(1), cv(2)
            (experts_ready, xT_mm, xT_out, gu_mm, gate_done, hidden_done, hT_mm, hT_out, y_mm, y_out,
             pool_steps) = (psem("m_" + n) for n in
                            ("experts_ready",  "xT_mm", "xT_out", "gu_mm", "gate_done", "hidden_done",
                             "hT_mm", "hT_out", "y_mm", "y_out", "pool_steps"))
            w_in = [psem(f"m_w_in{r}") for r in range(RING)]
            x_in = [psem(f"m_x_in{b}") for b in range(2)]
            y_stored = [psem(f"m_y_stored{b}") for b in range(2)]

            def schedule(eng, turn, steps=None, per=0):
                def tile(t):
                    return (t, t % 2, t // 2) if t >= 0 else None
                used = eng.value_load(expert_end[0:1, E - 1:E], min_val=E + 1, max_val=SLOTS + 1) - 1
                for g in range(-1, 3):
                    turn(tile(g - 1) if g > 0 else None, tile(g), tile(g + 1))
                with eng.Fori(0, (SLOTS - 2) // 2) as i:
                    with eng.If(i * 2 + 2 < used):
                        if steps:
                            steps.loop(i, per)
                        turn((i * 2 + 2, 0, i + 1), (i * 2 + 3, 1, i + 1), (i * 2 + 4, 0, i + 2))
                        turn((i * 2 + 3, 1, i + 1), (i * 2 + 4, 0, i + 2), (i * 2 + 5, 1, i + 2))
                return used

            @block.sync
            def _(sp):
                def load(e, r):
                    up, down = a["moe_up"], a["moe_down"]
                    one = (lambda x: x[e]) if isinstance(e, int) else (lambda x: x[bass.ds(e, 1)].rearrange("o p k n -> (o p) k n"))
                    sp.dma_start(up_ring[:, r * UPW:(r + 1) * UPW], one(up).rearrange("p k n -> p (k n)")).then_inc(w_in[r], 16)
                    sp.dma_start(down_ring[:, r * DOWNW:(r + 1) * DOWNW], one(down).rearrange("p k n -> p (k n)")).then_inc(w_in[r], 16)

                def landed(e, r):
                    sp.wait_ge(w_in[r], e)
                    sp.sem_inc(experts_ready, 1)

                for e in range(RING):
                    load(e, e)
                    if e:
                        landed(32, e - 1)
                with sp.Fori(1, E // RING) as n:
                    for r in range(RING):
                        e = n * RING + r
                        done = sp.value_load(expert_end[0:1, bass.ds(e - RING, 1)], min_val=2, max_val=SLOTS + 1)
                        sp.wait_ge(y_mm, done)
                        load(e, r)
                        landed(n * 32 if r == 0 else n * 32 + 32, (r - 1) % RING)
                landed(32 * E // RING, RING - 1)

            @block.gpsimd
            def _(pool):
                st = Steps(pool, pool_steps)

                def turn(before, g, after):
                    if after is not None:
                        t, b, half = after
                        wait_tile(pool, x_in[b], 16, shift(half, -1))
                        st.did(nc.gpsimd.tensor_copy(st_tok[:, b], slot_rows[:, t:t + 1] if isinstance(t, int) else slot_rows[:, bass.ds(t, 1)]))
                        st.settle()
                        st.did(nc.gpsimd.tensor_tensor(spare, neg_half[:], neg_half[:], ALU.add))
                        wait_tile(pool, xT_mm, 1, shift(t, -2))
                        st.settle()
                        st.did(nc.gpsimd.tensor_tensor(spare, neg_half[:], neg_half[:], ALU.add))
                        nc.gpsimd.indirect_dma_start(out=xg[:, b], out_offset=None, in_=h_moe,
                                                     in_offset=bass.IndirectOffsetOnAxis(ap=st_tok[:, b], axis=0)).then_inc(x_in[b], 16)
                schedule(pool, turn, st, POOL_M)

            @block.tensor
            def _(pe):
                def turn(before, g, after):
                    if before is not None:
                        t, b, _ = before
                        wait_tile(pe, hidden_done, 1, t)
                        wait_tile(pe, hT_out, 1, shift(t, -2))
                        for n in range(2):
                            mm = nc.tensor.transpose(psum[4 + b][0:FH, n * P:(n + 1) * P], hidden[:, b, n * FH:(n + 1) * FH], ident[:])
                        mm.then_inc(hT_mm, 1)
                    if g is not None:
                        t, b, _ = g
                        e = pe.value_load(tile_expert[0:1, bass.ds(t, 1)], min_val=0, max_val=E - 1)
                        wait_tile(pe, xT_out, 1, t)
                        wait_tile(pe, hidden_done, 1, shift(t, -2))
                        pe.wait_ge(experts_ready, e + 1)
                        for k in range(KC):
                            mm = nc.tensor.matmul(psum[2 + b][:, 0:2 * FI], xgT[:, b, k],
                                                  up_ring[:, bass.ds((e % RING) * UPW + k * 2 * FI, 2 * FI)],
                                                  start=(k == 0), stop=(k == KC - 1))
                        mm.then_inc(gu_mm, 1)
                    if after is not None:
                        t, b, half = after
                        wait_tile(pe, x_in[b], 16, half)
                        wait_tile(pe, xT_out, 1, shift(t, -2))
                        for k in range(KC):
                            mm = nc.tensor.transpose(psum[b][:, k * P:(k + 1) * P], xg[:, b, k * P:(k + 1) * P], ident[:])
                        mm.then_inc(xT_mm, 1)
                    if before is not None:
                        t, b, _ = before
                        e = pe.value_load(tile_expert[0:1, bass.ds(t, 1)], min_val=0, max_val=E - 1)
                        wait_tile(pe, hT_out, 1, t)
                        wait_tile(pe, y_out, 1, shift(t, -2))
                        for n in range(2):
                            mm = nc.tensor.matmul(psum[6 + b][:], hiddenT[:, b, n],
                                                  down_ring[:, bass.ds((e % RING) * DOWNW + n * C, C)],
                                                  start=(n == 0), stop=(n == 1))
                        mm.then_inc(y_mm, 1)
                pe.sem_inc(y_mm, 1)
                schedule(pe, turn)

            @block.scalar
            def _(act):
                y_rows = y_moe.rearrange("(g p) c -> g p c", p=P)

                def turn(before, g, after):
                    if before is not None:
                        t, b, _ = before
                        wait_tile(act, hT_mm, 1, t)
                        wait_tile(act, y_mm, 1, shift(t, -2), 2)
                        nc.scalar.copy(hiddenT[:, b], psum[4 + b][0:FH, 0:2 * P].rearrange("p (n q) -> p n q", n=2)).then_inc(hT_out, 1)
                    if g is not None:
                        t, b, _ = g
                        wait_tile(act, gu_mm, 1, t)
                        wait_tile(act, hidden_done, 1, shift(t, -2))
                        nc.scalar.activation(gate_act[:, b], psum[2 + b][:, 0:FI], ACT.Silu).then_inc(gate_done, 1)
                    if after is not None:
                        t, b, _ = after
                        wait_tile(act, xT_mm, 1, t)
                        wait_tile(act, gu_mm, 1, shift(t, -2))
                        nc.scalar.copy(xgT[:, b].rearrange("p k n -> p (k n)"), psum[b][:]).then_inc(xT_out, 1)
                    if before is not None:
                        t, b, _ = before
                        wait_tile(act, y_out, 1, t)
                        dst = y_rows[t] if isinstance(t, int) else y_rows[bass.ds(t, 1)].rearrange("o p c -> (o p) c")
                        act.dma_start(dst, y[:, b]).then_inc(y_stored[b], 16)
                schedule(act, turn)

            @block.vector
            def _(dve):
                def turn(before, g, after):
                    if g is not None:
                        t, b, _ = g
                        wait_tile(dve, gate_done, 1, t)
                        wait_tile(dve, hT_mm, 1, shift(t, -2))
                        nc.vector.tensor_tensor(hidden[:, b], gate_act[:, b], psum[2 + b][:, FI:2 * FI], ALU.mult).then_inc(hidden_done, 1)
                    if before is not None:
                        t, b, half = before
                        wait_tile(dve, y_mm, 1, t, 2)
                        wait_tile(dve, y_stored[b], 16, shift(half, -1))
                        nc.vector.tensor_tensor(y[:, b], psum[6 + b][:], mod[:, 0, 5], ALU.mult).then_inc(y_out, 1)
                used = schedule(dve, turn)
                for b in range(2):
                    dve.wait_ge(y_stored[b], (used + 1) // 2 * 16)
                    nc.vector.memset(dve_spare[:, b:b + 1], 0.0)


        with ExitStack() as ph, nc.Block() as block:
            psem = phase_semaphores(ph)

            NHEAD = C // HD
            NQK = NHEAD + NKV1
            V1 = HD + 1
            cv = Carver()
            wq, wkv, wo = cv(KC, C), cv(KC, 2 * NKV1 * HD), cv(KC, C)
            bqk_row, bv_row, bo = cv(NQK * HD), cv(NKV1 * HD), cv(C)
            rope = cv(2, 4, HD)
            yg = route_hot[:].rearrange("p t j e -> p (t j e)").bitcast(F32).rearrange("p (j c) -> p j c", j=TOPK)
            kT = cv(NKV1, HP, KEYS1)
            kst = cv(NKV1, P)
            qT = cv(2, KC, P)
            qk = cv(2, NQK, HD)
            rot = cv(NQK, HD)
            vrow = cv(2, NKV1, HD)
            v = cv(2, NKV1, V1)
            HM = P // META
            v_meta = cv(2, HM, V1)
            meta_head = cv(HM)
            spread = cv(P)[0:META]
            prob_meta = cv(2, HM, META)
            zeros_b = cv(HM * V1 // 2).bitcast(BF16)
            prob = cv(4, 2 * P)
            probT = cv(4, 3 * P)
            kx = cv(NKV1, HP, HD)
            hT = cv(KC, P)
            h = cv(C)
            o = cv(2, C)
            oT = cv(KC, P)
            st1, r1 = cv(8), cv(2)
            nmx = cv(2, NHEAD)
            rsum = cv(2, NHEAD)
            st_pos = cv(TOPK).bitcast(I32)
            spare = cv(2)
            names = ("w_in", "ready", "y_sum", "stats", "rstd", "xhat", "h_done", "hT_mm", "hT_out", "q_mm", "kv_mm", "q_rows",
                     "kv_rows", "roped", "kx_done", "kst_out", "kT_mm", "qT_mm", "k_act", "k_dve", "q_in", "v_in", "s_mm", "mx_done", "exp_done", "pT_mm",
                     "pT_act", "pT_dve", "o_mm", "o_out", "oT_mm", "oT_out", "wo_mm", "x_pre", "x_out", "spread_done", "meta_mm", "v_meta_done", "dve_steps", "pool_steps")
            (w_in, ready, y_sum, stats, rstd, xhat, h_done, hT_mm, hT_out, q_mm, kv_mm, q_rows,
             kv_rows, roped, kx_done, kst_out, kT_mm, qT_mm, k_act, k_dve, q_in, v_in, s_mm, mx_done, exp_done, pT_mm,
             pT_act, pT_dve, o_mm, o_out, oT_mm, oT_out, wo_mm, x_pre, x_out, spread_done, meta_mm, v_meta_done, dve_steps, pool_steps) = (psem("b_" + n) for n in names)
            y_in = [psem(f"b_y_in{j}") for j in range(TOPK)]
            rope_in = [psem(f"b_rope_in{b}") for b in range(2)]
            ba, bb = psum[6], psum[7]
            N_DMA = 8

            def schedule(eng, turn, steps=None, per=0):
                stages = (4, 3, 2, 1, 0, -1)

                def tile(t):
                    return (t, t % 2, t // 2) if 0 <= t < NT else None
                for t in range(-4, 4):
                    turn(*[tile(t + n) for n in stages])
                turns = (NT - 8) // 2
                with eng.Fori(0, turns) as i:
                    if steps:
                        steps.loop(i, per)
                    for t in (4, 5):
                        turn(*[(i * 2 + (t + n), (t + n) % 2, i + (t + n) // 2) for n in stages])
                if steps:
                    steps.end(turns)
                for t in range(NT - 4, NT + 1):
                    turn(*[tile(t + n) for n in stages])

            def at_step(m, w, n):
                if n >= 0:
                    return (m[0], m[1], n) if m is not None else None
                return (w[0], w[1], NHEAD + n) if w is not None else None

            def by_dve(n):
                return n % 4 == 0

            def turned(eng, t, n):
                if by_dve(n):
                    wait_tile(eng, pT_dve, NHEAD // 4, t, n // 4 + 1)
                else:
                    wait_tile(eng, pT_act, 3 * NHEAD // 4, t, n - n // 4)

            def copy_pT(eng, copy, t, n, done):
                wait_tile(eng, pT_mm, NHEAD, t, n + 1)
                if n >= 4:
                    wait_tile(eng, o_mm, NHEAD, t, n - 3)
                else:
                    wait_tile(eng, o_mm, NHEAD, shift(t, -1), NHEAD + n - 3)
                cols = slice(0, 3 * P if n % HM == HM - 1 else 2 * P)
                copy(probT[:, n % 4, cols], psum[n % 4][:, cols]).then_inc(done, 1)

            def copy_keys(eng, copy, t, b, half, quadrants, done):
                wait_tile(eng, kst_out, 1, t)
                wait_tile(eng, s_mm, NHEAD, shift(t, -1), 8 * half + 8)
                at = META + P * b
                kv = slice(2 * half, 2 * half + 2)
                for r in quadrants:
                    q = slice(HD * r, HD * r + HD)
                    if isinstance(t, int) and t == 0:
                        copy(kT[q, kv, r, 0:META], kst[q, kv, 0:META])
                    last = copy(kT[q, kv, r, at:at + P], kst[q, kv])
                last.then_inc(done, 1)

            @block.sync
            def _(sp):
                sp.dma_start(wq[:], a["L1_attn_Wq"].rearrange("(k p) n -> p k n", p=P)).then_inc(w_in, 16)
                sp.dma_start(wkv[:], a["L1_attn_Wkv"].rearrange("(k p) n -> p k n", p=P)).then_inc(w_in, 16)
                sp.dma_start(wo[:], a["L1_attn_Wo"].rearrange("(k p) n -> p k n", p=P)).then_inc(w_in, 16)
                sp.dma_start(bqk_row[:, 0:C], a["L1_attn_bq"].partition_broadcast(P)).then_inc(w_in, 16)
                sp.dma_start(bqk_row[:, C:], a["L1_attn_bkv"][0:NKV1 * HD].partition_broadcast(P)).then_inc(w_in, 16)
                sp.dma_start(bv_row, a["L1_attn_bkv"][NKV1 * HD:].partition_broadcast(P)).then_inc(w_in, 16)
                sp.dma_start(bo, a["L1_attn_bo"].partition_broadcast(P)).then_inc(w_in, 16)
                sp.dma_start(meta_head, a["meta_head"]).then_inc(w_in, 16)
                tables = a["rope"].rearrange("(t p) k d -> t p k d", p=P)

                def turn(g, s, p, f, m, w):
                    if s is not None:
                        t, b, half = s
                        wait_tile(sp, roped, 1, shift(t, -2))
                        one = tables[t] if isinstance(t, int) else tables[bass.ds(t, 1)].rearrange("o p k d -> (o p) k d")
                        sp.dma_start(rope[:, b], one).then_inc(rope_in[b], 16)
                schedule(sp, turn)
                for b in range(2):
                    sp.wait_ge(rope_in[b], 16 * NT // 2)

            @block.gpsimd
            def _(pool):
                st = Steps(pool, pool_steps)
                st.did(nc.gpsimd.memset(kT[:], 0.0))
                st.did(nc.gpsimd.memset(v[:], 0.0))
                st.did(nc.gpsimd.memset(zeros_b, 0.0))
                st.settle()
                st.did(nc.gpsimd.memset(v[:, :, :, HD:V1], 1.0))
                st.settle()
                pool.sem_inc(ready, 1)
                mul = lambda out, x, y: nc.gpsimd.tensor_tensor(out, x, y, ALU.mult)

                def absorb():
                    st.settle()
                    st.did(nc.gpsimd.tensor_tensor(spare[:, 0:1], neg_half[:], neg_half[:], ALU.add))

                def values(t, b, half):
                    kv = slice(2 * half, 2 * half + 2)
                    wait_tile(pool, kv_rows, 1, t)
                    wait_tile(pool, o_mm, NHEAD, shift(t, -1), 8 * half + 8)
                    absorb()
                    nc.gpsimd.tensor_copy(v[:, b, kv, 0:HD], vrow[:, b, kv]).then_inc(v_in, 1)

                def rotate(t, b, rows, at, n):
                    x = qk[:, b, rows]
                    pairs = x.rearrange("p h (i two) -> p h i two", two=2)
                    out = rot[:, rows].rearrange("p h (i two) -> p h i two", two=2)
                    tab = rope[:, b, at + 1].rearrange("p (i two) -> p i two", two=2)
                    for one in range(2):
                        st.did(mul(out[:, :, :, one], pairs[:, :, :, 1 - one],
                                   tab[:, :, one].unsqueeze(1).to_broadcast([P, n, HD // 2])))
                    st.settle()
                    st.did(mul(x, x, rope[:, b, at].unsqueeze(1).to_broadcast([P, n, HD])))
                    st.settle()
                    return nc.gpsimd.tensor_tensor(x, x, rot[:, rows], ALU.add)

                def turn(g, s, p, f, m, w):
                    if p is not None:
                        t = p[0]
                        wait_tile(pool, stats, 1, t)
                        nc.gpsimd.tensor_tensor(r1[:, 1:2], st1[:, 7:8], neg_half[:], ALU.pow).then_inc(rstd, 1)
                        wait_tile(pool, xhat, 1, t)
                        st.did(mul(h, h, mod[:, 1, 1]))
                        st.settle()
                        nc.gpsimd.tensor_tensor(h, h, mod[:, 1, 0], ALU.add).then_inc(h_done, 1)
                    if m is not None:
                        values(m[0], m[1], 1)
                    if w is not None:
                        t = w[0]
                        pool.wait_ge(ready, 2)
                        nc.gpsimd.tensor_tensor(tile_of(x_res, t), tile_of(x_res, t), bo, ALU.add).then_inc(x_pre, 1)
                    if g is not None:
                        t = g[0]
                        wait_tile(pool, y_in[TOPK - 1], 16, shift(t, -1))
                        absorb()
                        st.did(nc.gpsimd.tensor_copy(st_pos, tile_of(pos_u, t)))
                        for j in range(TOPK):
                            wait_tile(pool, y_sum, TOPK, shift(t, -1), j + 1)
                            absorb()
                            nc.gpsimd.indirect_dma_start(out=yg[:, j], out_offset=None, in_=y_moe,
                                                         in_offset=bass.IndirectOffsetOnAxis(ap=st_pos[:, j:j + 1], axis=0)).then_inc(y_in[j], 16)
                    if p is not None:
                        t, b, half = p
                        wait_tile(pool, rope_in[b], 16, half)
                        wait_tile(pool, q_rows, 1, t)
                        wait_tile(pool, roped, 1, shift(t, -1))
                        st.did(rotate(t, b, slice(0, NHEAD), 0, NHEAD))
                    if f is not None:
                        values(f[0], f[1], 0)
                    if p is not None:
                        wait_tile(pool, kv_rows, 1, t)
                        st.settle()
                        t, b, half = p
                        rotate(t, b, slice(NHEAD, NQK), 2, NKV1).then_inc(roped, 1)
                schedule(pool, turn, st, POOL_B)

            @block.scalar
            def _(act):
                copy = nc.scalar.copy

                def turn(g, s, p, f, m, w):
                    for n in range(NHEAD):
                        if at_step(m, w, n):
                            t, b, _ = m
                            wait_tile(act, mx_done, NHEAD, t, n + 1)
                            if n >= 4:
                                wait_tile(act, pT_mm, NHEAD, t, n - 3)
                            else:
                                wait_tile(act, pT_mm, NHEAD, shift(t, -1), NHEAD + n - 3)
                            bank, bias = psum[n % 4], nmx[:, b, n:n + 1]
                            nc.scalar.activation(prob_meta[:, n // HM, n % HM], bank[:, 0:META], ACT.Exp, bias=bias)
                            nc.scalar.activation(prob[:, n % 4], bank[:, META:KEYS1], ACT.Exp, bias=bias).then_inc(exp_done, 1)
                        back = at_step(m, w, n - 2)
                        if back and not by_dve(back[2]):
                            copy_pT(act, copy, back[0], back[2], pT_act)
                        if f is not None and n == 1:
                            t, b, _ = f
                            wait_tile(act, qT_mm, 1, t)
                            wait_tile(act, s_mm, NHEAD, shift(t, -2))
                            copy(qT[:, b].rearrange("p k n -> p (k n)"), bb[:]).then_inc(q_in, 1)
                        if m is not None and n == 2:
                            copy_keys(act, copy, m[0], m[1], 1, (2, 3), k_act)
                        if f is not None and n == 3:
                            t, b, _ = f
                            wait_tile(act, kT_mm, 1, t)
                            wait_tile(act, k_act, 2, shift(t, -1))
                            wait_tile(act, k_dve, 2, shift(t, -1))
                            copy(kst.rearrange("p c n -> p (c n)"), ba[:]).then_inc(kst_out, 1)
                        if p is not None and n == 4:
                            t = p[0]
                            wait_tile(act, hT_mm, 1, t)
                            wait_tile(act, kv_mm, 1, shift(t, -1))
                            copy(hT.rearrange("p k n -> p (k n)"), bb[:]).then_inc(hT_out, 1)
                        if f is not None and n == 10:
                            copy_keys(act, copy, f[0], f[1], 0, (2, 3), k_act)
                schedule(act, turn)

            @block.tensor
            def _(pe):
                def turn(g, s, p, f, m, w):
                    for n in range(NHEAD):
                        if m is not None:
                            t, b, _ = m
                            if n == 0:
                                wait_tile(pe, q_in, 1, t)
                            if n % 8 == 0:
                                for ks in (k_act, k_dve):
                                    wait_tile(pe, ks, 2, t, n // 8 + 1)
                            if n >= 4:
                                turned(pe, t, n - 4)
                            elif not (isinstance(t, int) and t == 0):
                                turned(pe, shift(t, -1), NHEAD + n - 4)
                            kind = t if isinstance(t, int) and t < 2 else 2 + b
                            bank = psum[n % 4][:, 0:KEYS1]
                            nc.tensor.matmul(bank, ident_b[:], mask1[:, kind], start=True, stop=False)
                            nc.tensor.matmul(bank, qT[:, b, n // HP], kT[:, n // HP, n % HP], start=False, stop=True).then_inc(s_mm, 1)
                        if at_step(m, w, n - 2):
                            t, b, one = at_step(m, w, n - 2)
                            wait_tile(pe, exp_done, NHEAD, t, one + 1)
                            for k in range(2):
                                mm = nc.tensor.transpose(psum[one % 4][:, k * P:(k + 1) * P], prob[:, one % 4, k * P:(k + 1) * P], ident[:])
                            if one % HM == HM - 1:
                                mm = nc.tensor.transpose(psum[one % 4][:, 2 * P:3 * P], prob_meta[:, one // HM].rearrange("p h k -> p (h k)"), ident[:])
                            mm.then_inc(pT_mm, 1)
                        if at_step(m, w, n - 4):
                            t, b, one = at_step(m, w, n - 4)
                            turned(pe, t, one)
                            if one % 8 == 0:
                                wait_tile(pe, v_in, 2, t, one // 8 + 1)
                                wait_tile(pe, o_out, 2, shift(t, -1), one // 8 + 1)
                                nc.tensor.matmul(psum[4 + one // HM][:, 0:HM * V1], ident_b[:], zeros_b, start=True, stop=False)
                            out = psum[4 + one // 8][:, (one % 8) * V1:(one % 8 + 1) * V1]
                            c = one // HP
                            nc.tensor.matmul(out, probT[:, one % 4, 0:P], v[:, 0, c], start=False, stop=False)
                            last = one % HM == HM - 1
                            mm = nc.tensor.matmul(out, probT[:, one % 4, P:2 * P], v[:, 1, c], start=False, stop=False)
                            if last:
                                pe.wait_ge(v_meta_done, 1)
                                mm = nc.tensor.matmul(psum[4 + one // HM][:, 0:HM * V1], probT[:, one % 4, 2 * P:],
                                                      v_meta[:, one // HM].rearrange("p h d -> p (h d)"), start=False, stop=True)
                            mm.then_inc(o_mm, 1)
                        if f is not None and isinstance(f[0], int) and f[0] == 0 and n == 0:
                            pe.wait_ge(spread_done, 1)
                            pe.wait_ge(kv_rows, 1)
                            nc.tensor.matmul(psum[5][:, 0:NKV1 * HD], spread, vrow[0:META, 0].rearrange("p h d -> p (h d)"),
                                             start=True, stop=True).then_inc(meta_mm, 1)
                        if f is not None and n == 0:
                            t, b, _ = f
                            wait_tile(pe, roped, 1, t)
                            for k in range(KC):
                                mm = nc.tensor.transpose(bb[:, k * P:(k + 1) * P], qk[:, b, HP * k:HP * k + HP].rearrange("p h d -> p (h d)"), ident[:])
                            mm.then_inc(qT_mm, 1)
                        if f is not None and n == 2:
                            t, b, _ = f
                            wait_tile(pe, kx_done, 1, t)
                            wait_tile(pe, x_out, 1, shift(t, -3))
                            for c in range(NKV1):
                                mm = nc.tensor.transpose(ba[:, c * P:(c + 1) * P], kx[:, c].rearrange("p r d -> p (r d)"), ident[:])
                            mm.then_inc(kT_mm, 1)
                        if p is not None and n == 3:
                            t = p[0]
                            wait_tile(pe, h_done, 1, t)
                            wait_tile(pe, q_in, 1, shift(t, -1))
                            for k in range(KC):
                                mm = nc.tensor.transpose(bb[:, k * P:(k + 1) * P], h[:, k * P:(k + 1) * P], ident[:])
                            mm.then_inc(hT_mm, 1)
                        if w is not None and n == 6:
                            t, b, _ = w
                            wait_tile(pe, o_out, 2, t)
                            if f is not None:
                                wait_tile(pe, kst_out, 1, f[0])
                            for k in range(KC):
                                mm = nc.tensor.transpose(ba[:, k * P:(k + 1) * P], o[:, b, k * P:(k + 1) * P], ident[:])
                            mm.then_inc(oT_mm, 1)
                        if p is not None and n == 6:
                            pe.wait_ge(w_in, 16 * N_DMA)
                            wait_tile(pe, hT_out, 1, p[0])
                            for k in range(KC):
                                mm = nc.tensor.matmul(bb[:], hT[:, k], wq[:, k], start=(k == 0), stop=(k == KC - 1))
                            mm.then_inc(q_mm, 1)
                        if w is not None and n == 9:
                            wait_tile(pe, oT_out, 1, w[0])
                            pe.wait_ge(ready, 2)
                            for k in range(KC):
                                mm = nc.tensor.matmul(ba[:], oT[:, k], wo[:, k], start=(k == 0), stop=(k == KC - 1))
                            mm.then_inc(wo_mm, 1)
                        if p is not None and n == 10:
                            wait_tile(pe, q_rows, 1, p[0])
                            for k in range(KC):
                                mm = nc.tensor.matmul(bb[:, 0:2 * NKV1 * HD], hT[:, k], wkv[:, k], start=(k == 0), stop=(k == KC - 1))
                            mm.then_inc(kv_mm, 1)
                schedule(pe, turn)

            @block.vector
            def _(dve):
                st = Steps(dve, dve_steps)
                dve.wait_ge(w_in, 16 * N_DMA)
                st.did(nc.vector.tensor_tensor(wo[:], wo[:], mod[:, 1, 2].unsqueeze(1).to_broadcast([P, KC, C]), ALU.mult))
                st.did(nc.vector.tensor_tensor(bo, bo, mod[:, 1, 2], ALU.mult))
                nc.vector.tensor_copy(spread.rearrange("p (h k) -> p h k", h=HM),
                                      ident[0:META, 0:META].unsqueeze(1).to_broadcast([META, HM, META])).then_inc(spread_done, 1)
                st.settle()
                dve.wait_ge(ready, 1)
                dve.sem_inc(ready, 1)

                def absorb():
                    st.settle()
                    st.did(nc.vector.memset(spare[:, 1:2], 0.0))

                def o_norm(t, b, i):
                    wait_tile(dve, o_mm, NHEAD, t, 8 * i + 8)
                    if i == 0:
                        wait_tile(dve, oT_mm, 1, shift(t, -2))
                    ob = psum[4 + i][:, 0:8 * V1].rearrange("p (h d) -> p h d", h=8)
                    rs = rsum[:, b, 8 * i:8 * i + 8]
                    st.did(nc.vector.reciprocal(rs.unsqueeze(2), ob[:, :, HD:V1]))
                    st.settle()
                    nc.vector.tensor_tensor(o[:, b, 256 * i:256 * i + 256].rearrange("p (h d) -> p h d", h=8), ob[:, :, 0:HD],
                                            rs.unsqueeze(2).to_broadcast([P, 8, HD]), ALU.mult).then_inc(o_out, 1)

                def turn(g, s, p, f, m, w):
                    for n in range(NHEAD):
                        if m is not None:
                            t, b, _ = m
                            wait_tile(dve, s_mm, NHEAD, t, n + 1)
                            if n == 0:
                                wait_tile(dve, exp_done, NHEAD, shift(t, -2))
                            nc.vector.tensor_reduce(nmx[:, b, n:n + 1], psum[n % 4][:, 0:KEYS1], AX.X, ALU.max,
                                                    negate=True).then_inc(mx_done, 1)
                        back = at_step(m, w, n - 2)
                        if back and by_dve(back[2]):
                            copy_pT(dve, nc.vector.tensor_copy, back[0], back[2], pT_dve)
                        if f is not None and isinstance(f[0], int) and f[0] == 0 and n == 0:
                            dve.wait_ge(meta_mm, 1)
                            for half in range(2):
                                st.did(nc.vector.tensor_copy(v_meta[:, half, :, HD:V1], meta_head.unsqueeze(2)))
                                for j in range(2):
                                    heads, c = slice(HP * j, HP * j + HP), 2 * half + j
                                    st.did(nc.vector.tensor_tensor(v_meta[:, half, heads, 0:HD],
                                                                   psum[5][:, c * HD:(c + 1) * HD].unsqueeze(1).to_broadcast([P, HP, HD]),
                                                                   meta_head[:, heads].unsqueeze(2).to_broadcast([P, HP, HD]), ALU.mult))
                            st.settle()
                            dve.sem_inc(v_meta_done, 1)
                        if f is not None and n == 0:
                            t, b, _ = f
                            wait_tile(dve, roped, 1, t)
                            wait_tile(dve, kT_mm, 1, shift(t, -1))
                            nc.vector.tensor_copy(kx[:], qk[:, b, NHEAD:].unsqueeze(2).to_broadcast([P, NKV1, HP, HD])).then_inc(kx_done, 1)
                        if p is not None and n == 0:
                            t = p[0]
                            wait_tile(dve, y_sum, TOPK, t)
                            wait_tile(dve, xhat, 1, shift(t, -1))
                            absorb()
                            st.did(nc.vector.bn_stats(st1[:, 0:6], tile_of(x_res, t)))
                            absorb()
                            st.did(nc.vector.bn_aggr(st1[:, 6:8], st1[:, 0:6]))
                            st.settle()
                            nc.vector.tensor_scalar(st1[:, 7:8], st1[:, 7:8], EPS, None, ALU.add).then_inc(stats, 1)
                        if p is not None and n == 1:
                            t = p[0]
                            wait_tile(dve, rstd, 1, t)
                            wait_tile(dve, stats, 1, t)
                            wait_tile(dve, hT_mm, 1, shift(t, -1))
                            nc.vector.tensor_scalar(h, tile_of(x_res, t), st1[:, 6:7], r1[:, 1:2],
                                                    ALU.subtract, ALU.mult).then_inc(xhat, 1)
                        if m is not None and n == 2:
                            copy_keys(dve, nc.vector.tensor_copy, m[0], m[1], 1, (0, 1), k_dve)
                        if w is not None and n == 4:
                            o_norm(w[0], w[1], 1)
                        if w is not None and n == 7:
                            t = w[0]
                            wait_tile(dve, oT_mm, 1, t)
                            wait_tile(dve, wo_mm, 1, shift(t, -1))
                            nc.vector.tensor_copy(oT.rearrange("p k n -> p (k n)"), ba[:]).then_inc(oT_out, 1)
                        if s is not None and n < TOPK:
                            t, b, _ = s
                            xt = tile_of(x_res, t)
                            wait_tile(dve, y_in[n], 16, t)
                            if n:
                                wait_tile(dve, y_sum, TOPK, t, n)
                            wt = route_w[:, t, n:n + 1] if isinstance(t, int) else tile_of(route_w, t)[:, n:n + 1]
                            nc.vector.scalar_tensor_tensor(xt, yg[:, n], wt, xt, ALU.mult, ALU.add).then_inc(y_sum, 1)
                        if p is not None and n == 8:
                            t, b, _ = p
                            wait_tile(dve, q_mm, 1, t)
                            wait_tile(dve, qT_mm, 1, shift(t, -2))
                            wait_tile(dve, kx_done, 1, shift(t, -2))
                            nc.vector.tensor_tensor(qk[:, b, 0:NHEAD].rearrange("p h d -> p (h d)"), bb[:], bqk_row[:, 0:C], ALU.add).then_inc(q_rows, 1)
                        if w is not None and n == 11:
                            t = w[0]
                            wait_tile(dve, wo_mm, 1, t)
                            wait_tile(dve, x_pre, 1, t)
                            nc.vector.tensor_tensor(tile_of(x_res, t), ba[:], tile_of(x_res, t), ALU.add).then_inc(x_out, 1)
                        if f is not None and n == 10:
                            copy_keys(dve, nc.vector.tensor_copy, f[0], f[1], 0, (0, 1), k_dve)
                        if m is not None and n == 12:
                            o_norm(m[0], m[1], 0)
                        if p is not None and n == 12:
                            t, b, _ = p
                            wait_tile(dve, kv_mm, 1, t)
                            st.did(nc.vector.tensor_tensor(qk[:, b, NHEAD:].rearrange("p h d -> p (h d)"), bb[:, 0:NKV1 * HD], bqk_row[:, C:], ALU.add))
                            st.settle()
                            wait_tile(dve, v_in, 2, shift(t, -2))
                            nc.vector.tensor_tensor(vrow[:, b].rearrange("p h d -> p (h d)"), bb[:, NKV1 * HD:2 * NKV1 * HD], bv_row, ALU.add).then_inc(kv_rows, 1)
                schedule(dve, turn, st, DVE_B)
                wait_tile(dve, x_out, 1, NT - 1)

        with ExitStack() as ph, nc.Block() as block:
            psem = phase_semaphores(ph)

            NG = NT // GT
            FR = mybir.dt.float32r
            scoped.close()

            def fr(name, *shape):
                return ph.enter_context(nc.sbuf_tensor(name, [P, *shape], FR))[:]

            wd_lo, wd_hi = fr("wd_lo", FT, C), fr("wd_hi", FT, C)
            w_hi, w_lo = fr("w_hi", 2, KC, 2, P), fr("w_lo", 2, KC, 2, P)
            x_hi, x_lo = fr("x_hi", KC, GN), fr("x_lo", KC, GN)
            in_hi, in_lo = fr("in_hi", 2, GN), fr("in_lo", 2, GN)
            arena = ph.enter_context(nc.sbuf_tensor("ffn_arena", [P, RING * KC * 2 * P + GN + 64], F32))
            cv = Carver()
            raw = cv(RING, KC, 2, P)
            inner = cv(GN)
            scales = cv(2, FT)
            st1, r1 = cv(8), cv(2)
            spare = cv(1)
            old_mod, old_hot = mod[:, 0], route_hot[:].rearrange("p t j e -> p (t j e)").bitcast(F32)
            h, y, gate_act = old_mod[:, 0:2], old_mod[:, 2:4], old_mod[:, 4:6]
            hT, mixT = (old_hot[:, n * KC * GN:(n + 1) * KC * GN].rearrange("p (k n) -> p k n", k=KC) for n in range(2))
            names = ("scale_in", "stats", "rstd", "xhat", "h_done", "hT_mm", "hT_out", "mixed", "xT_mm", "x_hi_done",
                     "x_lo_done", "w_hi_done", "w_lo_done", "gate_mm", "up_mm", "gate_done", "inner_done", "in_hi_done",
                     "in_lo_done", "wd_hi_done", "wd_lo_done", "down_mm", "y_out", "scaled", "dve_steps", "pool_steps")
            (scale_in, stats, rstd, xhat, h_done, hT_mm, hT_out, mixed, xT_mm, x_hi_done,
             x_lo_done, w_hi_done, w_lo_done, gate_mm, up_mm, gate_done, inner_done, in_hi_done,
             in_lo_done, wd_hi_done, wd_lo_done, down_mm, y_out, scaled, dve_steps, pool_steps) = (psem("f_" + n) for n in names)
            w_in = [psem(f"f_w_in{r}") for r in range(RING)]
            y_stored = [psem(f"f_y_stored{b}") for b in range(2)]
            gate_bank, up_bank = psum[4], psum[5]

            def schedule(eng, prepare, group, finish, steps=None, per=0):
                prepare()
                group(0, False)
                with eng.Fori(1, NG - 1) as g:
                    if steps:
                        steps.loop(g - 1, per)
                    group(g, False)
                if steps:
                    steps.end(NG - 2)
                group(NG - 1, True)
                finish()

            def tile_at(f):
                return (f - 1) // 3 if f % 3 == 1 and 0 < f < 3 * GT else None

            def first(g):
                return isinstance(g, int) and g == 0

            def landed(eng, g, f):
                eng.wait_ge(w_in[f % RING], g * (16 * FT // RING) + 16 * (f // RING + 1))

            @block.sync
            def _(sp):
                sp.dma_start(scales[:], a["ug_cols"]).then_inc(scale_in, 16)
                for r in range(RING):
                    sp.dma_start(raw[:, r], a["ffn_up"][r]).then_inc(w_in[r], 16)

                def group(g, last):
                    for f in range(FT):
                        if last and f >= FT - RING:
                            break
                        nxt = (f + RING) % FT
                        sp.wait_ge(w_lo_done, g * FT + f + 1)
                        sp.dma_start(raw[:, nxt % RING], a["ffn_up"][nxt]).then_inc(w_in[nxt % RING], 16)
                schedule(sp, lambda: None, group, lambda: None)

            @block.gpsimd
            def _(pool):
                st = Steps(pool, pool_steps)

                def norm(t, b):
                    wait_tile(pool, stats, 1, t)
                    nc.gpsimd.tensor_tensor(r1[:, b:b + 1], st1[:, 7:8], neg_half[:], ALU.pow).then_inc(rstd, 1)
                    wait_tile(pool, xhat, 1, t)
                    st.did(nc.gpsimd.tensor_tensor(h[:, b], h[:, b], mod[:, 1, 4], ALU.mult))
                    st.settle()
                    nc.gpsimd.tensor_tensor(h[:, b], h[:, b], mod[:, 1, 3], ALU.add).then_inc(h_done, 1)
                norm(0, 0)
                norm(1, 1)
                with pool.Fori(0, NT // 2 - 1) as i:
                    st.loop(i, 2)
                    norm(i * 2 + 2, 0)
                    norm(i * 2 + 3, 1)
                st.end(NT // 2 - 1)

            @block.tensor
            def _(pe):
                def product(bank, pairs):
                    passes = [(x, y) for (x_h, x_l), (y_h, y_l) in pairs for x, y in ((x_h, y_h), (x_h, y_l), (x_l, y_h))]
                    for n, (x, y) in enumerate(passes):
                        mm = nc.tensor.matmul(bank, x, y, start=(n == 0), stop=(n == len(passes) - 1))
                    return mm

                def transposes(t, i):
                    b = i % 2
                    wait_tile(pe, h_done, 1, t)
                    wait_tile(pe, hT_out, 1, shift(t, -2))
                    for k in range(KC):
                        mm = nc.tensor.transpose(psum[6 + b][:, k * P:(k + 1) * P], h[:, b, k * P:(k + 1) * P], ident[:])
                    mm.then_inc(hT_mm, 1)

                def transform(g, k):
                    wait_tile(pe, mixed, 1, g)
                    if k >= 2:
                        wait_tile(pe, x_lo_done, KC, g, k - 1)
                    nc.tensor.matmul(psum[6 + k % 2][:], had[:], hT[:, k], start=True, stop=True).then_inc(xT_mm, 1)

                def prepare():
                    for i in range(GT):
                        transposes(i, i)
                    for k in range(KC):
                        transform(0, k)

                def down(g, f):
                    n, b = g * FT + f, f % 2
                    wait_tile(pe, in_lo_done, 1, n)
                    if f == 0:
                        wait_tile(pe, y_out, GT, shift(g, -1))
                    if first(g):
                        wait_tile(pe, wd_lo_done, 1, f)
                    for i in range(GT):
                        tokens = slice(i * P, (i + 1) * P)
                        x_h, x_l = in_hi[:, b, tokens], in_lo[:, b, tokens]
                        for j, (x, w) in enumerate(((x_h, wd_hi[:, f]), (x_h, wd_lo[:, f]), (x_l, wd_hi[:, f]))):
                            mm = nc.tensor.matmul(psum[i][:], x, w, start=(f == 0 and j == 0), stop=(f == FT - 1 and j == 2))
                    mm.then_inc(down_mm, 1)

                def group(g, last):
                    wait_tile(pe, x_lo_done, KC, g)
                    for f in range(FT):
                        n, b = g * FT + f, f % 2
                        wait_tile(pe, w_lo_done, 1, n)
                        wait_tile(pe, gate_done, 1, shift(n, -1))
                        pair = lambda k, half: ((w_hi[:, b, k, half], w_lo[:, b, k, half]), (x_hi[:, k], x_lo[:, k]))
                        product(gate_bank[:], [pair(k, 0) for k in range(KC)]).then_inc(gate_mm, 1)
                        wait_tile(pe, inner_done, 1, shift(n, -1))
                        product(up_bank[:], [pair(k, 1) for k in range(KC)]).then_inc(up_mm, 1)
                        if not last and f == FT - 1:
                            transform(g + 1, 0)
                            transform(g + 1, 1)
                        if f:
                            down(g, f - 1)
                        elif not first(g):
                            down(g - 1, FT - 1)
                        if not last and tile_at(f - 2) is not None:
                            i = tile_at(f - 2)
                            transposes((g + 1) * GT + i, i)
                    if not last:
                        transform(g + 1, 2)
                        transform(g + 1, 3)
                schedule(pe, prepare, group, lambda: down(NG - 1, FT - 1))

            @block.scalar
            def _(act):
                out_rows = out[0].rearrange("(t p) c -> t p c", p=P)

                def copy_hT(t, i):
                    wait_tile(act, hT_mm, 1, t)
                    if i == 0:
                        wait_tile(act, xT_mm, 1, shift(t, -1))
                    nc.scalar.copy(hT[:, :, i * P:(i + 1) * P], psum[6 + i % 2][:].rearrange("p (k n) -> p k n", k=KC)).then_inc(hT_out, 1)

                def split_x(g, k):
                    wait_tile(act, xT_mm, KC, g, k + 1)
                    nc.scalar.copy(x_hi[:, k], psum[6 + k % 2][:]).then_inc(x_hi_done, 1)

                def split_w(g, f):
                    n = g * FT + f
                    landed(act, g, f)
                    wait_tile(act, up_mm, 1, shift(n, -2))
                    nc.scalar.copy(w_hi[:, f % 2], raw[:, f % RING]).then_inc(w_hi_done, 1)

                def store(g, i):
                    t = g * GT + i
                    wait_tile(act, y_out, 1, t)
                    dst = out_rows[t] if isinstance(t, int) else out_rows[bass.ds(t, 1)].rearrange("o p c -> (o p) c")
                    act.dma_start(dst, y[:, i % 2]).then_inc(y_stored[i % 2], 16)

                def prepare():
                    split_w(0, 0)
                    for i in range(GT):
                        copy_hT(i, i)
                    for k in range(KC):
                        split_x(0, k)
                    act.wait_ge(scaled, 1)

                def group(g, last):
                    for f in range(FT):
                        n, b = g * FT + f, f % 2
                        if f < FT - 1:
                            split_w(g, f + 1)
                        elif not last:
                            split_w(g + 1, 0)
                        wait_tile(act, gate_mm, 1, n)
                        wait_tile(act, inner_done, 1, shift(n, -2))
                        nc.scalar.activation(gate_act[:, b], gate_bank[:], ACT.Silu, scale=scales[:, 0, f:f + 1]).then_inc(gate_done, 1)
                        if first(g):
                            nc.scalar.copy(wd_hi[:, f], wd[:, f]).then_inc(wd_hi_done, 1)
                        wait_tile(act, inner_done, 1, n)
                        wait_tile(act, down_mm, 1, shift(n, -2))
                        nc.scalar.copy(in_hi[:, b], inner).then_inc(in_hi_done, 1)
                        if not last and tile_at(f - 2) is not None:
                            i = tile_at(f - 2)
                            copy_hT((g + 1) * GT + i, i)
                        if f == 0 and not first(g):
                            for i in range(GT):
                                store(g - 1, i)
                    if not last:
                        for k in range(KC):
                            split_x(g + 1, k)

                def finish():
                    for i in range(GT):
                        store(NG - 1, i)
                schedule(act, prepare, group, finish)
                for b in range(2):
                    act.wait_ge(y_stored[b], 16 * NT // 2)

            @block.vector
            def _(dve):
                st = Steps(dve, dve_steps)
                sub = lambda out, x, y: nc.vector.tensor_tensor(out, x, y, ALU.subtract)

                def absorb():
                    st.settle()
                    st.did(nc.vector.memset(spare[:], 0.0))

                def stats_of(t):
                    wait_tile(dve, xhat, 1, shift(t, -1))
                    absorb()
                    st.did(nc.vector.bn_stats(st1[:, 0:6], tile_of(x_res, t)))
                    absorb()
                    st.did(nc.vector.bn_aggr(st1[:, 6:8], st1[:, 0:6]))
                    st.settle()
                    nc.vector.tensor_scalar(st1[:, 7:8], st1[:, 7:8], EPS, None, ALU.add).then_inc(stats, 1)

                def xhat_of(t, b):
                    wait_tile(dve, rstd, 1, t)
                    wait_tile(dve, stats, 1, t)
                    wait_tile(dve, hT_mm, 1, shift(t, -2))
                    nc.vector.tensor_scalar(h[:, b], tile_of(x_res, t), st1[:, 6:7], r1[:, b:b + 1],
                                            ALU.subtract, ALU.mult).then_inc(xhat, 1)

                def mix(g):
                    wait_tile(dve, hT_out, GT, g)
                    pairs = lambda x, n: x.rearrange("p (x two n) c -> p x two n c", two=2, n=n)
                    sv, dv = pairs(hT, 1), pairs(mixT, 1)
                    for x in range(KC // 2):
                        st.did(nc.vector.tensor_tensor(dv[:, x, 0], sv[:, x, 0], sv[:, x, 1], ALU.add))
                        st.did(nc.vector.tensor_tensor(dv[:, x, 1], sv[:, x, 0], sv[:, x, 1], ALU.subtract))
                    st.settle()
                    sv, dv = pairs(mixT, 2), pairs(hT, 2)
                    st.did(nc.vector.tensor_tensor(dv[:, 0, 0], sv[:, 0, 0], sv[:, 0, 1], ALU.add))
                    st.settle()
                    nc.vector.tensor_tensor(dv[:, 0, 1], sv[:, 0, 0], sv[:, 0, 1], ALU.subtract).then_inc(mixed, 1)

                def rest_x(g, k):
                    wait_tile(dve, x_hi_done, KC, g, k + 1)
                    sub(x_lo[:, k], psum[6 + k % 2][:], x_hi[:, k].bitcast(F32)).then_inc(x_lo_done, 1)

                def rest_w(g, f):
                    n, b = g * FT + f, f % 2
                    wait_tile(dve, w_hi_done, 1, n)
                    sub(w_lo[:, b], raw[:, f % RING], w_hi[:, b].bitcast(F32)).then_inc(w_lo_done, 1)

                def outputs(g):
                    for i in range(GT):
                        t = g * GT + i
                        wait_tile(dve, down_mm, FT, g)
                        wait_tile(dve, y_stored[i % 2], 16, shift(g * (GT // 2) + i // 2, -1))
                        nc.vector.tensor_tensor(y[:, i % 2], psum[i][:], tile_of(x_res, t), ALU.add).then_inc(y_out, 1)

                def prepare():
                    dve.wait_ge(scale_in, 16)
                    nc.vector.tensor_scalar(scales[:], scales[:], float(C) ** -0.5, None, ALU.mult).then_inc(scaled, 1)
                    dve.wait_ge(scaled, 1)
                    rest_w(0, 0)
                    for t in range(GT):
                        stats_of(t)
                        xhat_of(t, t % 2)
                    mix(0)
                    for k in range(KC):
                        rest_x(0, k)

                def group(g, last):
                    for f in range(FT):
                        n, b = g * FT + f, f % 2
                        if f < FT - 1:
                            rest_w(g, f + 1)
                        elif not last:
                            rest_w(g + 1, 0)
                        i = tile_at(f)
                        if not last and i is not None:
                            stats_of((g + 1) * GT + i)
                        wait_tile(dve, gate_done, 1, n)
                        wait_tile(dve, up_mm, 1, n)
                        wait_tile(dve, in_lo_done, 1, shift(n, -1))
                        nc.vector.scalar_tensor_tensor(inner, up_bank[:], scales[:, 1, f:f + 1], gate_act[:, b],
                                                       ALU.mult, ALU.mult).then_inc(inner_done, 1)
                        if first(g):
                            wait_tile(dve, wd_hi_done, 1, f)
                            sub(wd_lo[:, f], wd[:, f], wd_hi[:, f].bitcast(F32)).then_inc(wd_lo_done, 1)
                        wait_tile(dve, in_hi_done, 1, n)
                        sub(in_lo[:, b], inner, in_hi[:, b].bitcast(F32)).then_inc(in_lo_done, 1)
                        if not last and i is not None:
                            xhat_of((g + 1) * GT + i, i % 2)
                        if not last and f == FT - 3:
                            mix(g + 1)
                        if f == 0 and not first(g):
                            outputs(g - 1)
                    if not last:
                        for k in range(KC):
                            rest_x(g + 1, k)
                schedule(dve, prepare, group, lambda: outputs(NG - 1), st, DVE_F)
                wait_tile(dve, y_out, 1, NT - 1)



_IN = ["L0_attn_x", "L0_attn_Wq", "L0_attn_Wk", "L0_attn_bk", "L0_attn_Wv", "L0_attn_bv", "L0_attn_Wo",
       "L0_attn_bo", "L0_ffn_similarity", "L0_wmod", "L1_attn_Wq", "L1_attn_bq", "L1_attn_Wkv", "L1_attn_bkv",
       "L1_attn_Wo", "L1_attn_bo", "L1_ffn_SU_ug", "L1_ffn_Wscale_dp",
       "L1_wmod"]


def constants():
    import numpy as np

    r = np.arange(P)
    had = np.ones((1, 1), np.float32)
    while had.shape[0] < P:
        had = np.block([[had, had], [had, -had]]).astype(np.float32)
    squares = np.stack([np.eye(P), (r[:, None] < r[None, :]), had]).astype(np.float32)
    at = HOP * (r[:, None] // W0)
    k0 = np.arange(KEYS0)[None]
    mask0 = np.where((k0 >= at) & (k0 < at + W0), 0.0, NEG).astype(np.float32)
    mask1 = np.full((4, P, KEYS1), NEG, np.float32)
    for n in range(4):
        q = n * P + r[:, None]
        even = n - n % 2
        odd = n if n % 2 else n - 1
        key = np.concatenate([np.arange(META), even * P + r, odd * P + r])[None]
        local = np.arange(KEYS1)[None] >= META
        ok = (key <= q) & np.where(local, (key >= META) & (key > q - P), True)
        mask1[n][ok] = 0.0
    freq = (1.0 / np.float32(10000.0) ** (np.arange(0, HD, 2, dtype=np.float32) / np.float32(HD))).astype(np.float32)
    ang = np.arange(S, dtype=np.float32)[:, None] * freq
    cos, sin = np.repeat(np.cos(ang), 2, -1), np.repeat(np.sin(ang), 2, -1)
    sin[:, 0::2] *= -1
    rope = np.stack([cos * SCALE1, sin * SCALE1, cos, sin], 1).astype(np.float32)
    meta_head = (r[:, None] // META == np.arange(P // META)).astype(np.float32)
    return {"meta_head": meta_head, "squares": squares, "mask0": mask0, "mask1": mask1, "rope": rope}


def kernel(**inputs):
    import numpy as np
    import concourse.bacc as bacc
    from concourse.bass_utils import run_bass_kernel_spmd

    arrays = {n: np.ascontiguousarray(inputs[n]) for n in _IN}
    arrays["gate_T"] = np.ascontiguousarray(np.asarray(inputs["L0_ffn_gate_weight"]).T)
    cs = np.stack([np.asarray(inputs["L0_c"])[0], np.asarray(inputs["L1_c"])[0]])
    arrays["c_cols"] = np.ascontiguousarray(cs.reshape(2, KC, P).transpose(2, 0, 1))
    arrays["bq_cols"] = np.ascontiguousarray(np.asarray(inputs["L0_attn_bq"]).reshape(KC, P).T)
    arrays["su_dp_cols"] = np.ascontiguousarray(np.asarray(inputs["L1_ffn_SU_dp"]).reshape(FT, P).T)
    ug_scale = np.asarray(inputs["L1_ffn_Wscale_ug"]).reshape(2, FT, P)
    arrays["ug_cols"] = np.ascontiguousarray(ug_scale[::-1].transpose(2, 0, 1))
    up = np.asarray(inputs["L0_ffn_gate_up_proj"]).reshape(E, 2 * FI, KC, P)
    arrays["moe_up"] = np.ascontiguousarray(up.transpose(0, 3, 2, 1))
    down = np.asarray(inputs["L0_ffn_down_proj"]).reshape(E, C, 2, FH)
    arrays["moe_down"] = np.ascontiguousarray(down.transpose(0, 3, 2, 1))
    ug = np.stack([np.asarray(inputs["L1_ffn_W_gate"]), np.asarray(inputs["L1_ffn_W_up"])]).reshape(2, FT, P, KC, P)
    arrays["ffn_up"] = np.ascontiguousarray(ug.transpose(1, 4, 3, 0, 2))
    arrays["ffn_down"] = np.ascontiguousarray(np.asarray(inputs["L1_ffn_W_down"]).reshape(C, FT, P).transpose(2, 1, 0))
    arrays.update(constants())

    nc = bacc.Bacc("TRN2", target_bir_lowering=False, num_devices=1)
    aps = {n: nc.dram_tensor("in_" + n, a.shape, mybir.dt.from_np(a.dtype), kind="ExternalInput").ap()
           for n, a in arrays.items()}
    out = nc.dram_tensor("out_0", (1, S, C), F32, kind="ExternalOutput").ap()
    adaln_two_layers(nc, aps, out)
    r = run_bass_kernel_spmd(nc, [{"in_" + n: a for n, a in arrays.items()}], core_ids=[0])
    return r.results[0]["out_0"]
```
